# Optimizing a Trainium2 kernel written in Bass

```python
import numpy as np
import jax
import jax.numpy as jnp

def _softmax(x, axis=-1):
    return jax.nn.softmax(x, axis=axis)

def _gelu(x):
    return jax.nn.gelu(x, approximate=True)

def _silu(x):
    return jax.nn.silu(x)

def _sigmoid(x):
    return jax.nn.sigmoid(x)

def _layernorm(x, axis=-1, eps=1e-05):
    m = jnp.mean(x, axis=axis, keepdims=True)
    v = jnp.var(x, axis=axis, keepdims=True)
    return (x - m) / jnp.sqrt(v + eps)

def _scatter_add(tgt, idx, src, axis=0):
    return tgt.at[idx].add(src)

def _segment_sum(src, seg, n):
    return jax.ops.segment_sum(src, seg, n)
kernel_name = 'mk_macaron_d2_jaxref_r8_98b5f8'

def setup_inputs(seed: int=0):
    np.random.seed(seed)
    _w = jnp.asarray

    def _L0_attn_setup():
        import jax, jax.numpy as jnp
        import numpy as np
        B, S, HID = (2, 256, 256)
        NH, D_NOPE, D_ROPE, D_Q, D_V, LORA = (16, 128, 64, 192, 128, 64)
        SCALE = D_Q ** (-0.5)
        EPS = 1e-06

        def _rms_norm(x, weight, eps=EPS):
            xf = x.astype(jnp.float32)
            var = jnp.mean(xf * xf, axis=-1, keepdims=True)
            return (weight * (xf * jax.lax.rsqrt(var + eps))).astype(x.dtype)

        def _rotate_half(x):
            half = x.shape[-1] // 2
            return jnp.concatenate([-x[..., half:], x[..., :half]], axis=-1)
        key = jax.random.key(seed)
        ks = jax.random.split(key, 5)
        return {'hidden_states': jax.random.normal(ks[0], (B, S, HID), dtype=jnp.float32), 'Wq': jax.random.normal(ks[1], (NH * D_Q, HID), dtype=jnp.float32) * 0.02, 'Wkva': jax.random.normal(ks[2], (LORA + D_ROPE, HID), dtype=jnp.float32) * 0.02, 'kv_a_norm_weight': jnp.ones((LORA,), dtype=jnp.float32), 'Wkvb': jax.random.normal(ks[3], (NH * (D_NOPE + D_V), LORA), dtype=jnp.float32) * 0.02, 'Wo': jax.random.normal(ks[4], (HID, NH * D_V), dtype=jnp.float32) * 0.02, 'cos': jnp.ones((1, D_ROPE), dtype=jnp.float32), 'sin': jnp.zeros((1, D_ROPE), dtype=jnp.float32)}
    _L0_attn_in = _L0_attn_setup()

    def _L0_ffn_setup():
        import jax, jax.numpy as jnp
        import numpy as np

        def ternary_quantize(t, threshold, scale):
            return jnp.where(t > threshold, scale, jnp.where(t < -threshold, -scale, 0.0)).astype(t.dtype)
        key = jax.random.key(seed)
        k1, k2, k3 = jax.random.split(key, 3)
        B, S, D = (4, 512, 256)
        x = jax.random.normal(k1, (B, S, D), dtype=jnp.float32)
        weight = jax.random.normal(k2, (D, D), dtype=jnp.float32) * 0.02
        rram_variation = jax.random.normal(k3, (D, D), dtype=jnp.float32) * 0.05
        return {'x': x, 'weight': weight, 'rram_variation': rram_variation}
    _L0_ffn_in = _L0_ffn_setup()

    def _L1_attn_setup():
        import jax, jax.numpy as jnp
        import numpy as np
        key = jax.random.key(seed)
        ks = jax.random.split(key, 5)
        B, S, D = (1, 512, 256)
        H, Dh = (16, 128)
        scale = 1.0 / np.sqrt(D).astype(np.float32)
        return {'x': jax.random.normal(ks[0], (B, S, D), dtype=jnp.float32), 'W_K': jax.random.normal(ks[1], (H, Dh, D), dtype=jnp.float32) * scale, 'W_Q': jax.random.normal(ks[2], (H, Dh, D), dtype=jnp.float32) * scale, 'W_V': jax.random.normal(ks[3], (H, Dh, D), dtype=jnp.float32) * scale, 'W_O': jax.random.normal(ks[4], (D, H * Dh), dtype=jnp.float32) * scale}
    _L1_attn_in = _L1_attn_setup()

    def _L1_ffn_setup():
        import jax, jax.numpy as jnp
        import numpy as np
        NUM_EXPERTS = 128
        NUM_KEPT = 48
        TOP_K = 8
        HIDDEN = 256
        INTER = 96
        CAP = 96
        BATCH, SEQ = (2, 128)
        key = jax.random.key(seed)
        k1, k2, k3, k4 = jax.random.split(key, 4)
        hidden_states = jax.random.normal(k1, (BATCH, SEQ, HIDDEN), jnp.float32)
        gate_weight = jax.random.normal(k2, (NUM_EXPERTS, HIDDEN), jnp.float32) * 0.02
        gate_up_proj = jax.random.normal(k3, (NUM_KEPT, 2 * INTER, HIDDEN), jnp.float32) * 0.02
        down_proj = jax.random.normal(k4, (NUM_KEPT, HIDDEN, INTER), jnp.float32) * 0.02
        o2n = -np.ones(NUM_EXPERTS, np.int32)
        o2n[np.arange(NUM_KEPT) * 2] = np.arange(NUM_KEPT, dtype=np.int32)
        old_to_new = jnp.asarray(o2n)
        return {'hidden_states': hidden_states, 'gate_weight': gate_weight, 'gate_up_proj': gate_up_proj, 'down_proj': down_proj, 'old_to_new': old_to_new}
    _L1_ffn_in = _L1_ffn_setup()
    _d = {'L0_attn_hidden_states': _L0_attn_in['hidden_states'], 'L0_attn_Wq': _L0_attn_in['Wq'], 'L0_attn_Wkva': _L0_attn_in['Wkva'], 'L0_attn_kv_a_norm_weight': _L0_attn_in['kv_a_norm_weight'], 'L0_attn_Wkvb': _L0_attn_in['Wkvb'], 'L0_attn_Wo': _L0_attn_in['Wo'], 'L0_attn_cos': _L0_attn_in['cos'], 'L0_attn_sin': _L0_attn_in['sin'], 'L0_ffn_weight': _L0_ffn_in['weight'], 'L0_ffn_rram_variation': _L0_ffn_in['rram_variation'], 'L1_attn_W_K': _L1_attn_in['W_K'], 'L1_attn_W_Q': _L1_attn_in['W_Q'], 'L1_attn_W_V': _L1_attn_in['W_V'], 'L1_attn_W_O': _L1_attn_in['W_O'], 'L1_ffn_gate_weight': _L1_ffn_in['gate_weight'], 'L1_ffn_gate_up_proj': _L1_ffn_in['gate_up_proj'], 'L1_ffn_down_proj': _L1_ffn_in['down_proj'], 'L1_ffn_old_to_new': _L1_ffn_in['old_to_new']}
    _x0 = _d['L0_attn_hidden_states']
    _d['L0_attn_hidden_states'] = jax.random.normal(jax.random.fold_in(jax.random.key(seed), 1), (4, 512, 256), dtype=_x0.dtype)
    del _x0
    return _d

def reference(L0_attn_hidden_states, L0_attn_Wq, L0_attn_Wkva, L0_attn_kv_a_norm_weight, L0_attn_Wkvb, L0_attn_Wo, L0_attn_cos, L0_attn_sin, L0_ffn_weight, L0_ffn_rram_variation, L1_attn_W_K, L1_attn_W_Q, L1_attn_W_V, L1_attn_W_O, L1_ffn_gate_weight, L1_ffn_gate_up_proj, L1_ffn_down_proj, L1_ffn_old_to_new):

    def _L0_attn_ref(hidden_states, Wq, Wkva, kv_a_norm_weight, Wkvb, Wo, cos, sin):
        import jax, jax.numpy as jnp
        import numpy as np
        B, S, HID = (2, 256, 256)
        NH, D_NOPE, D_ROPE, D_Q, D_V, LORA = (16, 128, 64, 192, 128, 64)
        SCALE = D_Q ** (-0.5)
        EPS = 1e-06

        def _rms_norm(x, weight, eps=EPS):
            xf = x.astype(jnp.float32)
            var = jnp.mean(xf * xf, axis=-1, keepdims=True)
            return (weight * (xf * jax.lax.rsqrt(var + eps))).astype(x.dtype)

        def _rotate_half(x):
            half = x.shape[-1] // 2
            return jnp.concatenate([-x[..., half:], x[..., :half]], axis=-1)
        b, s, _ = hidden_states.shape
        q = (hidden_states @ Wq.T).reshape(b, s, NH, D_Q).transpose(0, 2, 1, 3)
        q_nope, q_pe = (q[..., :D_NOPE], q[..., D_NOPE:])
        ckv = hidden_states @ Wkva.T
        compressed_kv, k_pe = (ckv[..., :LORA], ckv[..., LORA:])
        k_pe = k_pe.reshape(b, s, 1, D_ROPE).transpose(0, 2, 1, 3)
        kv = _rms_norm(compressed_kv, kv_a_norm_weight) @ Wkvb.T
        kv = kv.reshape(b, s, NH, D_NOPE + D_V).transpose(0, 2, 1, 3)
        k_nope, v = (kv[..., :D_NOPE], kv[..., D_NOPE:])
        q_pe = q_pe * cos + _rotate_half(q_pe) * sin
        k_pe = k_pe * cos + _rotate_half(k_pe) * sin
        q_full = jnp.concatenate([q_nope, q_pe], axis=-1)
        k_full = jnp.concatenate([k_nope, jnp.broadcast_to(k_pe, (b, NH, s, D_ROPE))], axis=-1)
        scores = jnp.einsum('bhqd,bhkd->bhqk', q_full, k_full) * SCALE
        causal = jnp.tril(jnp.ones((s, s), dtype=bool))
        scores = jnp.where(causal, scores, jnp.finfo(scores.dtype).min)
        attn = jax.nn.softmax(scores.astype(jnp.float32), axis=-1).astype(v.dtype)
        out = jnp.einsum('bhqk,bhkd->bhqd', attn, v)
        out = out.transpose(0, 2, 1, 3).reshape(b, s, NH * D_V)
        return out @ Wo.T

    def _L0_ffn_ref(x, weight, rram_variation):
        import jax, jax.numpy as jnp
        import numpy as np

        def ternary_quantize(t, threshold, scale):
            return jnp.where(t > threshold, scale, jnp.where(t < -threshold, -scale, 0.0)).astype(t.dtype)
        TH_X, SC_X = (0.33, 0.5)
        TH_W, SC_W = (0.2, 0.6)
        x_q = ternary_quantize(x, TH_X, SC_X)
        w_q = ternary_quantize(weight, TH_W, SC_W)
        w_rram = w_q + rram_variation
        return jnp.einsum('bsd,od->bso', x_q, w_rram)

    def _L1_attn_ref(x, W_K, W_Q, W_V, W_O):
        import jax, jax.numpy as jnp
        import numpy as np
        b, pos, d_model = x.shape
        d_head = W_K.shape[1]
        k = jnp.einsum('ihd,bpd->biph', W_K, x)
        q = jnp.einsum('ihd,bpd->biph', W_Q, x)
        v = jnp.einsum('ihd,bpd->biph', W_V, x)
        scores = jnp.einsum('biph,biqh->biqp', k, q)
        mask = jnp.tril(jnp.ones((pos, pos), dtype=x.dtype))
        masked = scores * mask - jnp.float32(10000000000.0) * (1.0 - mask)
        attn = jax.nn.softmax(masked / jnp.sqrt(jnp.float32(d_head)), axis=-1)
        z = jnp.einsum('biqp,biph->biqh', attn, v)
        z_flat = jnp.transpose(z, (0, 2, 1, 3)).reshape(b, pos, -1)
        out = jnp.einsum('df,bqf->bqd', W_O, z_flat)
        return out

    def _L1_ffn_ref(hidden_states, gate_weight, gate_up_proj, down_proj, old_to_new):
        import jax, jax.numpy as jnp
        import numpy as np
        NUM_EXPERTS = 128
        NUM_KEPT = 48
        TOP_K = 8
        HIDDEN = 256
        INTER = 96
        CAP = 96
        BATCH, SEQ = (2, 128)
        B, S, H = hidden_states.shape
        x = hidden_states.reshape(-1, H)
        T = x.shape[0]
        logits = x @ gate_weight.T
        logits = jnp.where(old_to_new[None, :] == -1, -jnp.inf, logits)
        probs = jax.nn.softmax(logits.astype(jnp.float32), axis=-1).astype(logits.dtype)
        top_v, top_i = jax.lax.top_k(probs, TOP_K)
        top_v = top_v / jnp.sum(top_v, axis=-1, keepdims=True)
        sel_new = old_to_new[top_i]
        E = gate_up_proj.shape[0]
        flat_e = sel_new.reshape(-1)
        flat_w = top_v.reshape(-1)
        tok = jnp.repeat(jnp.arange(T), TOP_K)
        oh = (flat_e[:, None] == jnp.arange(E)[None, :]).astype(jnp.int32)
        pos = jnp.sum(jnp.cumsum(oh, axis=0) * oh, axis=-1) - 1
        valid = pos < CAP
        pos_c = jnp.where(valid, pos, CAP)
        xb = jnp.zeros((E, CAP + 1, H), x.dtype).at[flat_e, pos_c].set(x[tok])
        xb = xb[:, :CAP]
        gu = jnp.einsum('ech,eoh->eco', xb, gate_up_proj)
        g, u = jnp.split(gu, 2, axis=-1)
        h = jax.nn.silu(g) * u
        out = jnp.einsum('eci,ehi->ech', h, down_proj)
        y = out[flat_e, jnp.minimum(pos_c, CAP - 1)]
        w = flat_w * valid.astype(flat_w.dtype)
        final = jnp.zeros_like(x).at[tok].add(y * w[:, None])
        return final.reshape(B, S, H)
    x = L0_attn_hidden_states
    x = x + 0.5 * _L0_ffn_ref(_layernorm(x, axis=-1), L0_ffn_weight, L0_ffn_rram_variation)
    x = x + _L0_attn_ref(_layernorm(x, axis=-1), L0_attn_Wq, L0_attn_Wkva, L0_attn_kv_a_norm_weight, L0_attn_Wkvb, L0_attn_Wo, L0_attn_cos, L0_attn_sin)
    x = x + 0.5 * _L0_ffn_ref(_layernorm(x, axis=-1), L0_ffn_weight, L0_ffn_rram_variation)
    x = x + 0.5 * _L1_ffn_ref(_layernorm(x, axis=-1), L1_ffn_gate_weight, L1_ffn_gate_up_proj, L1_ffn_down_proj, L1_ffn_old_to_new)
    x = x + _L1_attn_ref(_layernorm(x, axis=-1), L1_attn_W_K, L1_attn_W_Q, L1_attn_W_V, L1_attn_W_O)
    x = x + 0.5 * _L1_ffn_ref(_layernorm(x, axis=-1), L1_ffn_gate_weight, L1_ffn_gate_up_proj, L1_ffn_down_proj, L1_ffn_old_to_new)
    return x

_drawn_inputs = setup_inputs


def setup_inputs(seed=0):
    import zlib

    import numpy as np

    out = dict(_drawn_inputs(seed))
    spreads = {'L0_attn_kv_a_norm_weight': (1.0, 0.6),
     'L0_attn_cos': (1.0, 0.6),
     'L0_attn_sin': (0.0, 0.8)}
    factors = {'L0_attn_Wq': 8.0,
     'L1_ffn_gate_weight': 8.0,
     'L1_ffn_gate_up_proj': 8.0,
     'L1_ffn_down_proj': 8.0}
    for name, (base, spread) in spreads.items():
        noise = np.random.default_rng([zlib.crc32(name.encode()), seed]).standard_normal(out[name].shape)
        drawn = base * np.exp(spread * noise) if base else spread * noise
        out[name] = jnp.asarray(drawn.astype(out[name].dtype))
    for name, factor in factors.items():
        out[name] = (out[name] * factor).astype(out[name].dtype)
    return out
```

```python
from contextlib import ExitStack

import numpy as np
import concourse.bass as bass
from concourse import mybir

F32 = mybir.dt.float32
F16 = mybir.dt.float16
BF16 = mybir.dt.bfloat16
I32 = mybir.dt.int32
U32 = mybir.dt.uint32
ALU = mybir.AluOpType
ACT = mybir.ActivationFunctionType
X = mybir.AxisListType.X

P = 128
T, D = 2048, 256
NT = T // P
S, B = 512, 4
TPB = S // P
KD = D // P
H = 16
NOPE, ROPE, LORA, DV = 128, 64, 64, 128
E_OLD, E, INTER, CAP, TOPK = 128, 48, 96, 96, 8
SLOTS = E * CAP

W_SCALE = 1024.0
P_SCALE = 4096.0
O_SCALE = 16.0

FREE = 1

Q_AT = {3: 0, 2: 512, 0: 896, 1: 1024}
K_AT = {0: 0, 1: 512, 3: 896, 2: 1024}
CAUSAL = 1280


def dyn(start, size):
    return bass.ds(start, size)



class Chain:

    def __init__(self, eng, done, start, per):
        self.eng, self.done, self.start, self.per, self.n = eng, done, start, per, 0

    def link(self, ins, spare=None):
        self.n += 1
        ins.then_inc(self.done, 1)
        self.eng.wait_ge(self.done, self.start + self.n)
        if spare is not None:
            self.eng.memset(spare, 0.0)

    def end(self):
        assert self.n == self.per, self.n


def prepare(nc, d, G, sem, sb, ps):
    loaded_x, loaded_w, loaded_g = sem("loaded_x"), sem("loaded_w"), sem("loaded_gate")
    zeroed, consts = sem("consts_zeroed"), sem("consts")
    chain = sem("prep_chain")
    picked, gate_mm, gate_hi, scratch = sem("gate_picked"), sem("gate_mm"), sem("gate_hi"), sem("slots_zeroed")
    zero_ready = sem("zero_ready")
    ZR = 12
    with ExitStack() as c, nc.Block("prepare") as block:
        w = sb("w_raw", [P, KD, D], F32, c)
        rram = sb("rram_raw", [P, KD, D], F32, c)
        sign = sb("sign", [P, KD, D], F32, c)
        gate = sb("gate_raw", [P, D], F32, c)
        o2n_i = sb("o2n_i", [P, 1], I32, c)
        o2n = sb("o2n", [P, 1], F32, c)
        cols = sb("cols", [P, E], F32, c)
        sel = sb("sel", [P, E], F32, c)
        ones = sb("ones", [P, P], F32, c)
        zero = sb("zero", [P, ZR * D], F32, c)
        gp = ps("gp", [P, KD + 1, E], F32, c)

        @block.sync
        def _(sp):
            sp.dma_start(w[:, :, :], d["ffn_wT"].rearrange("(k p) o -> p k o", p=P)).then_inc(loaded_w, 16)
            sp.dma_start(rram[:, :, :], d["rramT"].rearrange("(k p) o -> p k o", p=P)).then_inc(loaded_w, 16)
            sp.dma_start(gate[:, :], d["gate_w"]).then_inc(loaded_g, 16)
            sp.dma_start(o2n_i[:, :], d["o2n"]).then_inc(loaded_g, 16)
            sp.dma_start(G["x"][:, :].rearrange("p (t d) -> p t d", d=D), d["x"].rearrange("(t p) d -> p t d", p=P)).then_inc(loaded_x, 16)
            sp.wait_ge(zero_ready, 1)
            for table in ("scratch_a", "scratch_b"):
                rows = d[table].rearrange("(a p r) d -> a p (r d)", p=P, r=ZR)
                for i in range(SLOTS // (P * ZR)):
                    sp.dma_start(rows[i], zero[:, :]).then_inc(scratch, 16)
            sp.wait_ge(scratch, 16 * 2 * SLOTS // (P * ZR))
            sp.wait_ge(loaded_x, 16)

        @block.gpsimd
        def _(pool):
            for t, v in ((G["ident"], 0.0), (G["ident_h"], 0.0), (G["ident_b"], 0.0), (G["mask_b"], 0.0),
                         (G["tri_b"], 1.0), (G["ones_b"], 1.0), (ones, 1.0)):
                pool.memset(t[:, :], v).then_inc(zeroed, 1)
            pool.wait_ge(zeroed, 7)
            for t in (G["ident"], G["ident_h"], G["ident_b"]):
                pool.affine_select(out=t[:, :], in_=t[:, :], compare_op=ALU.not_equal, fill=1.0, base=0,
                                   pattern=[[-1, P]], channel_multiplier=1).then_inc(consts, 1)
            pool.affine_select(out=G["mask_b"][:, :], in_=G["mask_b"][:, :], compare_op=ALU.is_ge, fill=-1e30,
                               base=0, pattern=[[-1, P]], channel_multiplier=1).then_inc(consts, 1)
            pool.affine_select(out=G["tri_b"][:, :], in_=G["tri_b"][:, :], compare_op=ALU.is_ge, fill=0.0,
                               base=0, pattern=[[1, P]], channel_multiplier=-1).then_inc(consts, 1)
            pool.iota(cols[:, :], pattern=[[1, E]], base=0, channel_multiplier=0,
                      allow_small_or_imprecise_dtypes=True).then_inc(consts, 1)

        @block.scalar
        def _(act):
            act.wait_ge(gate_mm, 1)
            act.activation(G["gate"][:, :, 0, :], gp[:, 0:KD, :], ACT.Copy, scale=W_SCALE).then_inc(gate_hi, 1)

        @block.tensor
        def _(pe):
            pe.wait_ge(picked, 1)
            for k in range(KD):
                pe.matmul(gp[:, k, :], gate[:, k * P:(k + 1) * P], sel[:, :], start=True, stop=True)
            pe.matmul(gp[:, KD, :], ones[:, :], sel[:, :], start=True, stop=True).then_inc(gate_mm, 1)

        @block.vector
        def _(dve):
            ch = Chain(dve, chain, 0, 10)
            dve.memset(zero[:, :], 0.0).then_inc(zero_ready, 1)
            dve.wait_ge(loaded_g, 32)
            dve.wait_ge(consts, 6)
            ch.link(dve.tensor_copy(o2n[:, :], o2n_i[:, :]))
            dve.tensor_scalar(sel[:, :], cols[:, :], o2n[:, 0:1], None, ALU.is_equal).then_inc(picked, 1)
            dve.wait_ge(loaded_w, 32)
            ch.link(dve.tensor_scalar(sign[:, :, :], w[:, :, :], 0.2, None, ALU.is_gt))
            ch.link(dve.scalar_tensor_tensor(sign[:, :, :], w[:, :, :], -0.2, sign[:, :, :], ALU.is_lt, ALU.subtract))
            ch.link(dve.scalar_tensor_tensor(w[:, :, :], sign[:, :, :], -0.6, rram[:, :, :], ALU.mult, ALU.add))
            for part in range(3):
                ch.link(dve.tensor_copy(G["ffn_w"][:, :, part, :], w[:, :, :]))
                if part < 2:
                    ch.link(dve.tensor_tensor(w[:, :, :], w[:, :, :], G["ffn_w"][:, :, part, :], ALU.subtract))
            dve.wait_ge(gate_hi, 1)
            dve.scalar_tensor_tensor(G["gate"][:, :, 1, :], gp[:, 0:KD, :], W_SCALE, G["gate"][:, :, 0, :],
                                     ALU.mult, ALU.subtract)
            ch.link(dve.tensor_scalar(G["absent"][:, :], gp[:, KD, :], 0.5, -3e38, ALU.is_lt, ALU.mult))
            ch.end()


def absorb(nc, d, G, sem, sb, ps):
    loaded = {n: sem(f"loaded_{n}") for n in ("wq", "wk", "wpe", "wv", "wo", "kva", "rope")}
    rot_made, rot_mm, rot_sq, pe_mm = sem("rot_made"), sem("rot_mm"), sem("rot_sq"), sem("rope_mm")
    swap0, swap1, chain = sem("swap_zeroed"), sem("swap_made"), sem("absorb_chain")
    filled, high, done = sem("absorb_filled"), sem("absorb_high"), sem("absorb_done")
    q_w, vo_w, kv_w = G["q_w"], G["vo_w"], G["kv_w"]
    HPB = 4
    with ExitStack() as c, nc.Block("absorb") as block:
        wq = sb("wq", [P, H, D], F32, c)
        wk = sb("wk", [P, H, LORA], F32, c)
        wv = sb("wv", [P, H, LORA], F32, c)
        wo = sb("wo", [P, H, D], F32, c)
        wpe = sb("wpe", [P, KD, H * ROPE], F32, c)
        kva = sb("kva", [P, KD, LORA], F32, c)
        kpe = sb("kpe", [ROPE, D], F32, c)
        cs = sb("cs", [ROPE, 2], F32, c)
        swap = sb("swap", [ROPE, ROPE], F32, c)
        rot = sb("rot", [ROPE, ROPE], F32, c)
        rr = sb("rr", [ROPE, ROPE], F32, c)
        bank = [ps(f"ab{i}", [P, 512], F32, c) for i in range(4)]
        rp = ps("rp", [P, 4, ROPE], F32, c)

        @block.sync
        def _(sp):
            sp.dma_start(cs[:, 0:1], d["cos"].rearrange("a r -> r a")).then_inc(loaded["rope"], 16)
            sp.dma_start(cs[:, 1:2], d["sin"].rearrange("a r -> r a")).then_inc(loaded["rope"], 16)
            sp.dma_start(kpe[:, :], d["kpe_w"]).then_inc(loaded["rope"], 16)
            sp.dma_start(kva[:, :, :], d["kvaT"].rearrange("(k p) l -> p k l", p=P)).then_inc(loaded["kva"], 16)
            sp.dma_start(G["c_norm"][:, :], d["c_norm"]).then_inc(loaded["kva"], 16)
            kvb = d["kvb"].rearrange("(h r) l -> r h l", r=NOPE + DV)
            sp.dma_start(wq[:, :, :], d["wq"].rearrange("(h r) i -> r h i", r=NOPE + ROPE)[0:NOPE]).then_inc(loaded["wq"], 16)
            sp.dma_start(wk[:, :, :], kvb[0:NOPE]).then_inc(loaded["wk"], 16)
            sp.dma_start(wpe[:, :, :], d["wpeT"].rearrange("(k p) q -> p k q", p=P)).then_inc(loaded["wpe"], 16)
            sp.dma_start(wv[:, :, :], kvb[NOPE:NOPE + DV]).then_inc(loaded["wv"], 16)
            sp.dma_start(wo[:, :, :], d["woT"].rearrange("(h r) o -> r h o", r=DV)).then_inc(loaded["wo"], 16)

        @block.gpsimd
        def _(pool):
            pool.memset(swap[:, :], 0.0).then_inc(swap0, 1)
            pool.wait_ge(swap0, 1)
            half = ROPE // 2
            pool.affine_select(out=swap[:, :], in_=swap[:, :], compare_op=ALU.not_equal, fill=-1.0, base=half,
                               pattern=[[-1, ROPE]], channel_multiplier=1).then_inc(swap0, 1)
            pool.wait_ge(swap0, 2)
            pool.affine_select(out=swap[:, :], in_=swap[:, :], compare_op=ALU.not_equal, fill=1.0, base=-half,
                               pattern=[[-1, ROPE]], channel_multiplier=1).then_inc(swap1, 1)

        @block.tensor
        def _(pe):
            pe.wait_ge(rot_made, 1)
            pe.matmul(rp[0:ROPE, 0, :], rot[:, :], rot[:, :], start=True, stop=True).then_inc(rot_mm, 1)
            pe.wait_ge(rot_sq, 1)
            for k in range(KD):
                last = pe.matmul(rp[:, 1 + k, :], kpe[:, k * P:(k + 1) * P], rr[:, :], start=True, stop=True)
            last.then_inc(pe_mm, 1)
            pe.wait_ge(loaded["wq"], 16)
            pe.wait_ge(loaded["wk"], 16)
            for g in range(H // HPB):
                for hh in range(HPB):
                    h = g * HPB + hh
                    for k in range(KD):
                        at = (k * HPB + hh) * LORA
                        last = pe.matmul(bank[g][:, at:at + LORA], wq[:, h, k * P:(k + 1) * P], wk[:, h, :],
                                         start=True, stop=True)
                last.then_inc(filled, 1)
            pe.wait_ge(loaded["wv"], 16)
            pe.wait_ge(loaded["wo"], 16)
            for g in range(H // 4):
                pe.wait_ge(done, g + 1)
                for hh in range(4):
                    h = g * 4 + hh
                    last = pe.matmul(bank[g][(hh % 2) * 64:(hh % 2) * 64 + 64, (hh // 2) * D:(hh // 2 + 1) * D],
                                     wv[:, h, :], wo[:, h, :], start=True, stop=True)
                last.then_inc(filled, 1)

        def nope(g, part):
            return q_w[:, :, part, g * HPB * P:(g + 1) * HPB * P].rearrange("p k (h c) -> p k h c", h=HPB)[:, :, :, 0:LORA]

        def rope(k, part):
            return q_w[:, k, part, :].rearrange("p (h c) -> p h c", h=H)[:, :, LORA:P]

        def raw_rope(k):
            return wpe[:, k, :].rearrange("p (h c) -> p h c", h=H)

        @block.scalar
        def _(act):
            act.wait_ge(loaded["wpe"], 16)
            for k in range(KD):
                act.activation(rope(k, 0), raw_rope(k), ACT.Copy, scale=W_SCALE)
            act.wait_ge(loaded["kva"], 32)
            act.activation(kv_w[:, :, 0, 0:LORA], kva[:, :, :], ACT.Copy, scale=W_SCALE)
            act.wait_ge(pe_mm, 1)
            act.activation(kv_w[:, :, 0, LORA:P], rp[:, 1:3, :], ACT.Copy, scale=W_SCALE).then_inc(high, 1)
            for g in range(H // HPB):
                act.wait_ge(filled, g + 1)
                for k in range(KD):
                    last = act.activation(nope(g, 0)[:, k], bank[g][:, k * 256:(k + 1) * 256].rearrange("p (h c) -> p h c", h=HPB),
                                          ACT.Copy, scale=W_SCALE)
                last.then_inc(high, 1)
            for g in range(H // 4):
                act.wait_ge(filled, 4 + g + 1)
                act.activation(vo_w[:, 2 * g:2 * g + 2, 0, :], bank[g][:, :].rearrange("p (a o) -> p a o", a=2),
                               ACT.Copy, scale=W_SCALE).then_inc(high, 1)

        @block.vector
        def _(dve):
            ch = Chain(dve, chain, 0, 2)
            dve.wait_ge(loaded["rope"], 48)
            dve.wait_ge(swap1, 1)
            ch.link(dve.tensor_scalar(rot[:, :], swap[:, :], cs[:, 1:2], None, ALU.mult))
            dve.scalar_tensor_tensor(rot[:, :], G["ident"][0:ROPE, 0:ROPE], cs[:, 0:1], rot[:, :],
                                     ALU.mult, ALU.add).then_inc(rot_made, 1)
            dve.wait_ge(rot_mm, 1)
            dve.tensor_copy(rr[:, :], rp[0:ROPE, 0, :]).then_inc(rot_sq, 1)
            dve.wait_ge(high, 1)
            for k in range(KD):
                dve.scalar_tensor_tensor(rope(k, 1), raw_rope(k), W_SCALE, rope(k, 0), ALU.mult, ALU.subtract)
            dve.scalar_tensor_tensor(kv_w[:, :, 1, 0:LORA], kva[:, :, :], W_SCALE, kv_w[:, :, 0, 0:LORA],
                                     ALU.mult, ALU.subtract)
            dve.scalar_tensor_tensor(kv_w[:, :, 1, LORA:P], rp[:, 1:3, :], W_SCALE, kv_w[:, :, 0, LORA:P],
                                     ALU.mult, ALU.subtract)
            for g in range(H // HPB):
                dve.wait_ge(high, g + 2)
                for k in range(KD):
                    last = dve.scalar_tensor_tensor(nope(g, 1)[:, k], bank[g][:, k * 256:(k + 1) * 256].rearrange("p (h c) -> p h c", h=HPB),
                                                    W_SCALE, nope(g, 0)[:, k], ALU.mult, ALU.subtract)
                last.then_inc(done, 1)
            for g in range(H // 4):
                dve.wait_ge(high, 4 + g + 2)
                last = dve.scalar_tensor_tensor(vo_w[:, 2 * g:2 * g + 2, 1, :], bank[g][:, :].rearrange("p (a o) -> p a o", a=2),
                                                W_SCALE, vo_w[:, 2 * g:2 * g + 2, 0, :], ALU.mult, ALU.subtract)
            ch.link(last)
            ch.end()



def tiles(nc, d, G, sem, sb, ps, tag, ffn=False, latent=False, route=False):
    def s(name, used=True):
        return sem(f"{tag}_{name}") if used else None

    W = TPB * D
    x, hT = G["x"], G["hT"]
    stat_ready, rstd_ready, chain = s("stat_ready"), s("rstd_ready"), s("chain")
    consts = s("consts")
    q_ready, q_turned, qT_ready, y_ready, x_added = (
        s(n, ffn) for n in ("q_ready", "q_turned", "qT_ready", "y_ready", "x_added"))
    h_ready, h_hi, h_lo, h_turned = s("h_ready"), s("h_hi"), s("h_lo"), s("h_turned")
    hT_a, hT_v = s("hT_by_act"), s("hT_by_dve")
    ckv_mm, c_ready, c_hi, c_lo, k_turned, kT_ready = (
        s(n, latent) for n in ("ckv_mm", "c_ready", "c_hi", "c_lo", "k_turned", "kT_ready"))
    logit_mm, top_ready, e_ready, mask_ready, count_mm = (
        s(n, route) for n in ("logit_mm", "top_ready", "e_ready", "mask_ready", "count_mm"))
    idx_ready, scattered, route_chain = (s(n, route) for n in ("idx_ready", "scattered", "route_chain"))
    norms = int(ffn) + 1 + int(latent)
    LN_CHAIN, FFN_CHAIN = 2, 2
    with ExitStack() as c, nc.Block(f"tiles_{tag}") as block:
        stats = sb("stats", [P, TPB, 6], F32, c)
        mv = sb("mv", [P, TPB, 2], F32, c)
        var = sb("var", [P, TPB], F32, c)
        rstd = sb("rstd", [P, TPB], F32, c)
        minus_half = sb("minus_half", [P, TPB], F32, c)
        h = sb("h", [P, NT * D if route else W], F32, c)
        h_parts = sb("h_parts", [P, 2, W], F16, c)
        turn_ps = ps("turn_ps", [P, KD, 2, S], F16, c)
        if ffn:
            above = sb("above", [P, W], BF16, c)
            q = sb("q", [P, NT * D], BF16, c)
            qT = sb("qT", [P, KD, S], BF16, c)
            q_ps = ps("q_ps", [P, KD, S], BF16, c)
            y_ps = ps("y_ps", [P, W], F32, c)
        if latent:
            ckv = sb("ckv", [P, TPB, P], F32, c)
            sq = sb("sq", [P, TPB, LORA], F32, c)
            ckv_ps = ps("ckv_ps", [P, TPB, P], F32, c)
            k_ps = ps("k_ps", [P, 2, S], F16, c)
        if route:
            logit = sb("logit", [P, TPB, E], F32, c)
            top = sb("top", [P, TPB, TOPK], F32, c)
            edge = sb("edge", [P, TPB], F32, c)
            ntop = sb("ntop", [P, TPB], F32, c)
            mask = sb("mask", [P, TPB, E], BF16, c)
            mask_sum = sb("mask_sum", [P, E], BF16, c)
            added = sb("added", [P, E], BF16, c)
            prob = sb("prob", [P, TPB, E], F32, c)
            key = sb("key", [P, TPB, E], F32, c)
            keyt = sb("keyt", [P, TPB, TOPK], F32, c)
            late = sb("late", [P, TPB * TOPK], F32, c)
            den = sb("den", [P, TPB], F32, c)
            first_slot = sb("first_slot", [P, TPB, E], F32, c)
            same = sb("same", [P, TPB, TOPK, E], F32, c)
            logit_ps = ps("logit_ps", [P, TPB, E], F32, c)
            count_ps = ps("count_ps", [P, TPB, E], F32, c)
            CHAIN = 20

        def h_of(g):
            return h[:, dyn(g * W, W)] if route else h[:, :]

        @block.gpsimd
        def _(pool):
            pool.memset(minus_half[:, :], -0.5).then_inc(consts, 1)
            if route:
                pool.iota(first_slot[:, :, :], pattern=[[0, TPB], [CAP, E]], base=0, channel_multiplier=0,
                          allow_small_or_imprecise_dtypes=True).then_inc(consts, 1)
            pool.wait_ge(consts, 1 + int(route))
            with pool.Fori(0, norms * B) as n:
                pool.wait_ge(stat_ready, n + 1)
                pool.tensor_tensor(rstd[:, :], var[:, :], minus_half[:, :], ALU.pow).then_inc(rstd_ready, 1)
            if route:
                for t in range(NT):
                    if t % TPB == 0:
                        pool.wait_ge(idx_ready, FREE + t // TPB + 1)
                    for k in range(TOPK):
                        at = t * TOPK + k
                        pool.indirect_dma_start(
                            out=d["scratch_a"], out_offset=bass.IndirectOffsetOnAxis(ap=G["slot"][:, at:at + 1], axis=0),
                            in_=h[:, t * D:(t + 1) * D], in_offset=None, bounds_check=SLOTS - 1,
                            oob_is_err=False).then_inc(scattered, 16)
                pool.wait_ge(scattered, 16 * NT * TOPK)

        @block.scalar
        def _(act):
            act.sem_inc(h_turned, FREE)
            if ffn:
                with act.Fori(0, B) as g:
                    act.wait_ge(q_turned, g + 1)
                    act.activation(qT[:, :, :], q_ps[:, :, :], ACT.Copy).then_inc(qT_ready, 1)
            with act.Fori(0, B) as g:
                act.wait_ge(h_ready, g + 1)
                act.wait_ge(h_turned, FREE + g)
                act.activation(h_parts[:, 0, :], h_of(g), ACT.Copy).then_inc(h_hi, 1)
                act.wait_ge(h_turned, FREE + g + 1)
                act.activation(hT[:, 0, :, dyn(g * S, S)], turn_ps[:, 0, :, :], ACT.Copy).then_inc(hT_a, 1)
            if latent:
                with act.Fori(0, B) as g:
                    act.wait_ge(c_ready, FREE + g + 1)
                    act.activation(G["c"][:, dyn(g * TPB, TPB), 0, :], ckv[:, :, :], ACT.Copy).then_inc(c_hi, 1)
                    act.wait_ge(k_turned, g + 1)
                    act.activation(G["kT"][:, :, dyn(g * S, S)], k_ps[:, :, :], ACT.Copy).then_inc(kT_ready, 1)
            if route:
                with act.Fori(0, B) as g:
                    act.wait_ge(top_ready, g + 1)
                    for j in range(TPB):
                        last = act.activation(prob[:, j, :], logit[:, j, :], ACT.Exp, bias=ntop[:, j:j + 1])
                    last.then_inc(e_ready, 1)

        @block.tensor
        def _(pe):
            for free in (hT_a, hT_v, qT_ready, x_added, c_ready, kT_ready, mask_ready, idx_ready):
                if free is not None:
                    pe.sem_inc(free, FREE)
            if ffn:
                with pe.Fori(0, B) as g:
                    pe.wait_ge(q_ready, g + 1)
                    pe.wait_ge(qT_ready, FREE + g)
                    for j in range(TPB):
                        for k in range(KD):
                            last = pe.transpose(q_ps[:, k, j * P:(j + 1) * P],
                                                q[:, dyn(g * W + (j * D + k * P), P)], G["ident_b"][:, :])
                    last.then_inc(q_turned, 1)
                    pe.wait_ge(qT_ready, FREE + g + 1)
                    pe.wait_ge(x_added, FREE + g)
                    for j in range(TPB):
                        for k in range(KD):
                            for part in range(3):
                                last = pe.matmul(y_ps[:, j * D:(j + 1) * D], qT[:, k, j * P:(j + 1) * P],
                                                 G["ffn_w"][:, k, part, :], start=k + part == 0, stop=k * part == 2)
                    last.then_inc(y_ready, 1)
            with pe.Fori(0, B) as g:
                pe.wait_ge(h_lo, g + 1)
                pe.wait_ge(hT_a, FREE + g)
                pe.wait_ge(hT_v, FREE + g)
                for k in range(KD):
                    for part in range(2):
                        for j in range(TPB):
                            at = j * D + k * P
                            last = pe.transpose(turn_ps[:, k, part, j * P:(j + 1) * P], h_parts[:, part, at:at + P],
                                                G["ident_h"][:, :])
                last.then_inc(h_turned, 1)
            if latent:
                pe.wait_ge(hT_a, FREE + B)
                pe.wait_ge(hT_v, FREE + B)
                with pe.Fori(0, B) as g:
                    pe.wait_ge(c_ready, FREE + g)
                    for j in range(TPB):
                        for k in range(KD):
                            for a, b in ((0, 0), (0, 1), (1, 0)):
                                last = pe.matmul(ckv_ps[:, j, :], hT[:, k, a, dyn(g * S + j * P, P)],
                                                 G["kv_w"][:, k, b, :], start=k + a + b == 0, stop=k * a == 1)
                    last.then_inc(ckv_mm, 1)
                    pe.wait_ge(c_lo, FREE + g + 1)
                    pe.wait_ge(kT_ready, FREE + g)
                    for part in range(2):
                        for j in range(TPB):
                            last = pe.transpose(k_ps[:, part, j * P:(j + 1) * P],
                                                G["c"][:, dyn(g * TPB + j, 1), part, :].rearrange("p a c -> p (a c)"), G["ident_h"][:, :])
                    last.then_inc(k_turned, 1)
            if route:
                pe.wait_ge(hT_a, FREE + B)
                pe.wait_ge(hT_v, FREE + B)
                with pe.Fori(0, B) as g:
                    pe.wait_ge(mask_ready, FREE + g)
                    for j in range(TPB):
                        for k in range(KD):
                            for a, b in ((0, 0), (0, 1), (1, 0)):
                                last = pe.matmul(logit_ps[:, j, :], hT[:, k, a, dyn(g * S + j * P, P)],
                                                 G["gate"][:, k, b, :], start=k + a + b == 0, stop=k * a == 1)
                    last.then_inc(logit_mm, 1)
                    pe.wait_ge(mask_ready, FREE + g + 1)
                    pe.wait_ge(idx_ready, FREE + g)
                    for j in range(TPB):
                        pe.matmul(count_ps[:, j, :], G["ones_b"][:, :], mask_sum[:, :], start=True, stop=False)
                        for i in range(j):
                            pe.matmul(count_ps[:, j, :], G["ones_b"][:, :], mask[:, i, :], start=False, stop=False)
                        last = pe.matmul(count_ps[:, j, :], G["tri_b"][:, :], mask[:, j, :], start=False, stop=True)
                    last.then_inc(count_mm, 1)

        @block.vector
        def _(dve):
            def layernorm(g, turn, done):
                ch = Chain(dve, chain, turn * LN_CHAIN, LN_CHAIN)
                for j in range(TPB):
                    last = dve.bn_stats(stats[:, j, :], x[:, dyn((g * TPB + j) * D, D)])
                ch.link(last, G["spare"][:, 0:1])
                for j in range(TPB):
                    last = dve.bn_aggr(mv[:, j, :], stats[:, j, :])
                ch.link(last)
                dve.tensor_scalar(var[:, :], mv[:, :, 1], 1e-5, None, ALU.add).then_inc(stat_ready, 1)
                dve.wait_ge(rstd_ready, turn + 1)
                for j in range(TPB):
                    at = j * D
                    to = h[:, dyn(g * W + at, D)] if route else h[:, at:at + D]
                    last = dve.tensor_scalar(to, x[:, dyn(g * W + at, D)], mv[:, j, 0:1], rstd[:, j:j + 1],
                                             ALU.subtract, ALU.mult)
                last.then_inc(done, 1)
                ch.end()

            if ffn:
                ffn_chain = s("ffn_chain")
                with dve.Fori(0, B) as g:
                    layernorm(g, g, ffn_chain)
                    dve.wait_ge(ffn_chain, g * FFN_CHAIN + 1)
                    dve.tensor_scalar(above[:, :], h_of(g), 0.33, None, ALU.is_gt).then_inc(ffn_chain, 1)
                    dve.wait_ge(ffn_chain, g * FFN_CHAIN + 2)
                    dve.scalar_tensor_tensor(q[:, dyn(g * W, W)], h_of(g), -0.33, above[:, :],
                                             ALU.is_lt, ALU.subtract).then_inc(q_ready, 1)
                with dve.Fori(0, B) as g:
                    dve.wait_ge(y_ready, g + 1)
                    dve.scalar_tensor_tensor(x[:, dyn(g * W, W)], y_ps[:, :], -0.25, x[:, dyn(g * W, W)],
                                             ALU.mult, ALU.add).then_inc(x_added, 1)
                dve.wait_ge(x_added, FREE + B)
            with dve.Fori(0, B) as g:
                layernorm(g, g + B * int(ffn), h_ready)
                dve.wait_ge(h_hi, g + 1)
                dve.wait_ge(h_ready, g + 1)
                dve.tensor_tensor(h_parts[:, 1, :], h_of(g), h_parts[:, 0, :], ALU.subtract).then_inc(h_lo, 1)
                dve.wait_ge(h_turned, FREE + g + 1)
                dve.tensor_copy(hT[:, 1, :, dyn(g * S, S)], turn_ps[:, 1, :, :]).then_inc(hT_v, 1)
            if latent:
                latent_chain = s("latent_chain")
                dve.sem_inc(c_lo, FREE)
                with dve.Fori(0, B) as g:
                    ch = Chain(dve, latent_chain, g * 3, 3)
                    dve.wait_ge(ckv_mm, g + 1)
                    dve.wait_ge(c_lo, FREE + g)
                    ch.link(dve.tensor_scalar(ckv[:, :, :], ckv_ps[:, :, :], 1 / W_SCALE, None, ALU.mult))
                    ch.link(dve.tensor_tensor(sq[:, :, :], ckv[:, :, 0:LORA], ckv[:, :, 0:LORA], ALU.mult))
                    ch.link(dve.tensor_reduce(var[:, :], sq[:, :, :], X, ALU.add))
                    ch.end()
                    dve.tensor_scalar(var[:, :], var[:, :], 1 / LORA, 1e-6, ALU.mult, ALU.add).then_inc(stat_ready, 1)
                    dve.wait_ge(rstd_ready, g + 1 + B * (1 + int(ffn)))
                    for j in range(TPB):
                        last = dve.scalar_tensor_tensor(ckv[:, j, 0:LORA], ckv[:, j, 0:LORA], rstd[:, j:j + 1],
                                                        G["c_norm"][:, :], ALU.mult, ALU.mult)
                    last.then_inc(c_ready, 1)
                    dve.wait_ge(c_hi, g + 1)
                    dve.tensor_tensor(G["c"][:, dyn(g * TPB, TPB), 1, :], ckv[:, :, :],
                                      G["c"][:, dyn(g * TPB, TPB), 0, :], ALU.subtract).then_inc(c_lo, 1)
            if route:
                zeroed = s("sum_zeroed")
                dve.memset(mask_sum[:, :], 0.0).then_inc(zeroed, 1)
                dve.wait_ge(zeroed, 1)
                dve.wait_ge(consts, 2)
                with dve.Fori(0, B) as g:
                    ch = Chain(dve, route_chain, g * CHAIN, CHAIN)
                    dve.wait_ge(logit_mm, g + 1)
                    for j in range(TPB):
                        last = dve.scalar_tensor_tensor(logit[:, j, :], logit_ps[:, j, :], 1 / W_SCALE,
                                                        G["absent"][:, :], ALU.mult, ALU.add)
                    ch.link(last, G["spare"][:, 0:1])
                    for j in range(TPB):
                        last = dve.max(top[:, j, :], logit[:, j, :])
                    ch.link(last)
                    dve.tensor_scalar(ntop[:, :], top[:, :, 0], -1.0, None, ALU.mult).then_inc(top_ready, 1)
                    ch.link(dve.tensor_scalar(edge[:, :], top[:, :, TOPK - 1], -1e38, None, ALU.max))
                    for j in range(TPB):
                        last = dve.tensor_scalar(mask[:, j, :], logit[:, j, :], edge[:, j:j + 1], None, ALU.is_ge)
                    last.then_inc(mask_ready, 1)
                    dve.wait_ge(e_ready, g + 1)
                    dve.wait_ge(mask_ready, FREE + g + 1)
                    ch.link(dve.tensor_tensor(prob[:, :, :], prob[:, :, :], mask[:, :, :], ALU.mult))
                    ch.link(dve.tensor_reduce(den[:, :], prob[:, :, :], X, ALU.add))
                    ch.link(dve.reciprocal(den[:, :], den[:, :]))
                    for j in range(TPB):
                        last = dve.tensor_scalar(prob[:, j, :], prob[:, j, :], den[:, j:j + 1], 0.5, ALU.mult, ALU.mult)
                    ch.link(last)
                    dve.wait_ge(count_mm, g + 1)
                    ch.link(dve.tensor_tensor(key[:, :, :], count_ps[:, :, :], first_slot[:, :, :], ALU.add))
                    taken = same[:, :, 0, :]
                    ch.link(dve.scalar_tensor_tensor(taken, count_ps[:, :, :], float(CAP), mask[:, :, :],
                                                     ALU.is_le, ALU.mult))
                    ch.link(dve.tensor_tensor(key[:, :, :], key[:, :, :], taken, ALU.mult))
                    ch.link(dve.tensor_tensor(prob[:, :, :], prob[:, :, :], taken, ALU.mult), G["spare"][:, 0:1])
                    for j in range(TPB):
                        last = dve.max(keyt[:, j, :], key[:, j, :])
                    ch.link(last)
                    flat = keyt[:, :, :].rearrange("p j k -> p (j k)")
                    ch.link(dve.tensor_scalar(late[:, :], flat, 0.5, 1e6, ALU.is_lt, ALU.mult))
                    ch.link(dve.tensor_tensor(same[:, :, :, :], key[:, :, :].unsqueeze(2).to_broadcast([P, TPB, TOPK, E]),
                                              keyt[:, :, :].unsqueeze(3).to_broadcast([P, TPB, TOPK, E]), ALU.is_equal))
                    ch.link(dve.tensor_tensor(same[:, :, :, :], same[:, :, :, :],
                                              prob[:, :, :].unsqueeze(2).to_broadcast([P, TPB, TOPK, E]), ALU.mult))
                    ch.link(dve.tensor_reduce(G["slot_w"][:, dyn(g * TPB * TOPK, TPB * TOPK)], same[:, :, :, :].rearrange("p j k e -> p (j k) e"), X, ALU.add))
                    ch.link(dve.tensor_tensor(added[:, :], mask[:, 0, :], mask[:, 1, :], ALU.add))
                    ch.link(dve.tensor_tensor(added[:, :], added[:, :], mask[:, 2, :], ALU.add))
                    ch.link(dve.tensor_tensor(added[:, :], added[:, :], mask[:, 3, :], ALU.add))
                    ch.link(dve.tensor_tensor(mask_sum[:, :], mask_sum[:, :], added[:, :], ALU.add))
                    dve.scalar_tensor_tensor(G["slot"][:, dyn(g * TPB * TOPK, TPB * TOPK)], flat, -1.0, late[:, :],
                                             ALU.add, ALU.add).then_inc(idx_ready, 1)
                    ch.end()


def experts(nc, d, G, sem, sb, ps, tag):
    def s(name):
        return sem(f"{tag}_{name}")

    EC = 4
    NCH = E // EC
    SW = 256
    loaded = [s(f"loaded{i}") for i in range(2)]
    stored = [s(f"stored{i}") for i in range(2)]
    turned, xT_ready, gu_mm, e_ready, h_ready, y_mm, y_ready, chain = (
        s(n) for n in ("turned", "xT_ready", "gu_mm", "e_ready", "h_ready", "y_mm", "y_ready", "chain"))
    CHAIN = 3
    with ExitStack() as c, nc.Block(f"experts_{tag}") as block:
        gu = [sb(f"gu{i}", [P, EC, KD, 2 * INTER], F32, c) for i in range(2)]
        dn = [sb(f"dn{i}", [INTER, EC, D], F32, c) for i in range(2)]
        xs = [sb(f"xs{i}", [CAP, EC, D], F32, c) for i in range(2)]
        ys = [sb(f"ys{i}", [CAP, EC, D], F32, c) for i in range(2)]
        xT = sb("xT", [P, EC, KD * CAP], F32, c)
        e = sb("e", [INTER, EC, CAP], F32, c)
        hid = sb("hid", [INTER, EC, CAP], F32, c)
        t_ps = ps("t_ps", [P, EC, SW], F32, c)
        gu_ps = ps("gu_ps", [P, EC, SW], F32, c)
        y_ps = ps("ye_ps", [P, EC, D], F32, c)
        gu_d = d["gupT"].rearrange("(n m) (k p) o -> n p m k o", m=EC, p=P)
        dn_d = d["downT"].rearrange("(n m) i o -> n i m o", m=EC)
        xs_d = d["scratch_a"].rearrange("(n m s) i -> n s m i", m=EC, s=CAP)
        ys_d = d["scratch_b"].rearrange("(n m s) i -> n s m i", m=EC, s=CAP)

        @block.sync
        def _(sp):
            def load(n, par):
                for m in range(EC):
                    sp.dma_start(gu[par][:, m], gu_d[n, :, m]).then_inc(loaded[par], 16)
                sp.dma_start(dn[par][:, :, :], dn_d[n]).then_inc(loaded[par], 16)
                sp.dma_start(xs[par][:, :, :], xs_d[n]).then_inc(loaded[par], 16)

            load(0, 0)
            load(1, 1)
            for n in range(NCH):
                sp.wait_ge(y_ready, FREE + n + 1)
                sp.dma_start(ys_d[n], ys[n % 2][:, :, :]).then_inc(stored[n % 2], 16)
                if n + 2 < NCH:
                    load(n + 2, n % 2)
            for par in range(2):
                sp.wait_ge(stored[par], 16 + 16 * NCH // 2)

        LOADS = 16 * (EC + 2)

        @block.tensor
        def _(pe):
            def turn(it, n, par):
                pe.wait_ge(loaded[par], LOADS * (it + 1))
                pe.wait_ge(xT_ready, FREE + n)
                for m in range(EC):
                    for k in range(KD):
                        last = pe.transpose(t_ps[:, m, k * CAP:(k + 1) * CAP], xs[par][:, m, k * P:(k + 1) * P],
                                            G["ident"][0:CAP, 0:CAP])
                last.then_inc(turned, 1)

            def up(n, par):
                pe.wait_ge(xT_ready, FREE + n + 1)
                pe.wait_ge(h_ready, FREE + n)
                for m in range(EC):
                    for half in range(2):
                        for k in range(KD):
                            last = pe.matmul(gu_ps[0:INTER, m, half * CAP:(half + 1) * CAP],
                                             gu[par][:, m, k, half * INTER:(half + 1) * INTER],
                                             xT[:, m, k * CAP:(k + 1) * CAP], start=k == 0, stop=k == KD - 1)
                last.then_inc(gu_mm, 1)

            def down(n, par):
                pe.wait_ge(h_ready, FREE + n + 1)
                pe.wait_ge(y_ready, FREE + n)
                for m in range(EC):
                    last = pe.matmul(y_ps[0:CAP, m, :], hid[:, m, :], dn[par][:, m, :], start=True, stop=True)
                last.then_inc(y_mm, 1)

            for free in (xT_ready, h_ready, y_ready):
                pe.sem_inc(free, FREE)
            turn(0, 0, 0)
            with pe.Fori(0, NCH // 2 - 1) as it:
                for par in range(2):
                    n = it * 2 + par
                    up(n, par)
                    turn(it + par, n + 1, 1 - par)
                    down(n, par)
            it = NCH // 2 - 1
            up(2 * it, 0)
            turn(it, 2 * it + 1, 1)
            down(2 * it, 0)
            up(2 * it + 1, 1)
            down(2 * it + 1, 1)

        @block.scalar
        def _(act):
            with act.Fori(0, NCH) as n:
                act.wait_ge(turned, n + 1)
                act.activation(xT[:, :, :], t_ps[:, :, 0:KD * CAP], ACT.Copy).then_inc(xT_ready, 1)
                act.wait_ge(gu_mm, n + 1)
                act.activation(e[:, :, :], gu_ps[0:INTER, :, 0:CAP], ACT.Exp, scale=-1.0).then_inc(e_ready, 1)

        @block.vector
        def _(dve):
            for par in range(2):
                dve.sem_inc(stored[par], 16)
            with dve.Fori(0, NCH // 2) as it:
                for par in range(2):
                    n = it * 2 + par
                    ch = Chain(dve, chain, n * CHAIN, CHAIN)
                    dve.wait_ge(e_ready, n + 1)
                    ch.link(dve.tensor_scalar(e[:, :, :], e[:, :, :], 1.0, None, ALU.add))
                    ch.link(dve.reciprocal(e[:, :, :], e[:, :, :]))
                    ch.link(dve.tensor_tensor(e[:, :, :], gu_ps[0:INTER, :, 0:CAP], e[:, :, :], ALU.mult))
                    dve.tensor_tensor(hid[:, :, :], gu_ps[0:INTER, :, CAP:2 * CAP], e[:, :, :], ALU.mult).then_inc(h_ready, 1)
                    ch.end()
                    dve.wait_ge(y_mm, n + 1)
                    dve.wait_ge(stored[par], 16 * (it + 1))
                    dve.tensor_copy(ys[par][:, :, :], y_ps[0:CAP, :, :]).then_inc(y_ready, 1)

    NB = 4
    gathered = [s(f"gathered{i}") for i in range(NB)]
    cleared, combined, cchain = s("cleared"), s("combined"), s("combine_chain")
    with ExitStack() as c, nc.Block(f"combine_{tag}") as block:
        y = [sb(f"y{i}", [P, TOPK, D], F32, c) for i in range(NB)]

        @block.gpsimd
        def _(pool):
            pool.wait_ge(cleared, NB)
            for t in range(NT):
                if t >= NB:
                    pool.wait_ge(combined, t - NB + 1)
                for k in range(TOPK):
                    at = t * TOPK + k
                    pool.indirect_dma_start(
                        out=y[t % NB][:, k, :], out_offset=None, in_=d["scratch_b"],
                        in_offset=bass.IndirectOffsetOnAxis(ap=G["slot"][:, at:at + 1], axis=0),
                        bounds_check=SLOTS - 1, oob_is_err=False).then_inc(gathered[t % NB], 16)

        @block.vector
        def _(dve):
            for i in range(NB):
                dve.memset(y[i][:, :, :], 0.0).then_inc(cleared, 1)
            with dve.Fori(0, NT // NB) as it:
                for i in range(NB):
                    dve.wait_ge(gathered[i], 16 * TOPK * (it + 1))
                    at = (it * NB + i) * D
                    for k in range(TOPK):
                        xt = G["x"][:, dyn(at, D)]
                        ins = dve.scalar_tensor_tensor(xt, y[i][:, k, :], G["slot_w"][:, dyn((it * NB + i) * TOPK + k, 1)],
                                                       xt, ALU.mult, ALU.add)
                        if k < TOPK - 1:
                            ins.then_inc(cchain, 1)
                            dve.wait_ge(cchain, (it * NB + i) * (TOPK - 1) + k + 1)
                    ins.then_inc(combined, 1)


def load_l1(nc, d, G, sem, sb, ps, c):
    raw_in = [sem(f"raw_in{i}") for i in range(4)]
    high, low = sem("l1_high"), sem("l1_low")
    for n in ("w_q", "w_k", "w_v"):
        G[n] = sb(n, [P, KD, 2, H * P], F16, c)
    G["w_o"] = sb("w_o", [P, H, 2, D], F16, c)
    with ExitStack() as c1, nc.Block("load_l1") as block:
        raw = [sb(f"raw{i}", [P, 4096], F32, c1) for i in range(2)]
        src = [d[n].rearrange("(k p) q -> p k q", p=P) for n in ("wqT", "wkT", "wvT")]
        src.append(d["woT1"].rearrange("(h r) o -> r h o", r=P))
        shape = [(KD, H * P)] * 3 + [(H, D)]
        view = [raw[i % 2][:, :].rearrange("p (a b) -> p a b", a=shape[i][0]) for i in range(4)]
        parts = [G[n] for n in ("w_q", "w_k", "w_v", "w_o")]

        @block.sync
        def _(sp):
            for i in range(4):
                if i >= 2:
                    sp.wait_ge(low, i - 1)
                sp.dma_start(view[i], src[i]).then_inc(raw_in[i], 16)

        @block.scalar
        def _(act):
            for i in range(4):
                act.wait_ge(raw_in[i], 16)
                act.activation(parts[i][:, :, 0, :], view[i], ACT.Copy, scale=W_SCALE).then_inc(high, 1)

        @block.vector
        def _(dve):
            for i in range(4):
                dve.wait_ge(high, i + 1)
                dve.scalar_tensor_tensor(parts[i][:, :, 1, :], view[i], W_SCALE, parts[i][:, :, 0, :],
                                         ALU.mult, ALU.subtract).then_inc(low, 1)


def attention(nc, d, G, sem, sb, ps, tag, latent):
    def s(name):
        return sem(f"{tag}_{name}")

    NPROJ = 1 if latent else 3
    NO = H // 2 if latent else H
    scale = (NOPE + ROPE if latent else DV) ** -0.5
    proj_mm, proj_hi, proj_done = s("proj_mm"), s("proj_hi"), s("proj_done")
    s_mm, max_ready, exp_done, rinv_ready, p_ready = s("scores_mm"), s("max_ready"), s("exp_done"), s("rinv_ready"), s("p_ready")
    turned, t_hi, t_done = s("p_turned"), s("pT_hi"), s("pT_done")
    o_mm, o_hi, o_done, y_mm, y_done = s("o_mm"), s("o_hi"), s("o_done"), s("y_mm"), s("y_done")
    v_ready = s("v_ready") if latent else None
    hT = G["hT"]
    order = (3, 2, 0, 1)
    with ExitStack() as c, nc.Block(f"attention_{tag}") as block:
        qT = [sb(f"qT{i}", [P, 2, S], F16, c) for i in range(2)]
        if latent:
            v = [sb("v_batch", [P, TPB, 2, LORA], F16, c)] * 2
        else:
            kTh = [sb(f"kTh{i}", [P, 2, S], F16, c) for i in range(2)]
            v = [sb(f"v{i}", [P, TPB, 2, P], F16, c) for i in range(2)]
        p = [sb(f"p{i}", [P, CAUSAL], F32, c) for i in range(2)]
        pT = [sb(f"pT{i}", [P, 2, CAUSAL], F16, c) for i in range(2)]
        nmax = [sb(f"nmax{i}", [P, TPB], F32, c) for i in range(2)]
        scaled = sb("scaled", [P, 1], F32, c)
        total = [sb(f"total{i}", [P, TPB], F32, c) for i in range(2)]
        rinv = [sb(f"rinv{i}", [P, TPB], F32, c) for i in range(2)]
        oT = sb("oT", [P, NO, 2, S], F16, c)
        s_ps = ps("s_ps", [P, 1536], F32, c)
        t_ps = ps("pt_ps", [P, 1536], F32, c)
        o_ps = ps("o_ps", [P, S], F32, c)
        a_ps = ps("a_ps", [P, S], F32, c)

        def heads(eng, step, finish, start):
            with eng.Fori(0, B) as b:
                start(b)
                step(b, 0, 0, True, False)
                step(b, 1, 1, True, False)
                with eng.Fori(2, H - 2, 2) as h:
                    step(b, h, 0, False, False)
                    step(b, h + 1, 1, False, False)
                step(b, H - 2, 0, False, False)
                step(b, H - 1, 1, False, True)
                finish(b)

        @block.tensor
        def _(pe):
            def project(b, h, par, which):
                n = b * H + h
                pe.wait_ge(proj_done, FREE + n * NPROJ + which)
                tok = dyn(b * S, S)
                first = True
                if which < 2:
                    w = G["q_w"] if latent else (G["w_q"], G["w_k"])[which]
                    for k in range(KD):
                        for a, x in ((0, 0), (0, 1), (1, 0)):
                            last = pe.matmul(a_ps[:, :], w[:, k, a, dyn(h * P, P)], hT[:, k, x, tok],
                                             start=k + a + x == 0, stop=k * a == 1)
                else:
                    for j in range(TPB):
                        for k in range(KD):
                            for a, x in ((0, 0), (0, 1), (1, 0)):
                                last = pe.matmul(a_ps[:, j * P:(j + 1) * P], hT[:, k, a, dyn(b * S + j * P, P)],
                                                 G["w_v"][:, k, x, dyn(h * P, P)], start=k + a + x == 0, stop=k * a == 1)
                last.then_inc(proj_mm, 1)

            def scores(b, h, par, first):
                n = b * H + h
                pe.wait_ge(proj_done, FREE + n * NPROJ + (1 if latent else 2))
                if first and par == 0:
                    pe.wait_ge(y_done, FREE + b)
                for at, i in enumerate(order):
                    pe.wait_ge(exp_done, FREE + n * 4)
                    cols = (i + 1) * P
                    here = s_ps[:, Q_AT[i]:Q_AT[i] + cols]
                    for e, (a, x) in enumerate(((0, 0), (0, 1), (1, 0))):
                        keys = G["kT"][:, x, dyn(b * S, cols)] if latent else kTh[par][:, x, 0:cols]
                        last = pe.matmul(here, qT[par][:, a, i * P:(i + 1) * P], keys, start=e == 0, stop=e == 2)
                        if e == 0:
                            pe.matmul(s_ps[:, Q_AT[i] + i * P:Q_AT[i] + cols], G["ident_b"][:, :], G["mask_b"][:, :],
                                      start=False, stop=False)
                    last.then_inc(s_mm, 1)

            def turn(b, h, par):
                n = b * H + h
                pe.wait_ge(p_ready, n * 4 + 4)
                pe.wait_ge(t_done, FREE + n * 2)
                for j in (0, 1, 3, 2):
                    for i in range(j, TPB):
                        at = K_AT[j] + (i - j) * P
                        last = pe.transpose(t_ps[:, at:at + P], p[par][:, Q_AT[i] + j * P:Q_AT[i] + (j + 1) * P],
                                            G["ident"][:, :])
                    if j in (0, 2):
                        last.then_inc(turned, 1)

            def outputs(b, h, pars):
                n = b * H + h
                pe.wait_ge(t_done, FREE + n * 2 + 2)
                pe.wait_ge(o_done, FREE + b * NO + ((h >> 1) if latent else h))
                rows = P // len(pars)
                for j in range(TPB):
                    for e, (a, x) in enumerate(((0, 0), (0, 1), (1, 0))):
                        for side, par in enumerate(pars):
                            last = pe.matmul(o_ps[side * rows:(side + 1) * rows, j * P:S], v[par][:, j, a, :],
                                             pT[par][:, x, K_AT[j]:K_AT[j] + (TPB - j) * P],
                                             start=j + e == 0, stop=j == TPB - 1 and e == 2)
                last.then_inc(o_mm, 1)

            def step(b, h, par, first, last):
                if first and par == 0:
                    for which in range(NPROJ):
                        project(b, h, par, which)
                scores(b, h, par, first)
                if not last:
                    project(b, h + 1, 1 - par, 0)
                begun = not (first and par == 0)
                if begun:
                    turn(b, h - 1, 1 - par)
                if not last and not latent:
                    project(b, h + 1, 1 - par, 1)
                if latent:
                    if par == 0 and not first:
                        outputs(b, h - 1, (0, 1))
                elif begun:
                    outputs(b, h - 1, (1 - par,))
                if not last and not latent:
                    project(b, h + 1, 1 - par, 2)

            def finish(b):
                turn(b, H - 1, 1)
                outputs(b, H - 1, (0, 1) if latent else (1,))
                pe.wait_ge(o_done, FREE + (b + 1) * NO)
                w = G["vo_w"] if latent else G["w_o"]
                for i in range(TPB):
                    for m in range(NO):
                        for a, x in ((0, 0), (0, 1), (1, 0)):
                            last = pe.matmul(s_ps[:, i * D:(i + 1) * D], oT[:, m, a, i * P:(i + 1) * P], w[:, m, x, :],
                                             start=m + a + x == 0, stop=m == NO - 1 and a == 1)
                last.then_inc(y_mm, 1)

            def start(b):
                if latent:
                    pe.wait_ge(v_ready, b + 1)

            for free in (proj_done, exp_done, t_done, o_done, y_done):
                pe.sem_inc(free, FREE)
            heads(pe, step, finish, start)

        def proj_out(par, which):
            if which == 0:
                return (lambda part: qT[par][:, part, :]), a_ps[:, :]
            if which == 1:
                return (lambda part: kTh[par][:, part, :]), a_ps[:, :]
            return (lambda part: v[par][:, :, part, :]), a_ps[:, :].rearrange("p (j d) -> p j d", j=TPB)

        def proj_scale(which):
            return (scale if which == 0 else 1.0) / W_SCALE

        def o_index(b, h):
            return (h >> 1) if latent else h

        @block.scalar
        def _(act):
            def project(b, h, par, which):
                act.wait_ge(proj_mm, (b * H + h) * NPROJ + which + 1)
                to, src = proj_out(par, which)
                act.activation(to(0), src, ACT.Copy, scale=proj_scale(which)).then_inc(proj_hi, 1)

            def exps(b, h, par):
                act.wait_ge(max_ready, b * H + h + 1)
                for i in order:
                    cols = (i + 1) * P
                    act.activation(p[par][:, Q_AT[i]:Q_AT[i] + cols], s_ps[:, Q_AT[i]:Q_AT[i] + cols], ACT.Exp,
                                   bias=nmax[par][:, i:i + 1], accum_out=total[par][:, i:i + 1]).then_inc(exp_done, 1)

            def turn(b, h, par):
                n = b * H + h
                for q, (lo, hi) in enumerate(((0, 512), (512, CAUSAL))):
                    act.wait_ge(turned, n * 2 + q + 1)
                    act.activation(pT[par][:, 0, lo:hi], t_ps[:, lo:hi], ACT.Copy).then_inc(t_hi, 1)

            def outputs(b, h):
                at = o_index(b, h)
                act.wait_ge(o_mm, b * NO + at + 1)
                act.activation(oT[:, at, 0, :] if isinstance(at, int) else oT[:, dyn(at, 1), 0, :].rearrange("p a c -> p (a c)"),
                               o_ps[:, :], ACT.Copy, scale=O_SCALE / P_SCALE).then_inc(o_hi, 1)

            def step(b, h, par, first, last):
                if first and par == 0:
                    for which in range(NPROJ):
                        project(b, h, par, which)
                if not last:
                    project(b, h + 1, 1 - par, 0)
                begun = not (first and par == 0)
                if begun:
                    turn(b, h - 1, 1 - par)
                exps(b, h, par)
                if not last and not latent:
                    project(b, h + 1, 1 - par, 1)
                if (par == 0 and not first) if latent else begun:
                    outputs(b, h - 1)
                if not last and not latent:
                    project(b, h + 1, 1 - par, 2)

            def finish(b):
                turn(b, H - 1, 1)
                outputs(b, H - 1)

            def start(b):
                if latent:
                    act.wait_ge(y_mm, FREE + b)
                    act.activation(v[0][:, :, :, :], G["c"][:, dyn(b * TPB, TPB), :, 0:LORA], ACT.Copy).then_inc(v_ready, 1)

            act.sem_inc(y_mm, FREE)
            heads(act, step, finish, start)

        @block.vector
        def _(dve):
            def project(b, h, par, which):
                dve.wait_ge(proj_hi, (b * H + h) * NPROJ + which + 1)
                to, src = proj_out(par, which)
                dve.scalar_tensor_tensor(to(1), src, proj_scale(which), to(0), ALU.mult, ALU.subtract).then_inc(proj_done, 1)

            def maxima(b, h, par):
                n = b * H + h
                for i, upto in zip(order, (1, 3, 3, 4)):
                    dve.wait_ge(s_mm, n * 4 + upto)
                    last = dve.tensor_reduce(nmax[par][:, i:i + 1], s_ps[:, Q_AT[i]:Q_AT[i] + (i + 1) * P], X, ALU.max,
                                             negate=True)
                last.then_inc(max_ready, 1)

            def inverse(b, h, par):
                dve.wait_ge(exp_done, FREE + (b * H + h) * 4 + 4)
                dve.reciprocal(rinv[par][:, :], total[par][:, :]).then_inc(rinv_ready, 1)

            def turn(b, h, par):
                n = b * H + h
                for q, (lo, hi) in enumerate(((0, 512), (512, CAUSAL))):
                    dve.wait_ge(t_hi, n * 2 + q + 1)
                    dve.tensor_tensor(pT[par][:, 1, lo:hi], t_ps[:, lo:hi], pT[par][:, 0, lo:hi],
                                      ALU.subtract).then_inc(t_done, 1)

            def outputs(b, h):
                at = o_index(b, h)
                dve.wait_ge(o_hi, b * NO + at + 1)

                def part(n):
                    return oT[:, at, n, :] if isinstance(at, int) else oT[:, dyn(at, 1), n, :].rearrange("p a c -> p (a c)")
                dve.scalar_tensor_tensor(part(1), o_ps[:, :], O_SCALE / P_SCALE, part(0), ALU.mult,
                                         ALU.subtract).then_inc(o_done, 1)

            def step(b, h, par, first, last):
                if first and par == 0:
                    for which in range(NPROJ):
                        project(b, h, par, which)
                maxima(b, h, par)
                if not last:
                    project(b, h + 1, 1 - par, 0)
                begun = not (first and par == 0)
                if begun:
                    turn(b, h - 1, 1 - par)
                inverse(b, h, par)
                if not last and not latent:
                    project(b, h + 1, 1 - par, 1)
                if (par == 0 and not first) if latent else begun:
                    outputs(b, h - 1)
                if not last and not latent:
                    project(b, h + 1, 1 - par, 2)

            def finish(b):
                turn(b, H - 1, 1)
                outputs(b, H - 1)
                dve.wait_ge(y_mm, FREE + b + 1)
                dve.scalar_tensor_tensor(G["x"][:, dyn(b * TPB * D, TPB * D)], s_ps[:, 0:TPB * D], 1 / (W_SCALE * O_SCALE),
                                         G["x"][:, dyn(b * TPB * D, TPB * D)], ALU.mult, ALU.add).then_inc(y_done, 1)

            heads(dve, step, finish, lambda b: None)

        @block.gpsimd
        def _(pool):
            def step(b, h, par, first, last):
                pool.wait_ge(rinv_ready, b * H + h + 1)
                pool.tensor_tensor(scaled[:, 0:1], rinv[par][:, 0:1], rinv[par][:, 0:1], ALU.add)
                for i in order:
                    part = p[par][:, Q_AT[i]:Q_AT[i] + (i + 1) * P]
                    pool.tensor_scalar(part, part, rinv[par][:, i:i + 1], P_SCALE, ALU.mult, ALU.mult).then_inc(p_ready, 1)

            heads(pool, step, lambda b: None, lambda b: None)


def build(nc, d, out, until=99):
    ctx = ExitStack()
    with ctx:
        held = []

        def sem(name):
            held.append(nc.alloc_semaphore(name=name))
            return held[-1]

        def renew_semaphores():
            nc.clear_and_free_semaphores(held)
            held.clear()
            nc.all_engine_barrier()

        taken = set(d)

        def fresh(name):
            while name in taken:
                name += "_"
            taken.add(name)
            return name

        def sb(name, shape, dt=F32, c=ctx):
            return c.enter_context(nc.sbuf_tensor(fresh(name), shape, dt))

        def ps(name, shape, dt=F32, c=ctx):
            return c.enter_context(nc.psum_tensor(fresh(name), shape, dt))

        G = {"spare": sb("spare", [P, 1])}
        G["x"] = sb("x", [P, NT * D])
        G["ident"] = sb("ident", [P, P])
        G["ident_h"] = sb("ident_h", [P, P], F16)
        G["ident_b"] = sb("ident_b", [P, P], BF16)
        G["mask_b"] = sb("mask_b", [P, P], BF16)
        G["ffn_w"] = sb("ffn_w", [P, KD, 3, D], BF16)
        G["gate"] = sb("gate", [P, KD, 2, E], F16)
        G["absent"] = sb("absent", [P, E])
        G["tri_b"] = sb("tri_b", [P, P], BF16)
        G["ones_b"] = sb("ones_b", [P, P], BF16)
        G["hT"] = sb("hT", [P, KD, 2, T], F16)
        G["slot"] = sb("slot", [P, NT * TOPK], U32)
        G["slot_w"] = sb("slot_w", [P, NT * TOPK])
        prepare(nc, d, G, sem, sb, ps)
        if until > 1:
            with ExitStack() as c0:
                G["kT"] = sb("kT", [P, 2, T], F16, c0)
                G["c"] = sb("c_nat", [P, NT, 2, P], F16, c0)
                G["q_w"] = sb("q_w", [P, KD, 2, H * P], F16, c0)
                G["vo_w"] = sb("vo_w", [P, H // 2, 2, D], F16, c0)
                G["kv_w"] = sb("kv_w", [P, KD, 2, P], F16, c0)
                G["c_norm"] = sb("c_norm", [P, LORA], F32, c0)
                absorb(nc, d, G, sem, sb, ps)
                tiles(nc, d, G, sem, sb, ps, "a", ffn=True, latent=True)
                if until > 2:
                    attention(nc, d, G, sem, sb, ps, "l0", latent=True)
        if until > 3:
            tiles(nc, d, G, sem, sb, ps, "b", ffn=True, route=True)
        for rnd in range(2):
            if until > 4 + 2 * rnd:
                experts(nc, d, G, sem, sb, ps, f"m{rnd}")
            if rnd == 0 and until > 5:
                renew_semaphores()
                with ExitStack() as c1:
                    load_l1(nc, d, G, sem, sb, ps, c1)
                    tiles(nc, d, G, sem, sb, ps, "c")
                    attention(nc, d, G, sem, sb, ps, "l1", latent=False)
                tiles(nc, d, G, sem, sb, ps, "d", route=True)
        stored = sem("stored")
        with nc.Block("store") as block:
            @block.sync
            def _(sp):
                sp.dma_start(out.rearrange("(t p) d -> p t d", p=P), G["x"][:, :].rearrange("p (t d) -> p t d", d=D)).then_inc(stored, 16)
                sp.wait_ge(stored, 16)


kernel_until = 99


def kernel(**inputs):
    import numpy as _np
    import concourse.bacc as _bacc
    from concourse.bass_utils import run_bass_kernel_spmd as _run

    a = {k: _np.asarray(v) for k, v in inputs.items()}
    wq = a["L0_attn_Wq"]
    heads = wq.reshape(H, NOPE + ROPE, D)

    def turned(name):
        w = a[name]
        return w.reshape(-1, w.shape[-1]).T

    arrays = {
        "x": a["L0_attn_hidden_states"].reshape(T, D),
        "wq": wq,
        "wpeT": heads[:, NOPE:].transpose(2, 0, 1).reshape(D, H * ROPE),
        "kvaT": a["L0_attn_Wkva"][:LORA].T,
        "kpe_w": a["L0_attn_Wkva"][LORA:],
        "c_norm": _np.broadcast_to(a["L0_attn_kv_a_norm_weight"], (P, LORA)),
        "kvb": a["L0_attn_Wkvb"],
        "woT": turned("L0_attn_Wo"),
        "cos": a["L0_attn_cos"],
        "sin": a["L0_attn_sin"],
        "ffn_wT": turned("L0_ffn_weight"),
        "rramT": turned("L0_ffn_rram_variation"),
        "wkT": turned("L1_attn_W_K"),
        "wqT": turned("L1_attn_W_Q"),
        "wvT": turned("L1_attn_W_V"),
        "woT1": turned("L1_attn_W_O"),
        "gate_w": a["L1_ffn_gate_weight"],
        "gupT": a["L1_ffn_gate_up_proj"].transpose(0, 2, 1),
        "downT": a["L1_ffn_down_proj"].transpose(0, 2, 1),
        "o2n": a["L1_ffn_old_to_new"].reshape(E_OLD, 1),
    }
    arrays = {k: _np.ascontiguousarray(v) for k, v in arrays.items()}
    nc = _bacc.Bacc("TRN2", target_bir_lowering=False, num_devices=1)
    d = {k: nc.dram_tensor(k, v.shape, mybir.dt.from_np(v.dtype), kind="ExternalInput").ap() for k, v in arrays.items()}
    for name in ("scratch_a", "scratch_b"):
        d[name] = nc.dram_tensor(name, (SLOTS, D), F32).ap()
    out = nc.dram_tensor("out", (T, D), F32, kind="ExternalOutput").ap()
    build(nc, d, out, kernel_until)
    r = _run(nc, [arrays], core_ids=[0])
    return r.results[0]["out"].reshape(B, S, D)
```

```python
from contextlib import ExitStack

import numpy as np
import concourse.bass as bass
from concourse import mybir

F32 = mybir.dt.float32
F16 = mybir.dt.float16
BF16 = mybir.dt.bfloat16
I32 = mybir.dt.int32
U32 = mybir.dt.uint32
ALU = mybir.AluOpType
ACT = mybir.ActivationFunctionType
X = mybir.AxisListType.X

P = 128
T, D = 2048, 256
NT = T // P
S, B = 512, 4
TPB = S // P
KD = D // P
H = 16
NOPE, ROPE, LORA, DV = 128, 64, 64, 128
E_OLD, E, INTER, CAP, TOPK = 128, 48, 96, 96, 8
KG = 4
SLOTS = E * CAP

W_SCALE = 1024.0
P_SCALE = 4096.0
O_SCALE = 16.0

FREE = 1

Q_AT = {3: 0, 2: 512, 0: 896, 1: 1024}
K_AT = {2: 0, 0: 256, 1: 768, 3: 1152}
CAUSAL = 1280
HALF_AT = ((0, 768), (768, CAUSAL))


def dyn(start, size):
    return bass.ds(start, size)



def moved(pool, live, signal, due, t, always, move):
    for k in range(0, TOPK, KG):
        at = t * TOPK + k
        if always and k == 0:
            for i in range(KG):
                move(at + i).then_inc(signal, 16)
            pool.reg_add(due, due, 16 * KG)
            continue
        some = pool.value_load(live[0:1, at:at + 1], min_val=0, max_val=1)
        pool.reg_add(due, due, some * (16 * KG))
        with pool.If(some > 0):
            for i in range(KG):
                move(at + i).then_inc(signal, 16)


class Chain:

    def __init__(self, eng, done, start, per):
        self.eng, self.done, self.start, self.per, self.n = eng, done, start, per, 0

    def link(self, ins, spare=None):
        self.n += 1
        ins.then_inc(self.done, 1)
        self.eng.wait_ge(self.done, self.start + self.n)
        if spare is not None:
            self.eng.memset(spare, 0.0)

    def end(self):
        assert self.n == self.per, self.n


def prepare(nc, d, G, sem, sb, ps):
    loaded_x, loaded_w, loaded_g = sem("loaded_x"), sem("loaded_w"), sem("loaded_gate")
    zeroed, consts = sem("consts_zeroed"), sem("consts")
    chain = sem("prep_chain")
    picked, gate_mm, gate_hi, scratch = sem("gate_picked"), sem("gate_mm"), sem("gate_hi"), sem("slots_zeroed")
    zero_ready = sem("zero_ready")
    ZR = 12
    with ExitStack() as c, nc.Block("prepare") as block:
        w = sb("w_raw", [P, KD, D], F32, c)
        rram = sb("rram_raw", [P, KD, D], F32, c)
        sign = sb("sign", [P, KD, D], F32, c)
        gate = sb("gate_raw", [P, D], F32, c)
        o2n_i = sb("o2n_i", [P, 1], I32, c)
        o2n = sb("o2n", [P, 1], F32, c)
        cols = sb("cols", [P, E], F32, c)
        sel = sb("sel", [P, E], F32, c)
        ones = sb("ones", [P, P], F32, c)
        zero = sb("zero", [P, ZR * D], F32, c)
        gp = ps("gp", [P, KD + 1, E], F32, c)

        @block.sync
        def _(sp):
            sp.dma_start(w[:, :, :], d["ffn_wT"].rearrange("(k p) o -> p k o", p=P)).then_inc(loaded_w, 16)
            sp.dma_start(rram[:, :, :], d["rramT"].rearrange("(k p) o -> p k o", p=P)).then_inc(loaded_w, 16)
            sp.dma_start(gate[:, :], d["gate_w"]).then_inc(loaded_g, 16)
            sp.dma_start(o2n_i[:, :], d["o2n"]).then_inc(loaded_g, 16)
            sp.dma_start(G["x"][:, :].rearrange("p (t d) -> p t d", d=D), d["x"].rearrange("(t p) d -> p t d", p=P)).then_inc(loaded_x, 16)
            sp.wait_ge(zero_ready, 1)
            for table in ("scratch_a", "scratch_b"):
                rows = d[table].rearrange("(a p r) d -> a p (r d)", p=P, r=ZR)
                for i in range(SLOTS // (P * ZR)):
                    sp.dma_start(rows[i], zero[:, :]).then_inc(scratch, 16)
            sp.wait_ge(scratch, 16 * 2 * SLOTS // (P * ZR))
            sp.wait_ge(loaded_x, 16)

        @block.gpsimd
        def _(pool):
            for t, v in ((G["ident"], 0.0), (G["ident_h"], 0.0), (G["ident_b"], 0.0), (G["mask_b"], 0.0),
                         (G["tri_b"], 1.0), (G["ones_b"], 1.0), (ones, 1.0)):
                pool.memset(t[:, :], v).then_inc(zeroed, 1)
            pool.wait_ge(zeroed, 7)
            for t in (G["ident"], G["ident_h"], G["ident_b"]):
                pool.affine_select(out=t[:, :], in_=t[:, :], compare_op=ALU.not_equal, fill=1.0, base=0,
                                   pattern=[[-1, P]], channel_multiplier=1).then_inc(consts, 1)
            pool.affine_select(out=G["mask_b"][:, :], in_=G["mask_b"][:, :], compare_op=ALU.is_ge, fill=-1e30,
                               base=0, pattern=[[-1, P]], channel_multiplier=1).then_inc(consts, 1)
            pool.affine_select(out=G["tri_b"][:, :], in_=G["tri_b"][:, :], compare_op=ALU.is_ge, fill=0.0,
                               base=0, pattern=[[1, P]], channel_multiplier=-1).then_inc(consts, 1)
            pool.iota(cols[:, :], pattern=[[1, E]], base=0, channel_multiplier=0,
                      allow_small_or_imprecise_dtypes=True).then_inc(consts, 1)

        @block.scalar
        def _(act):
            act.wait_ge(gate_mm, 1)
            act.activation(G["gate"][:, :, 0, :], gp[:, 0:KD, :], ACT.Copy, scale=W_SCALE).then_inc(gate_hi, 1)

        @block.tensor
        def _(pe):
            pe.wait_ge(picked, 1)
            for k in range(KD):
                pe.matmul(gp[:, k, :], gate[:, k * P:(k + 1) * P], sel[:, :], start=True, stop=True)
            pe.matmul(gp[:, KD, :], ones[:, :], sel[:, :], start=True, stop=True).then_inc(gate_mm, 1)

        @block.vector
        def _(dve):
            ch = Chain(dve, chain, 0, 10)
            dve.memset(zero[:, :], 0.0).then_inc(zero_ready, 1)
            dve.wait_ge(loaded_g, 32)
            dve.wait_ge(consts, 6)
            ch.link(dve.tensor_copy(o2n[:, :], o2n_i[:, :]))
            dve.tensor_scalar(sel[:, :], cols[:, :], o2n[:, 0:1], None, ALU.is_equal).then_inc(picked, 1)
            dve.wait_ge(loaded_w, 32)
            ch.link(dve.tensor_scalar(sign[:, :, :], w[:, :, :], 0.2, None, ALU.is_gt))
            ch.link(dve.scalar_tensor_tensor(sign[:, :, :], w[:, :, :], -0.2, sign[:, :, :], ALU.is_lt, ALU.subtract))
            ch.link(dve.scalar_tensor_tensor(w[:, :, :], sign[:, :, :], -0.6, rram[:, :, :], ALU.mult, ALU.add))
            for part in range(3):
                ch.link(dve.tensor_copy(G["ffn_w"][:, :, part, :], w[:, :, :]))
                if part < 2:
                    ch.link(dve.tensor_tensor(w[:, :, :], w[:, :, :], G["ffn_w"][:, :, part, :], ALU.subtract))
            dve.wait_ge(gate_hi, 1)
            dve.scalar_tensor_tensor(G["gate"][:, :, 1, :], gp[:, 0:KD, :], W_SCALE, G["gate"][:, :, 0, :],
                                     ALU.mult, ALU.subtract)
            ch.link(dve.tensor_scalar(G["absent"][:, :], gp[:, KD, :], 0.5, -3e38, ALU.is_lt, ALU.mult))
            ch.end()


def absorb(nc, d, G, sem, sb, ps):
    loaded = {n: sem(f"loaded_{n}") for n in ("wq", "wk", "wpe", "wv", "wo", "kva", "rope")}
    rot_made, rot_mm, rot_sq, pe_mm = sem("rot_made"), sem("rot_mm"), sem("rot_sq"), sem("rope_mm")
    swap0, swap1, chain = sem("swap_zeroed"), sem("swap_made"), sem("absorb_chain")
    filled, high, done = sem("absorb_filled"), sem("absorb_high"), sem("absorb_done")
    q_w, vo_w, kv_w = G["q_w"], G["vo_w"], G["kv_w"]
    HPB = 4
    with ExitStack() as c, nc.Block("absorb") as block:
        wq = sb("wq", [P, H, D], F32, c)
        wk = sb("wk", [P, H, LORA], F32, c)
        wv = sb("wv", [P, H, LORA], F32, c)
        wo = sb("wo", [P, H, D], F32, c)
        wpe = sb("wpe", [P, KD, H * ROPE], F32, c)
        kva = sb("kva", [P, KD, LORA], F32, c)
        kpe = sb("kpe", [ROPE, D], F32, c)
        cs = sb("cs", [ROPE, 2], F32, c)
        swap = sb("swap", [ROPE, ROPE], F32, c)
        rot = sb("rot", [ROPE, ROPE], F32, c)
        rr = sb("rr", [ROPE, ROPE], F32, c)
        bank = [ps(f"ab{i}", [P, 512], F32, c) for i in range(4)]
        rp = ps("rp", [P, 4, ROPE], F32, c)

        @block.sync
        def _(sp):
            sp.dma_start(cs[:, 0:1], d["cos"].rearrange("a r -> r a")).then_inc(loaded["rope"], 16)
            sp.dma_start(cs[:, 1:2], d["sin"].rearrange("a r -> r a")).then_inc(loaded["rope"], 16)
            sp.dma_start(kpe[:, :], d["kpe_w"]).then_inc(loaded["rope"], 16)
            sp.dma_start(kva[:, :, :], d["kvaT"].rearrange("(k p) l -> p k l", p=P)).then_inc(loaded["kva"], 16)
            sp.dma_start(G["c_norm"][:, :], d["c_norm"]).then_inc(loaded["kva"], 16)
            kvb = d["kvb"].rearrange("(h r) l -> r h l", r=NOPE + DV)
            sp.dma_start(wq[:, :, :], d["wq"].rearrange("(h r) i -> r h i", r=NOPE + ROPE)[0:NOPE]).then_inc(loaded["wq"], 16)
            sp.dma_start(wk[:, :, :], kvb[0:NOPE]).then_inc(loaded["wk"], 16)
            sp.dma_start(wpe[:, :, :], d["wpeT"].rearrange("(k p) q -> p k q", p=P)).then_inc(loaded["wpe"], 16)
            sp.dma_start(wv[:, :, :], kvb[NOPE:NOPE + DV]).then_inc(loaded["wv"], 16)
            sp.dma_start(wo[:, :, :], d["woT"].rearrange("(h r) o -> r h o", r=DV)).then_inc(loaded["wo"], 16)

        @block.gpsimd
        def _(pool):
            pool.memset(swap[:, :], 0.0).then_inc(swap0, 1)
            pool.wait_ge(swap0, 1)
            half = ROPE // 2
            pool.affine_select(out=swap[:, :], in_=swap[:, :], compare_op=ALU.not_equal, fill=-1.0, base=half,
                               pattern=[[-1, ROPE]], channel_multiplier=1).then_inc(swap0, 1)
            pool.wait_ge(swap0, 2)
            pool.affine_select(out=swap[:, :], in_=swap[:, :], compare_op=ALU.not_equal, fill=1.0, base=-half,
                               pattern=[[-1, ROPE]], channel_multiplier=1).then_inc(swap1, 1)

        @block.tensor
        def _(pe):
            pe.wait_ge(rot_made, 1)
            pe.matmul(rp[0:ROPE, 0, :], rot[:, :], rot[:, :], start=True, stop=True).then_inc(rot_mm, 1)
            pe.wait_ge(rot_sq, 1)
            for k in range(KD):
                last = pe.matmul(rp[:, 1 + k, :], kpe[:, k * P:(k + 1) * P], rr[:, :], start=True, stop=True)
            last.then_inc(pe_mm, 1)
            pe.wait_ge(loaded["wq"], 16)
            pe.wait_ge(loaded["wk"], 16)
            for g in range(H // HPB):
                for hh in range(HPB):
                    h = g * HPB + hh
                    for k in range(KD):
                        at = (k * HPB + hh) * LORA
                        last = pe.matmul(bank[g][:, at:at + LORA], wq[:, h, k * P:(k + 1) * P], wk[:, h, :],
                                         start=True, stop=True)
                last.then_inc(filled, 1)
            pe.wait_ge(loaded["wv"], 16)
            pe.wait_ge(loaded["wo"], 16)
            for g in range(H // 4):
                pe.wait_ge(done, g + 1)
                for hh in range(4):
                    h = g * 4 + hh
                    last = pe.matmul(bank[g][(hh % 2) * 64:(hh % 2) * 64 + 64, (hh // 2) * D:(hh // 2 + 1) * D],
                                     wv[:, h, :], wo[:, h, :], start=True, stop=True)
                last.then_inc(filled, 1)

        def nope(g, part):
            return q_w[:, :, part, g * HPB * P:(g + 1) * HPB * P].rearrange("p k (h c) -> p k h c", h=HPB)[:, :, :, 0:LORA]

        def rope(k, part):
            return q_w[:, k, part, :].rearrange("p (h c) -> p h c", h=H)[:, :, LORA:P]

        def raw_rope(k):
            return wpe[:, k, :].rearrange("p (h c) -> p h c", h=H)

        @block.scalar
        def _(act):
            act.wait_ge(loaded["wpe"], 16)
            for k in range(KD):
                act.activation(rope(k, 0), raw_rope(k), ACT.Copy, scale=W_SCALE)
            act.wait_ge(loaded["kva"], 32)
            act.activation(kv_w[:, :, 0, 0:LORA], kva[:, :, :], ACT.Copy, scale=W_SCALE)
            act.wait_ge(pe_mm, 1)
            act.activation(kv_w[:, :, 0, LORA:P], rp[:, 1:3, :], ACT.Copy, scale=W_SCALE).then_inc(high, 1)
            for g in range(H // HPB):
                act.wait_ge(filled, g + 1)
                for k in range(KD):
                    last = act.activation(nope(g, 0)[:, k], bank[g][:, k * 256:(k + 1) * 256].rearrange("p (h c) -> p h c", h=HPB),
                                          ACT.Copy, scale=W_SCALE)
                last.then_inc(high, 1)
            for g in range(H // 4):
                act.wait_ge(filled, 4 + g + 1)
                act.activation(vo_w[:, 2 * g:2 * g + 2, 0, :], bank[g][:, :].rearrange("p (a o) -> p a o", a=2),
                               ACT.Copy, scale=W_SCALE).then_inc(high, 1)

        @block.vector
        def _(dve):
            ch = Chain(dve, chain, 0, 2)
            dve.wait_ge(loaded["rope"], 48)
            dve.wait_ge(swap1, 1)
            ch.link(dve.tensor_scalar(rot[:, :], swap[:, :], cs[:, 1:2], None, ALU.mult))
            dve.scalar_tensor_tensor(rot[:, :], G["ident"][0:ROPE, 0:ROPE], cs[:, 0:1], rot[:, :],
                                     ALU.mult, ALU.add).then_inc(rot_made, 1)
            dve.wait_ge(rot_mm, 1)
            dve.tensor_copy(rr[:, :], rp[0:ROPE, 0, :]).then_inc(rot_sq, 1)
            dve.wait_ge(high, 1)
            for k in range(KD):
                dve.scalar_tensor_tensor(rope(k, 1), raw_rope(k), W_SCALE, rope(k, 0), ALU.mult, ALU.subtract)
            dve.scalar_tensor_tensor(kv_w[:, :, 1, 0:LORA], kva[:, :, :], W_SCALE, kv_w[:, :, 0, 0:LORA],
                                     ALU.mult, ALU.subtract)
            dve.scalar_tensor_tensor(kv_w[:, :, 1, LORA:P], rp[:, 1:3, :], W_SCALE, kv_w[:, :, 0, LORA:P],
                                     ALU.mult, ALU.subtract)
            for g in range(H // HPB):
                dve.wait_ge(high, g + 2)
                for k in range(KD):
                    last = dve.scalar_tensor_tensor(nope(g, 1)[:, k], bank[g][:, k * 256:(k + 1) * 256].rearrange("p (h c) -> p h c", h=HPB),
                                                    W_SCALE, nope(g, 0)[:, k], ALU.mult, ALU.subtract)
                last.then_inc(done, 1)
            for g in range(H // 4):
                dve.wait_ge(high, 4 + g + 2)
                last = dve.scalar_tensor_tensor(vo_w[:, 2 * g:2 * g + 2, 1, :], bank[g][:, :].rearrange("p (a o) -> p a o", a=2),
                                                W_SCALE, vo_w[:, 2 * g:2 * g + 2, 0, :], ALU.mult, ALU.subtract)
            ch.link(last)
            ch.end()



def tiles(nc, d, G, sem, sb, ps, tag, ffn=False, latent=False, route=False):
    def s(name, used=True):
        return sem(f"{tag}_{name}") if used else None

    W = TPB * D
    x, hT = G["x"], G["hT"]
    stat_ready, rstd_ready, chain = s("stat_ready"), s("rstd_ready"), s("chain")
    consts = s("consts")
    q_ready, q_turned, qT_ready, y_ready, x_added = (
        s(n, ffn) for n in ("q_ready", "q_turned", "qT_ready", "y_ready", "x_added"))
    h_ready, h_hi, h_lo, h_turned = s("h_ready"), s("h_hi"), s("h_lo"), s("h_turned")
    hT_a, hT_v = s("hT_by_act"), s("hT_by_dve")
    ckv_mm, c_ready, c_hi, c_lo, k_turned, kT_ready = (
        s(n, latent) for n in ("ckv_mm", "c_ready", "c_hi", "c_lo", "k_turned", "kT_ready"))
    logit_mm, top_ready, e_ready, mask_ready, count_mm = (
        s(n, route) for n in ("logit_mm", "top_ready", "e_ready", "mask_ready", "count_mm"))
    idx_ready, scattered, route_chain, held_ready, live_mm = (
        s(n, route) for n in ("idx_ready", "scattered", "route_chain", "held_ready", "live_mm"))
    norms = int(ffn) + 1 + int(latent)
    LN_CHAIN, FFN_CHAIN = 2, 2
    with ExitStack() as c, nc.Block(f"tiles_{tag}") as block:
        stats = sb("stats", [P, TPB, 6], F32, c)
        mv = sb("mv", [P, TPB, 2], F32, c)
        var = sb("var", [P, TPB], F32, c)
        rstd = sb("rstd", [P, TPB], F32, c)
        minus_half = sb("minus_half", [P, TPB], F32, c)
        h = sb("h", [P, NT * D if route else W], F32, c)
        h_parts = sb("h_parts", [P, 2, W], F16, c)
        turn_ps = ps("turn_ps", [P, KD, 2, S], F16, c)
        if ffn:
            above = sb("above", [P, W], BF16, c)
            q = sb("q", [P, NT * D], BF16, c)
            qT = sb("qT", [P, KD, S], BF16, c)
            q_ps = ps("q_ps", [P, KD, S], BF16, c)
            y_ps = ps("y_ps", [P, W], F32, c)
        if latent:
            ckv = sb("ckv", [P, TPB, P], F32, c)
            sq = sb("sq", [P, TPB, LORA], F32, c)
            ckv_ps = ps("ckv_ps", [P, TPB, P], F32, c)
            k_ps = ps("k_ps", [P, 2, S], F16, c)
        if route:
            logit = sb("logit", [P, TPB, E], F32, c)
            top = sb("top", [P, TPB, TOPK], F32, c)
            edge = sb("edge", [P, TPB], F32, c)
            ntop = sb("ntop", [P, TPB], F32, c)
            mask = sb("mask", [P, TPB, E], BF16, c)
            mask_sum = sb("mask_sum", [P, E], BF16, c)
            added = sb("added", [P, E], BF16, c)
            prob = sb("prob", [P, TPB, E], F32, c)
            key = sb("key", [P, TPB, E], F32, c)
            keyt = sb("keyt", [P, TPB, TOPK], F32, c)
            late = sb("late", [P, TPB * TOPK], F32, c)
            most = sb("most", [P, 1], F32, c)
            held = sb("held", [P, TPB * TOPK], BF16, c)
            den = sb("den", [P, TPB], F32, c)
            first_slot = sb("first_slot", [P, TPB, E], F32, c)
            same = sb("same", [P, TPB, TOPK, E], F32, c)
            logit_ps = ps("logit_ps", [P, TPB, E], F32, c)
            count_ps = ps("count_ps", [P, TPB, E], F32, c)
            live_ps = ps("live_ps", [P, TPB * TOPK], F32, c)
            CHAIN = 23

        def h_of(g):
            return h[:, dyn(g * W, W)] if route else h[:, :]

        @block.gpsimd
        def _(pool):
            pool.memset(minus_half[:, :], -0.5).then_inc(consts, 1)
            if route:
                pool.iota(first_slot[:, :, :], pattern=[[0, TPB], [CAP, E]], base=0, channel_multiplier=0,
                          allow_small_or_imprecise_dtypes=True).then_inc(consts, 1)
            pool.wait_ge(consts, 1 + int(route))
            with pool.Fori(0, norms * B) as n:
                pool.wait_ge(stat_ready, n + 1)
                pool.tensor_tensor(rstd[:, :], var[:, :], minus_half[:, :], ALU.pow).then_inc(rstd_ready, 1)
            if route:
                due = pool.alloc_register(f"{tag}_scatters_due")
                pool.reg_mov(due, 0)
                for t in range(NT):
                    if t % TPB == 0:
                        pool.wait_ge(idx_ready, FREE + t // TPB + 1)
                    moved(pool, G["live"], scattered, due, t, t == 0, lambda at: pool.indirect_dma_start(
                        out=d["scratch_a"], out_offset=bass.IndirectOffsetOnAxis(ap=G["slot"][:, at:at + 1], axis=0),
                        in_=h[:, t * D:(t + 1) * D], in_offset=None, bounds_check=SLOTS - 1, oob_is_err=False))
                pool.wait_ge(scattered, due)
                pool.free_register(due)

        @block.scalar
        def _(act):
            act.sem_inc(h_turned, FREE)
            if ffn:
                with act.Fori(0, B) as g:
                    act.wait_ge(q_turned, g + 1)
                    act.activation(qT[:, :, :], q_ps[:, :, :], ACT.Copy).then_inc(qT_ready, 1)
            with act.Fori(0, B) as g:
                act.wait_ge(h_ready, g + 1)
                act.wait_ge(h_turned, FREE + g)
                act.activation(h_parts[:, 0, :], h_of(g), ACT.Copy).then_inc(h_hi, 1)
                act.wait_ge(h_turned, FREE + g + 1)
                act.activation(hT[:, 0, :, dyn(g * S, S)], turn_ps[:, 0, :, :], ACT.Copy).then_inc(hT_a, 1)
            if latent:
                with act.Fori(0, B) as g:
                    act.wait_ge(c_ready, FREE + g + 1)
                    act.activation(G["c"][:, dyn(g * TPB, TPB), 0, :], ckv[:, :, :], ACT.Copy).then_inc(c_hi, 1)
                    act.wait_ge(k_turned, g + 1)
                    act.activation(G["kT"][:, :, dyn(g * S, S)], k_ps[:, :, :], ACT.Copy).then_inc(kT_ready, 1)
            if route:
                with act.Fori(0, B) as g:
                    act.wait_ge(top_ready, g + 1)
                    for j in range(TPB):
                        last = act.activation(prob[:, j, :], logit[:, j, :], ACT.Exp, bias=ntop[:, j:j + 1])
                    last.then_inc(e_ready, 1)

        @block.tensor
        def _(pe):
            for free in (hT_a, hT_v, qT_ready, x_added, c_ready, kT_ready, mask_ready, idx_ready):
                if free is not None:
                    pe.sem_inc(free, FREE)
            if ffn:
                with pe.Fori(0, B) as g:
                    pe.wait_ge(q_ready, g + 1)
                    pe.wait_ge(qT_ready, FREE + g)
                    for j in range(TPB):
                        for k in range(KD):
                            last = pe.transpose(q_ps[:, k, j * P:(j + 1) * P],
                                                q[:, dyn(g * W + (j * D + k * P), P)], G["ident_b"][:, :])
                    last.then_inc(q_turned, 1)
                    pe.wait_ge(qT_ready, FREE + g + 1)
                    pe.wait_ge(x_added, FREE + g)
                    for j in range(TPB):
                        for k in range(KD):
                            for part in range(3):
                                last = pe.matmul(y_ps[:, j * D:(j + 1) * D], qT[:, k, j * P:(j + 1) * P],
                                                 G["ffn_w"][:, k, part, :], start=k + part == 0, stop=k * part == 2)
                    last.then_inc(y_ready, 1)
            with pe.Fori(0, B) as g:
                pe.wait_ge(h_lo, g + 1)
                pe.wait_ge(hT_a, FREE + g)
                pe.wait_ge(hT_v, FREE + g)
                for k in range(KD):
                    for part in range(2):
                        for j in range(TPB):
                            at = j * D + k * P
                            last = pe.transpose(turn_ps[:, k, part, j * P:(j + 1) * P], h_parts[:, part, at:at + P],
                                                G["ident_h"][:, :])
                last.then_inc(h_turned, 1)
            if latent:
                pe.wait_ge(hT_a, FREE + B)
                pe.wait_ge(hT_v, FREE + B)
                with pe.Fori(0, B) as g:
                    pe.wait_ge(c_ready, FREE + g)
                    for j in range(TPB):
                        for k in range(KD):
                            for a, b in ((0, 0), (0, 1), (1, 0)):
                                last = pe.matmul(ckv_ps[:, j, :], hT[:, k, a, dyn(g * S + j * P, P)],
                                                 G["kv_w"][:, k, b, :], start=k + a + b == 0, stop=k * a == 1)
                    last.then_inc(ckv_mm, 1)
                    pe.wait_ge(c_lo, FREE + g + 1)
                    pe.wait_ge(kT_ready, FREE + g)
                    for part in range(2):
                        for j in range(TPB):
                            last = pe.transpose(k_ps[:, part, j * P:(j + 1) * P],
                                                G["c"][:, dyn(g * TPB + j, 1), part, :].rearrange("p a c -> p (a c)"), G["ident_h"][:, :])
                    last.then_inc(k_turned, 1)
            if route:
                pe.wait_ge(hT_a, FREE + B)
                pe.wait_ge(hT_v, FREE + B)
                with pe.Fori(0, B) as g:
                    pe.wait_ge(mask_ready, FREE + g)
                    for j in range(TPB):
                        for k in range(KD):
                            for a, b in ((0, 0), (0, 1), (1, 0)):
                                last = pe.matmul(logit_ps[:, j, :], hT[:, k, a, dyn(g * S + j * P, P)],
                                                 G["gate"][:, k, b, :], start=k + a + b == 0, stop=k * a == 1)
                    last.then_inc(logit_mm, 1)
                    pe.wait_ge(mask_ready, FREE + g + 1)
                    pe.wait_ge(idx_ready, FREE + g)
                    for j in range(TPB):
                        pe.matmul(count_ps[:, j, :], G["ones_b"][:, :], mask_sum[:, :], start=True, stop=False)
                        for i in range(j):
                            pe.matmul(count_ps[:, j, :], G["ones_b"][:, :], mask[:, i, :], start=False, stop=False)
                        last = pe.matmul(count_ps[:, j, :], G["tri_b"][:, :], mask[:, j, :], start=False, stop=True)
                    last.then_inc(count_mm, 1)
                    pe.wait_ge(held_ready, g + 1)
                    pe.matmul(live_ps[:, :], G["ones_b"][:, :], held[:, :], start=True, stop=True).then_inc(live_mm, 1)

        @block.vector
        def _(dve):
            def layernorm(g, turn, done):
                ch = Chain(dve, chain, turn * LN_CHAIN, LN_CHAIN)
                for j in range(TPB):
                    last = dve.bn_stats(stats[:, j, :], x[:, dyn((g * TPB + j) * D, D)])
                ch.link(last, G["spare"][:, 0:1])
                for j in range(TPB):
                    last = dve.bn_aggr(mv[:, j, :], stats[:, j, :])
                ch.link(last)
                dve.tensor_scalar(var[:, :], mv[:, :, 1], 1e-5, None, ALU.add).then_inc(stat_ready, 1)
                dve.wait_ge(rstd_ready, turn + 1)
                for j in range(TPB):
                    at = j * D
                    to = h[:, dyn(g * W + at, D)] if route else h[:, at:at + D]
                    last = dve.tensor_scalar(to, x[:, dyn(g * W + at, D)], mv[:, j, 0:1], rstd[:, j:j + 1],
                                             ALU.subtract, ALU.mult)
                last.then_inc(done, 1)
                ch.end()

            if ffn:
                ffn_chain = s("ffn_chain")
                with dve.Fori(0, B) as g:
                    layernorm(g, g, ffn_chain)
                    dve.wait_ge(ffn_chain, g * FFN_CHAIN + 1)
                    dve.tensor_scalar(above[:, :], h_of(g), 0.33, None, ALU.is_gt).then_inc(ffn_chain, 1)
                    dve.wait_ge(ffn_chain, g * FFN_CHAIN + 2)
                    dve.scalar_tensor_tensor(q[:, dyn(g * W, W)], h_of(g), -0.33, above[:, :],
                                             ALU.is_lt, ALU.subtract).then_inc(q_ready, 1)
                with dve.Fori(0, B) as g:
                    dve.wait_ge(y_ready, g + 1)
                    dve.scalar_tensor_tensor(x[:, dyn(g * W, W)], y_ps[:, :], -0.25, x[:, dyn(g * W, W)],
                                             ALU.mult, ALU.add).then_inc(x_added, 1)
                dve.wait_ge(x_added, FREE + B)
            with dve.Fori(0, B) as g:
                layernorm(g, g + B * int(ffn), h_ready)
                dve.wait_ge(h_hi, g + 1)
                dve.wait_ge(h_ready, g + 1)
                dve.tensor_tensor(h_parts[:, 1, :], h_of(g), h_parts[:, 0, :], ALU.subtract).then_inc(h_lo, 1)
                dve.wait_ge(h_turned, FREE + g + 1)
                dve.tensor_copy(hT[:, 1, :, dyn(g * S, S)], turn_ps[:, 1, :, :]).then_inc(hT_v, 1)
            if latent:
                latent_chain = s("latent_chain")
                dve.sem_inc(c_lo, FREE)
                with dve.Fori(0, B) as g:
                    ch = Chain(dve, latent_chain, g * 3, 3)
                    dve.wait_ge(ckv_mm, g + 1)
                    dve.wait_ge(c_lo, FREE + g)
                    ch.link(dve.tensor_scalar(ckv[:, :, :], ckv_ps[:, :, :], 1 / W_SCALE, None, ALU.mult))
                    ch.link(dve.tensor_tensor(sq[:, :, :], ckv[:, :, 0:LORA], ckv[:, :, 0:LORA], ALU.mult))
                    ch.link(dve.tensor_reduce(var[:, :], sq[:, :, :], X, ALU.add))
                    ch.end()
                    dve.tensor_scalar(var[:, :], var[:, :], 1 / LORA, 1e-6, ALU.mult, ALU.add).then_inc(stat_ready, 1)
                    dve.wait_ge(rstd_ready, g + 1 + B * (1 + int(ffn)))
                    for j in range(TPB):
                        last = dve.scalar_tensor_tensor(ckv[:, j, 0:LORA], ckv[:, j, 0:LORA], rstd[:, j:j + 1],
                                                        G["c_norm"][:, :], ALU.mult, ALU.mult)
                    last.then_inc(c_ready, 1)
                    dve.wait_ge(c_hi, g + 1)
                    dve.tensor_tensor(G["c"][:, dyn(g * TPB, TPB), 1, :], ckv[:, :, :],
                                      G["c"][:, dyn(g * TPB, TPB), 0, :], ALU.subtract).then_inc(c_lo, 1)
            if route:
                zeroed = s("sum_zeroed")
                dve.memset(mask_sum[:, :], 0.0).then_inc(zeroed, 1)
                dve.wait_ge(zeroed, 1)
                dve.wait_ge(consts, 2)
                with dve.Fori(0, B) as g:
                    ch = Chain(dve, route_chain, g * CHAIN, CHAIN)
                    dve.wait_ge(logit_mm, g + 1)
                    for j in range(TPB):
                        last = dve.scalar_tensor_tensor(logit[:, j, :], logit_ps[:, j, :], 1 / W_SCALE,
                                                        G["absent"][:, :], ALU.mult, ALU.add)
                    ch.link(last, G["spare"][:, 0:1])
                    for j in range(TPB):
                        last = dve.max(top[:, j, :], logit[:, j, :])
                    ch.link(last)
                    dve.tensor_scalar(ntop[:, :], top[:, :, 0], -1.0, None, ALU.mult).then_inc(top_ready, 1)
                    ch.link(dve.tensor_scalar(edge[:, :], top[:, :, TOPK - 1], -1e38, None, ALU.max))
                    for j in range(TPB):
                        last = dve.tensor_scalar(mask[:, j, :], logit[:, j, :], edge[:, j:j + 1], None, ALU.is_ge)
                    last.then_inc(mask_ready, 1)
                    dve.wait_ge(e_ready, g + 1)
                    dve.wait_ge(mask_ready, FREE + g + 1)
                    ch.link(dve.tensor_tensor(prob[:, :, :], prob[:, :, :], mask[:, :, :], ALU.mult))
                    ch.link(dve.tensor_reduce(den[:, :], prob[:, :, :], X, ALU.add))
                    ch.link(dve.reciprocal(den[:, :], den[:, :]))
                    for j in range(TPB):
                        last = dve.tensor_scalar(prob[:, j, :], prob[:, j, :], den[:, j:j + 1], 0.5, ALU.mult, ALU.mult)
                    ch.link(last)
                    dve.wait_ge(count_mm, g + 1)
                    ch.link(dve.tensor_tensor(key[:, :, :], count_ps[:, :, :], first_slot[:, :, :], ALU.add))
                    taken = same[:, :, 0, :]
                    ch.link(dve.scalar_tensor_tensor(taken, count_ps[:, :, :], float(CAP), mask[:, :, :],
                                                     ALU.is_le, ALU.mult))
                    ch.link(dve.tensor_tensor(key[:, :, :], key[:, :, :], taken, ALU.mult))
                    ch.link(dve.tensor_tensor(prob[:, :, :], prob[:, :, :], taken, ALU.mult), G["spare"][:, 0:1])
                    for j in range(TPB):
                        last = dve.max(keyt[:, j, :], key[:, j, :])
                    ch.link(last)
                    flat = keyt[:, :, :].rearrange("p j k -> p (j k)")
                    dve.tensor_scalar(held[:, :], flat, 0.5, None, ALU.is_gt).then_inc(held_ready, 1)
                    ch.link(dve.tensor_scalar(late[:, :], flat, 0.5, 1e6, ALU.is_lt, ALU.mult))
                    ch.link(dve.tensor_tensor(same[:, :, :, :], key[:, :, :].unsqueeze(2).to_broadcast([P, TPB, TOPK, E]),
                                              keyt[:, :, :].unsqueeze(3).to_broadcast([P, TPB, TOPK, E]), ALU.is_equal))
                    ch.link(dve.tensor_tensor(same[:, :, :, :], same[:, :, :, :],
                                              prob[:, :, :].unsqueeze(2).to_broadcast([P, TPB, TOPK, E]), ALU.mult))
                    ch.link(dve.tensor_reduce(G["slot_w"][:, dyn(g * TPB * TOPK, TPB * TOPK)], same[:, :, :, :].rearrange("p j k e -> p (j k) e"), X, ALU.add))
                    ch.link(dve.tensor_tensor(added[:, :], mask[:, 0, :], mask[:, 1, :], ALU.add))
                    ch.link(dve.tensor_tensor(added[:, :], added[:, :], mask[:, 2, :], ALU.add))
                    ch.link(dve.tensor_tensor(added[:, :], added[:, :], mask[:, 3, :], ALU.add))
                    ch.link(dve.tensor_tensor(mask_sum[:, :], mask_sum[:, :], added[:, :], ALU.add))
                    dve.wait_ge(live_mm, g + 1)
                    ch.link(dve.tensor_scalar(G["live"][:, dyn(g * TPB * TOPK, TPB * TOPK)], live_ps[:, :], 0.5, None, ALU.is_gt))
                    ch.link(dve.tensor_reduce(most[:, :], live_ps[:, :], X, ALU.max))
                    ch.link(dve.tensor_scalar(G["live_four"][:, dyn(g, 1)], most[:, :], 0.5, None, ALU.is_gt))
                    dve.scalar_tensor_tensor(G["slot"][:, dyn(g * TPB * TOPK, TPB * TOPK)], flat, -1.0, late[:, :],
                                             ALU.add, ALU.add).then_inc(idx_ready, 1)
                    ch.end()


def experts(nc, d, G, sem, sb, ps, tag):
    def s(name):
        return sem(f"{tag}_{name}")

    EC = 4
    NCH = E // EC
    SW = 256
    RING = 3
    HID_SCALE = 16.0
    loaded = [s(f"loaded{i}") for i in range(RING)]
    stored = [s(f"stored{i}") for i in range(RING)]
    turned, xT_hi, xT_lo, w_hi, w_lo, gu_mm, gate_ready, hid_ready, hid_hi, hid_lo, y_mm, y_ready = (
        s(n) for n in ("turned", "xT_hi", "xT_lo", "w_hi", "w_lo", "gu_mm", "gate_ready", "hid_ready",
                       "hid_hi", "hid_lo", "y_mm", "y_ready"))
    NB = 4
    cleared = s("cleared")
    with ExitStack() as c_out:
        y = [sb(f"y{i}", [P, TOPK, D], F32, c_out) for i in range(NB)]
        with ExitStack() as c, nc.Block(f"experts_{tag}") as block:
            gu = [sb(f"gu{i}", [P, EC, KD, 2 * INTER], F32, c) for i in range(RING)]
            gu_s = [sb(f"gu_s{i}", [P, 2, EC, KD, 2 * INTER], F16, c) for i in range(RING)]
            dn = [sb(f"dn{i}", [INTER, EC, D], F32, c) for i in range(RING)]
            dn_s = [sb(f"dn_s{i}", [INTER, 2, EC, D], F16, c) for i in range(RING)]
            xs = [sb(f"xs{i}", [CAP, EC, D], F32, c) for i in range(RING)]
            xT = [sb(f"xT{i}", [P, 2, EC, KD * CAP], F16, c) for i in range(RING)]
            gate = [sb(f"gate{i}", [INTER, EC, CAP], F32, c) for i in range(RING)]
            hid = [sb(f"hid{i}", [INTER, EC, CAP], F32, c) for i in range(RING)]
            hid_s = [sb(f"hid_s{i}", [INTER, 2, EC, CAP], F16, c) for i in range(RING)]
            ys = [sb(f"ys{i}", [CAP, EC, D], F32, c) for i in range(RING)]
            t_ps = ps("t_ps", [P, EC, SW], F32, c)
            gu_ps = ps("gu_ps", [P, EC, SW], F32, c)
            y_ps = ps("ye_ps", [P, EC, D], F32, c)
            gu_d = d["gupT"].rearrange("(n m) (k p) o -> n p m k o", m=EC, p=P)
            dn_d = d["downT"].rearrange("(n m) i o -> n i m o", m=EC)
            xs_d = d["scratch_a"].rearrange("(n m s) i -> n s m i", m=EC, s=CAP)
            ys_d = d["scratch_b"].rearrange("(n m s) i -> n s m i", m=EC, s=CAP)
            LOADS = 16 * (EC + 2)

            def steps(eng, step):
                last = NCH // RING - 1
                for i in range(RING):
                    step(0, i)
                with eng.Fori(1, last) as it:
                    for i in range(RING):
                        step(it, i)
                for i in range(RING):
                    step(last, i)

            def after(it, i):
                if isinstance(it, int) and it * RING + i == NCH - 1:
                    return None
                return it + (i + 1) // RING, (i + 1) % RING

            def before(it, i):
                if isinstance(it, int) and it * RING + i == 0:
                    return None
                return (it, i - 1) if i else (it - 1, RING - 1)

            @block.sync
            def _(sp):
                for n in range(NCH + 4):
                    if n < NCH:
                        i = n % RING
                        if n >= RING:
                            sp.wait_ge(w_lo, n - RING + 1)
                            sp.wait_ge(turned, n - RING + 1)
                        for m in range(EC):
                            sp.dma_start(gu[i][:, m], gu_d[n, :, m]).then_inc(loaded[i], 16)
                        sp.dma_start(dn[i][:, :, :], dn_d[n]).then_inc(loaded[i], 16)
                        sp.dma_start(xs[i][:, :, :], xs_d[n]).then_inc(loaded[i], 16)
                    if n >= 4:
                        o = n - 4
                        sp.wait_ge(y_ready, FREE + o + 1)
                        sp.dma_start(ys_d[o], ys[o % RING][:, :, :]).then_inc(stored[o % RING], 16)
                for i in range(RING):
                    sp.wait_ge(stored[i], 16 + 16 * NCH // RING)

            @block.tensor
            def _(pe):
                def turn(it, i):
                    pe.wait_ge(loaded[i], LOADS * (it + 1))
                    pe.wait_ge(xT_lo, FREE + it * RING + i)
                    for m in range(EC):
                        for k in range(KD):
                            last = pe.transpose(t_ps[:, m, k * CAP:(k + 1) * CAP], xs[i][:, m, k * P:(k + 1) * P],
                                                G["ident"][0:CAP, 0:CAP])
                    last.then_inc(turned, 1)

                def up(it, i):
                    n = it * RING + i
                    pe.wait_ge(xT_lo, FREE + n + 1)
                    pe.wait_ge(w_lo, n + 1)
                    pe.wait_ge(hid_ready, FREE + n)
                    for m in range(EC):
                        for half in range(2):
                            for k in range(KD):
                                for a, b in ((0, 0), (0, 1), (1, 0)):
                                    last = pe.matmul(gu_ps[0:INTER, m, half * CAP:(half + 1) * CAP],
                                                     gu_s[i][:, a, m, k, half * INTER:(half + 1) * INTER],
                                                     xT[i][:, b, m, k * CAP:(k + 1) * CAP],
                                                     start=k + a + b == 0, stop=k * a == 1)
                    last.then_inc(gu_mm, 1)

                def down(it, i):
                    n = it * RING + i
                    pe.wait_ge(hid_lo, n + 1)
                    pe.wait_ge(y_ready, FREE + n)
                    for m in range(EC):
                        for a, b in ((0, 0), (0, 1), (1, 0)):
                            last = pe.matmul(y_ps[0:CAP, m, :], hid_s[i][:, a, m, :], dn_s[i][:, b, m, :],
                                             start=a + b == 0, stop=a == 1)
                    last.then_inc(y_mm, 1)

                def step(it, i):
                    if after(it, i):
                        turn(*after(it, i))
                    up(it, i)
                    if before(it, i):
                        down(*before(it, i))

                for free in (xT_lo, hid_ready, y_ready):
                    pe.sem_inc(free, FREE)
                turn(0, 0)
                steps(pe, step)
                down(NCH // RING - 1, RING - 1)

            @block.scalar
            def _(act):
                def split(it, i):
                    act.wait_ge(turned, it * RING + i + 1)
                    act.activation(xT[i][:, 0, :, :], t_ps[:, :, 0:KD * CAP], ACT.Copy).then_inc(xT_hi, 1)
                    act.activation(gu_s[i][:, 0], gu[i][:, :, :, :], ACT.Copy, scale=W_SCALE)
                    act.activation(dn_s[i][:, 0], dn[i][:, :, :], ACT.Copy, scale=W_SCALE).then_inc(w_hi, 1)

                def out(it, i):
                    act.wait_ge(y_mm, it * RING + i + 1)
                    act.wait_ge(stored[i], 16 * (it + 1))
                    act.activation(ys[i][:, :, :], y_ps[0:CAP, :, :], ACT.Copy,
                                   scale=1 / (W_SCALE * HID_SCALE)).then_inc(y_ready, 1)

                def step(it, i):
                    if after(it, i):
                        split(*after(it, i))
                    n = it * RING + i
                    act.wait_ge(gu_mm, n + 1)
                    act.activation(gate[i][:, :, :], gu_ps[0:INTER, :, 0:CAP], ACT.Silu,
                                   scale=1 / W_SCALE).then_inc(gate_ready, 1)
                    act.wait_ge(hid_ready, FREE + n + 1)
                    act.activation(hid_s[i][:, 0], hid[i][:, :, :], ACT.Copy).then_inc(hid_hi, 1)
                    if before(it, i):
                        out(*before(it, i))

                for i in range(RING):
                    act.sem_inc(stored[i], 16)
                split(0, 0)
                steps(act, step)
                out(NCH // RING - 1, RING - 1)

            @block.vector
            def _(dve):
                def split(it, i):
                    n = it * RING + i
                    dve.wait_ge(xT_hi, n + 1)
                    dve.tensor_tensor(xT[i][:, 1, :, :], t_ps[:, :, 0:KD * CAP], xT[i][:, 0, :, :],
                                      ALU.subtract).then_inc(xT_lo, 1)
                    dve.wait_ge(w_hi, n + 1)
                    dve.scalar_tensor_tensor(gu_s[i][:, 1], gu[i][:, :, :, :], W_SCALE, gu_s[i][:, 0], ALU.mult, ALU.subtract)
                    dve.scalar_tensor_tensor(dn_s[i][:, 1], dn[i][:, :, :], W_SCALE, dn_s[i][:, 0], ALU.mult,
                                             ALU.subtract).then_inc(w_lo, 1)

                def step(it, i):
                    if after(it, i):
                        split(*after(it, i))
                    n = it * RING + i
                    dve.wait_ge(gate_ready, n + 1)
                    dve.scalar_tensor_tensor(hid[i][:, :, :], gu_ps[0:INTER, :, CAP:2 * CAP], HID_SCALE / W_SCALE,
                                             gate[i][:, :, :], ALU.mult, ALU.mult).then_inc(hid_ready, 1)
                    dve.wait_ge(hid_hi, n + 1)
                    dve.tensor_tensor(hid_s[i][:, 1], hid[i][:, :, :], hid_s[i][:, 0], ALU.subtract).then_inc(hid_lo, 1)

                split(0, 0)
                steps(dve, step)

            @block.gpsimd
            def _(pool):
                for i in range(NB):
                    pool.memset(y[i][:, :, :], 0.0).then_inc(cleared, 1)
                pool.wait_ge(cleared, NB)

        combine(nc, d, G, s, y, tag)


def combine(nc, d, G, s, y, tag):
    NB = len(y)
    LAG = 2
    gathered = [s(f"gathered{i}") for i in range(NB)]
    rows_ready, combined, added = s("rows_ready"), s("combined"), s("added")
    with nc.Block(f"combine_{tag}") as block:
        @block.gpsimd
        def _(pool):
            due = [pool.alloc_register(f"{tag}_gathers_due{i}") for i in range(NB)]
            for i in range(NB):
                pool.reg_mov(due[i], 0)

            def arrived(t):
                pool.wait_ge(gathered[t % NB], due[t % NB])
                pool.sem_inc(rows_ready, 1)

            def gather(g):
                for t in range(g * NB, (g + 1) * NB):
                    if g:
                        pool.wait_ge(combined, t - NB + 1)
                    moved(pool, G["live"], gathered[t % NB], due[t % NB], t, g == 0, lambda at: pool.indirect_dma_start(
                        out=y[t % NB][:, at % TOPK, :], out_offset=None, in_=d["scratch_b"],
                        in_offset=bass.IndirectOffsetOnAxis(ap=G["slot"][:, at:at + 1], axis=0),
                        bounds_check=SLOTS - 1, oob_is_err=False))
                    if t >= g * NB + LAG:
                        arrived(t - LAG)
                for t in range((g + 1) * NB - LAG, (g + 1) * NB):
                    arrived(t)

            gather(0)
            for g in range(1, NT // NB):
                some = pool.value_load(G["live_four"][0:1, g:g + 1], min_val=0, max_val=1)
                with pool.If(some > 0):
                    gather(g)
                with pool.Else():
                    pool.sem_inc(rows_ready, NB)
            for i in range(NB):
                pool.free_register(due[i])

        @block.vector
        def _(dve):
            dve.sem_inc(added, FREE)
            def add(t, i, ks):
                xt = G["x"][:, dyn(t * D, D)]
                for k in ks:
                    dve.wait_ge(added, FREE + t * TOPK + k)
                    dve.scalar_tensor_tensor(xt, y[i][:, k, :], G["slot_w"][:, dyn(t * TOPK + k, 1)], xt,
                                             ALU.mult, ALU.add).then_inc(added, 1)

            def live(t, k):
                return dve.value_load(G["live"][0:1, dyn(t * TOPK + k, 1)], min_val=0, max_val=1)

            with dve.Fori(0, NT // NB) as it:
                some = dve.value_load(G["live_four"][0:1, dyn(it, 1)], min_val=0, max_val=1)
                with dve.If(some > 0):
                    for i in range(NB):
                        t = it * NB + i
                        dve.wait_ge(rows_ready, t + 1)
                        with dve.If(live(t, 0) > 0):
                            add(t, i, range(KG))
                            with dve.If(live(t, KG) > 0):
                                add(t, i, range(KG, TOPK))
                            with dve.Else():
                                dve.sem_inc(added, TOPK - KG)
                        with dve.Else():
                            dve.sem_inc(added, TOPK)
                        dve.wait_ge(added, FREE + (t + 1) * TOPK)
                        dve.sem_inc(combined, 1)
                with dve.Else():
                    dve.sem_inc(added, NB * TOPK)
                    dve.sem_inc(combined, NB)


def load_l1(nc, d, G, sem, sb, ps, c):
    raw_in = [sem(f"raw_in{i}") for i in range(4)]
    high, low = sem("l1_high"), sem("l1_low")
    for n in ("w_q", "w_k", "w_v"):
        G[n] = sb(n, [P, KD, 2, H * P], F16, c)
    G["w_o"] = sb("w_o", [P, H, 2, D], F16, c)
    with ExitStack() as c1, nc.Block("load_l1") as block:
        raw = [sb(f"raw{i}", [P, 4096], F32, c1) for i in range(2)]
        src = [d[n].rearrange("(k p) q -> p k q", p=P) for n in ("wqT", "wkT", "wvT")]
        src.append(d["woT1"].rearrange("(h r) o -> r h o", r=P))
        shape = [(KD, H * P)] * 3 + [(H, D)]
        view = [raw[i % 2][:, :].rearrange("p (a b) -> p a b", a=shape[i][0]) for i in range(4)]
        parts = [G[n] for n in ("w_q", "w_k", "w_v", "w_o")]

        @block.sync
        def _(sp):
            for i in range(4):
                if i >= 2:
                    sp.wait_ge(low, i - 1)
                sp.dma_start(view[i], src[i]).then_inc(raw_in[i], 16)

        @block.scalar
        def _(act):
            for i in range(4):
                act.wait_ge(raw_in[i], 16)
                act.activation(parts[i][:, :, 0, :], view[i], ACT.Copy, scale=W_SCALE).then_inc(high, 1)

        @block.vector
        def _(dve):
            for i in range(4):
                dve.wait_ge(high, i + 1)
                dve.scalar_tensor_tensor(parts[i][:, :, 1, :], view[i], W_SCALE, parts[i][:, :, 0, :],
                                         ALU.mult, ALU.subtract).then_inc(low, 1)


def attention(nc, d, G, sem, sb, ps, tag, latent):
    def s(name):
        return sem(f"{tag}_{name}")

    NPROJ = 1 if latent else 3
    NO = H // 2 if latent else H
    scale = (NOPE + ROPE if latent else DV) ** -0.5
    proj_mm, proj_hi, proj_done = s("proj_mm"), s("proj_hi"), s("proj_done")
    s_mm, max_ready, exp_done, rinv_ready, p_ready = s("scores_mm"), s("max_ready"), s("exp_done"), s("rinv_ready"), s("p_ready")
    turned, t_hi, t_done = s("p_turned"), s("pT_hi"), s("pT_done")
    o_mm, o_hi, o_done, y_mm, y_done = s("o_mm"), s("o_hi"), s("o_done"), s("y_mm"), s("y_done")
    v_ready = s("v_ready") if latent else None
    hT = G["hT"]
    order = (3, 2, 0, 1)
    PIECES = 4
    HALVES = 2
    A_BANKS = 1 if latent else 2
    QUERY, KEYS, VALUES = range(3)

    def proj_count(b, h, which):
        if latent:
            return b * H + h
        ends = isinstance(h, int)
        if which == VALUES:
            return b * 3 * H + (3 * H - 1 if ends and h == H - 1 else h * 3 + 4)
        if which == KEYS:
            return b * 3 * H + (1 if ends and h == 0 else h * 3)
        return b * 3 * H + (0 if ends and h == 0 else h * 3 - 1)

    with ExitStack() as c, nc.Block(f"attention_{tag}") as block:
        qT = [sb(f"qT{i}", [P, 2, S], F16, c) for i in range(2)]
        if latent:
            v = [sb("v_batch", [P, TPB, 2, LORA], F16, c)] * 2
        else:
            kTh = [sb(f"kTh{i}", [P, 2, S], F16, c) for i in range(2)]
            v = [sb(f"v{i}", [P, TPB, 2, P], F16, c) for i in range(2)]
        p = [sb(f"p{i}", [P, CAUSAL], F32, c) for i in range(2)]
        pT = [sb(f"pT{i}", [P, 2, CAUSAL], F16, c) for i in range(2)]
        nmax = [sb(f"nmax{i}", [P, TPB], F32, c) for i in range(2)]
        scaled = sb("scaled", [P, 2], F32, c)
        total = [sb(f"total{i}", [P, TPB], F32, c) for i in range(2)]
        rinv = [sb(f"rinv{i}", [P, TPB], F32, c) for i in range(2)]
        oT = sb("oT", [P, NO, 2, S], F16, c)
        T_AT = 6 * 512 - CAUSAL if latent else 5 * 512 - CAUSAL
        s_ps = ps("s_ps", [P, T_AT + CAUSAL], F32, c)
        t_ps = s_ps[:, T_AT:T_AT + CAUSAL]
        o_ps = ps("o_ps", [P, S], F32, c)
        a_ps = [ps(f"a_ps{i}", [P, S], F32, c) for i in range(A_BANKS)]

        def heads(eng, step, finish, start):
            with eng.Fori(0, B) as b:
                start(b)
                for h in range(4):
                    step(b, h, h % 2)
                with eng.Fori(4, H - 4, 2) as h:
                    step(b, h, 0)
                    step(b, h + 1, 1)
                for h in range(H - 4, H):
                    step(b, h, h % 2)
                finish(b)

        def inner(h):
            return not isinstance(h, int)

        def a_bank(h, par, which):
            if latent:
                return a_ps[0]
            if not inner(h) and h == 0 and which != VALUES:
                return a_ps[which]
            return a_ps[1 - par if which == QUERY else par]

        def first(b, h, par, project):
            if not inner(h) and h == 0:
                project(b, 0, 0, QUERY)
                if latent:
                    project(b, 1, 1, QUERY)
                else:
                    project(b, 0, 0, KEYS)

        @block.tensor
        def _(pe):
            def project(b, h, par, which):
                pe.wait_ge(proj_done, proj_count(b, h, which) + 1)
                tok, to = dyn(b * S, S), a_bank(h, par, which)
                if which != VALUES:
                    w = G["q_w"] if latent else (G["w_q"], G["w_k"])[which]
                    for k in range(KD):
                        for a, x in ((0, 0), (0, 1), (1, 0)):
                            last = pe.matmul(to[:, :], w[:, k, a, dyn(h * P, P)], hT[:, k, x, tok],
                                             start=k + a + x == 0, stop=k * a == 1)
                else:
                    for j in range(TPB):
                        for k in range(KD):
                            for a, x in ((0, 0), (0, 1), (1, 0)):
                                last = pe.matmul(to[:, j * P:(j + 1) * P], hT[:, k, a, dyn(b * S + j * P, P)],
                                                 G["w_v"][:, k, x, dyn(h * P, P)], start=k + a + x == 0, stop=k * a == 1)
                last.then_inc(proj_mm, 1)

            def scores(b, h, par):
                n = b * H + h
                pe.wait_ge(proj_done, A_BANKS + proj_count(b, h, KEYS) + 1)
                if not inner(h) and h == 0:
                    pe.wait_ge(y_done, FREE + b)
                for i, upto in zip(order, (1, 3, 3, 4)):
                    pe.wait_ge(exp_done, n * PIECES + upto)
                    if not latent and i == 1:
                        pe.wait_ge(t_done, t_count(b, h))
                    cols = (i + 1) * P
                    here = s_ps[:, Q_AT[i]:Q_AT[i] + cols]
                    for e, (a, x) in enumerate(((0, 0), (0, 1), (1, 0))):
                        keys = G["kT"][:, x, dyn(b * S, cols)] if latent else kTh[par][:, x, 0:cols]
                        last = pe.matmul(here, qT[par][:, a, i * P:(i + 1) * P], keys, start=e == 0, stop=e == 2)
                        if e == 0:
                            pe.matmul(s_ps[:, Q_AT[i] + i * P:Q_AT[i] + cols], G["ident_b"][:, :], G["mask_b"][:, :],
                                      start=False, stop=False)
                    last.then_inc(s_mm, 1)

            def t_count(b, h):
                return FREE + b * H * HALVES + (0 if not inner(h) and h < 2 else (h - 1) * HALVES)

            def turn(b, h, par):
                n = b * H + h
                pe.wait_ge(p_ready, n * PIECES + PIECES)
                if not latent:
                    pe.wait_ge(exp_done, (n + (2 if inner(h) or h < H - 1 else 1)) * PIECES + PIECES)
                for half, tiles in enumerate(((2, 0), (1, 3))):
                    pe.wait_ge(t_done, n * HALVES + half + 1)
                    for j in tiles:
                        for i in range(j, TPB):
                            at = K_AT[j] + (i - j) * P
                            last = pe.transpose(t_ps[:, at:at + P], p[par][:, Q_AT[i] + j * P:Q_AT[i] + (j + 1) * P],
                                                G["ident"][:, :])
                    last.then_inc(turned, 1)

            def outputs(b, h, pars):
                pe.wait_ge(t_done, (b * H + h) * HALVES + 2 * HALVES)
                if not latent:
                    pe.wait_ge(proj_done, A_BANKS + proj_count(b, h, VALUES) + 1)
                pe.wait_ge(o_done, FREE + b * NO + ((h >> 1) if latent else h))
                rows = P // len(pars)
                for j in range(TPB):
                    for e, (a, x) in enumerate(((0, 0), (0, 1), (1, 0))):
                        for side, par in enumerate(pars):
                            last = pe.matmul(o_ps[side * rows:(side + 1) * rows, j * P:S], v[par][:, j, a, :],
                                             pT[par][:, x, K_AT[j]:K_AT[j] + (TPB - j) * P],
                                             start=j + e == 0, stop=j == TPB - 1 and e == 2)
                last.then_inc(o_mm, 1)

            def step(b, h, par):
                first(b, h, par, project)
                if latent and par == 0 and (inner(h) or h >= 4):
                    outputs(b, h - 3, (0, 1))
                if inner(h) or h >= 2:
                    turn(b, h - 2, par)
                if not latent and (inner(h) or h >= 1):
                    project(b, h - 1, 1 - par, VALUES)
                scores(b, h, par)
                if latent:
                    if inner(h) or h < H - 2:
                        project(b, h + 2, par, QUERY)
                    return
                if inner(h) or h < H - 1:
                    project(b, h + 1, 1 - par, QUERY)
                if inner(h) or h >= 2:
                    outputs(b, h - 2, (par,))
                if inner(h) or h < H - 1:
                    project(b, h + 1, 1 - par, KEYS)

            def finish(b):
                if latent:
                    outputs(b, H - 3, (0, 1))
                turn(b, H - 2, 0)
                if not latent:
                    project(b, H - 1, 1, VALUES)
                    outputs(b, H - 2, (0,))
                turn(b, H - 1, 1)
                outputs(b, H - 1, (0, 1) if latent else (1,))
                pe.wait_ge(o_done, FREE + (b + 1) * NO)
                w = G["vo_w"] if latent else G["w_o"]
                for i in range(TPB):
                    for m in range(NO):
                        for a, x in ((0, 0), (0, 1), (1, 0)):
                            last = pe.matmul(s_ps[:, i * D:(i + 1) * D], oT[:, m, a, i * P:(i + 1) * P], w[:, m, x, :],
                                             start=m + a + x == 0, stop=m == NO - 1 and a == 1)
                last.then_inc(y_mm, 1)

            def start(b):
                if latent:
                    pe.wait_ge(v_ready, b + 1)

            for free in (o_done, y_done):
                pe.sem_inc(free, FREE)
            pe.sem_inc(proj_done, A_BANKS)
            pe.sem_inc(exp_done, PIECES)
            pe.sem_inc(t_done, HALVES)
            heads(pe, step, finish, start)

        def proj_out(h, par, which):
            src = a_bank(h, par, which)[:, :]
            if which == QUERY:
                return (lambda part: qT[par][:, part, :]), src
            if which == KEYS:
                return (lambda part: kTh[par][:, part, :]), src
            return (lambda part: v[par][:, :, part, :]), src.rearrange("p (j d) -> p j d", j=TPB)

        def proj_scale(which):
            return (scale if which == QUERY else 1.0) / W_SCALE

        def o_part(at, part):
            return oT[:, at, part, :] if isinstance(at, int) else oT[:, dyn(at, 1), part, :].rearrange("p a c -> p (a c)")

        @block.scalar
        def _(act):
            def project(b, h, par, which):
                act.wait_ge(proj_mm, proj_count(b, h, which) + 1)
                to, src = proj_out(h, par, which)
                act.activation(to(0), src, ACT.Copy, scale=proj_scale(which)).then_inc(proj_hi, 1)

            def exps(b, h, par):
                for i, upto in zip(order, (1, 3, 3, 4)):
                    act.wait_ge(max_ready, (b * H + h) * PIECES + upto)
                    cols = (i + 1) * P
                    act.activation(p[par][:, Q_AT[i]:Q_AT[i] + cols], s_ps[:, Q_AT[i]:Q_AT[i] + cols], ACT.Exp,
                                   bias=nmax[par][:, i:i + 1], accum_out=total[par][:, i:i + 1]).then_inc(exp_done, 1)

            def turn(b, h, par):
                n = b * H + h
                for half, (lo, hi) in enumerate(HALF_AT):
                    act.wait_ge(turned, n * HALVES + half + 1)
                    act.activation(pT[par][:, 0, lo:hi], t_ps[:, lo:hi], ACT.Copy).then_inc(t_hi, 1)

            def outputs(b, h):
                at = (h >> 1) if latent else h
                act.wait_ge(o_mm, b * NO + at + 1)
                act.activation(o_part(at, 0), o_ps[:, :], ACT.Copy, scale=O_SCALE / P_SCALE).then_inc(o_hi, 1)

            def start(b):
                if latent:
                    act.wait_ge(y_mm, FREE + b)
                    act.activation(v[0][:, :, :, :], G["c"][:, dyn(b * TPB, TPB), :, 0:LORA], ACT.Copy).then_inc(v_ready, 1)

            def step(b, h, par):
                first(b, h, par, project)
                if latent and (inner(h) or 1 <= h < H - 1):
                    project(b, h + 1, 1 - par, QUERY)
                if inner(h) or h >= 2:
                    turn(b, h - 2, par)
                if latent and par == 0 and (inner(h) or h >= 4):
                    outputs(b, h - 4)
                if not latent and (inner(h) or h >= 1):
                    project(b, h - 1, 1 - par, VALUES)
                exps(b, h, par)
                if latent:
                    return
                if inner(h) or h < H - 1:
                    project(b, h + 1, 1 - par, QUERY)
                if inner(h) or h >= 2:
                    outputs(b, h - 2)
                if inner(h) or h < H - 1:
                    project(b, h + 1, 1 - par, KEYS)

            def finish(b):
                if latent:
                    outputs(b, H - 4)
                turn(b, H - 2, 0)
                if not latent:
                    project(b, H - 1, 1, VALUES)
                    outputs(b, H - 2)
                turn(b, H - 1, 1)
                outputs(b, H - 1)

            act.sem_inc(y_mm, FREE)
            heads(act, step, finish, start)

        @block.vector
        def _(dve):
            def project(b, h, par, which):
                dve.wait_ge(proj_hi, proj_count(b, h, which) + 1)
                to, src = proj_out(h, par, which)
                dve.scalar_tensor_tensor(to(1), src, proj_scale(which), to(0), ALU.mult, ALU.subtract).then_inc(proj_done, 1)

            def maxima(b, h, par):
                n = b * H + h
                for i, upto in zip(order, (1, 3, 3, 4)):
                    dve.wait_ge(s_mm, n * PIECES + upto)
                    dve.tensor_reduce(nmax[par][:, i:i + 1], s_ps[:, Q_AT[i]:Q_AT[i] + (i + 1) * P], X, ALU.max,
                                      negate=True).then_inc(max_ready, 1)

            def inverse(b, h, par):
                dve.wait_ge(exp_done, (b * H + h) * PIECES + 2 * PIECES)
                dve.reciprocal(rinv[par][:, :], total[par][:, :]).then_inc(rinv_ready, 1)

            def turn(b, h, par):
                n = b * H + h
                for half, (lo, hi) in enumerate(HALF_AT):
                    dve.wait_ge(t_hi, n * HALVES + half + 1)
                    dve.tensor_tensor(pT[par][:, 1, lo:hi], t_ps[:, lo:hi], pT[par][:, 0, lo:hi],
                                      ALU.subtract).then_inc(t_done, 1)

            def outputs(b, h):
                at = (h >> 1) if latent else h
                dve.wait_ge(o_hi, b * NO + at + 1)
                dve.scalar_tensor_tensor(o_part(at, 1), o_ps[:, :], O_SCALE / P_SCALE, o_part(at, 0), ALU.mult,
                                         ALU.subtract).then_inc(o_done, 1)

            def step(b, h, par):
                first(b, h, par, project)
                if inner(h) or h >= 1:
                    inverse(b, h - 1, 1 - par)
                if latent and (inner(h) or 1 <= h < H - 1):
                    project(b, h + 1, 1 - par, QUERY)
                if latent and par == 0:
                    maxima(b, h, par)
                if inner(h) or h >= 2:
                    turn(b, h - 2, par)
                if not latent and (inner(h) or h >= 1):
                    project(b, h - 1, 1 - par, VALUES)
                if not latent or par == 1:
                    maxima(b, h, par)
                if latent:
                    if par == 0 and (inner(h) or h >= 4):
                        outputs(b, h - 4)
                    return
                if inner(h) or h < H - 1:
                    project(b, h + 1, 1 - par, QUERY)
                if inner(h) or h >= 2:
                    outputs(b, h - 2)
                if inner(h) or h < H - 1:
                    project(b, h + 1, 1 - par, KEYS)

            def finish(b):
                if latent:
                    outputs(b, H - 4)
                inverse(b, H - 1, 1)
                turn(b, H - 2, 0)
                if not latent:
                    project(b, H - 1, 1, VALUES)
                    outputs(b, H - 2)
                turn(b, H - 1, 1)
                outputs(b, H - 1)
                dve.wait_ge(y_mm, FREE + b + 1)
                dve.scalar_tensor_tensor(G["x"][:, dyn(b * TPB * D, TPB * D)], s_ps[:, 0:TPB * D], 1 / (W_SCALE * O_SCALE),
                                         G["x"][:, dyn(b * TPB * D, TPB * D)], ALU.mult, ALU.add).then_inc(y_done, 1)

            heads(dve, step, finish, lambda b: None)

        @block.gpsimd
        def _(pool):
            def step(b, h, par):
                pool.wait_ge(rinv_ready, b * H + h + 1)
                pool.tensor_tensor(scaled[:, par:par + 1], rinv[par][:, 0:1], rinv[par][:, 0:1], ALU.add)
                for i in order:
                    part = p[par][:, Q_AT[i]:Q_AT[i] + (i + 1) * P]
                    pool.tensor_scalar(part, part, rinv[par][:, i:i + 1], P_SCALE, ALU.mult, ALU.mult).then_inc(p_ready, 1)

            heads(pool, step, lambda b: None, lambda b: None)


def build(nc, d, out, until=99):
    ctx = ExitStack()
    with ctx:
        held = []

        def sem(name):
            held.append(nc.alloc_semaphore(name=name))
            return held[-1]

        def renew_semaphores():
            nc.clear_and_free_semaphores(held)
            held.clear()
            nc.all_engine_barrier()

        taken = set(d)

        def fresh(name):
            while name in taken:
                name += "_"
            taken.add(name)
            return name

        def sb(name, shape, dt=F32, c=ctx):
            return c.enter_context(nc.sbuf_tensor(fresh(name), shape, dt))

        def ps(name, shape, dt=F32, c=ctx):
            return c.enter_context(nc.psum_tensor(fresh(name), shape, dt))

        G = {"spare": sb("spare", [P, 1])}
        G["x"] = sb("x", [P, NT * D])
        G["ident"] = sb("ident", [P, P])
        G["ident_h"] = sb("ident_h", [P, P], F16)
        G["ident_b"] = sb("ident_b", [P, P], BF16)
        G["mask_b"] = sb("mask_b", [P, P], BF16)
        G["ffn_w"] = sb("ffn_w", [P, KD, 3, D], BF16)
        G["gate"] = sb("gate", [P, KD, 2, E], F16)
        G["absent"] = sb("absent", [P, E])
        G["tri_b"] = sb("tri_b", [P, P], BF16)
        G["ones_b"] = sb("ones_b", [P, P], BF16)
        G["hT"] = sb("hT", [P, KD, 2, T], F16)
        G["slot"] = sb("slot", [P, NT * TOPK], U32)
        G["slot_w"] = sb("slot_w", [P, NT * TOPK])
        G["live_four"] = sb("live_four", [P, NT // TPB], I32)
        G["live"] = sb("live", [P, NT * TOPK], I32)
        prepare(nc, d, G, sem, sb, ps)
        if until > 1:
            with ExitStack() as c0:
                G["kT"] = sb("kT", [P, 2, T], F16, c0)
                G["c"] = sb("c_nat", [P, NT, 2, P], F16, c0)
                G["q_w"] = sb("q_w", [P, KD, 2, H * P], F16, c0)
                G["vo_w"] = sb("vo_w", [P, H // 2, 2, D], F16, c0)
                G["kv_w"] = sb("kv_w", [P, KD, 2, P], F16, c0)
                G["c_norm"] = sb("c_norm", [P, LORA], F32, c0)
                absorb(nc, d, G, sem, sb, ps)
                tiles(nc, d, G, sem, sb, ps, "a", ffn=True, latent=True)
                if until > 2:
                    attention(nc, d, G, sem, sb, ps, "l0", latent=True)
        if until > 3:
            tiles(nc, d, G, sem, sb, ps, "b", ffn=True, route=True)
        for rnd in range(2):
            if until > 4 + 2 * rnd:
                experts(nc, d, G, sem, sb, ps, f"m{rnd}")
            if rnd == 0 and until > 5:
                renew_semaphores()
                with ExitStack() as c1:
                    load_l1(nc, d, G, sem, sb, ps, c1)
                    tiles(nc, d, G, sem, sb, ps, "c")
                    attention(nc, d, G, sem, sb, ps, "l1", latent=False)
                tiles(nc, d, G, sem, sb, ps, "d", route=True)
        stored = sem("stored")
        with nc.Block("store") as block:
            @block.sync
            def _(sp):
                sp.dma_start(out.rearrange("(t p) d -> p t d", p=P), G["x"][:, :].rearrange("p (t d) -> p t d", d=D)).then_inc(stored, 16)
                sp.wait_ge(stored, 16)


kernel_until = 99


def kernel(**inputs):
    import numpy as _np
    import concourse.bacc as _bacc
    from concourse.bass_utils import run_bass_kernel_spmd as _run

    a = {k: _np.asarray(v) for k, v in inputs.items()}
    wq = a["L0_attn_Wq"]
    heads = wq.reshape(H, NOPE + ROPE, D)

    def turned(name):
        w = a[name]
        return w.reshape(-1, w.shape[-1]).T

    arrays = {
        "x": a["L0_attn_hidden_states"].reshape(T, D),
        "wq": wq,
        "wpeT": heads[:, NOPE:].transpose(2, 0, 1).reshape(D, H * ROPE),
        "kvaT": a["L0_attn_Wkva"][:LORA].T,
        "kpe_w": a["L0_attn_Wkva"][LORA:],
        "c_norm": _np.broadcast_to(a["L0_attn_kv_a_norm_weight"], (P, LORA)),
        "kvb": a["L0_attn_Wkvb"],
        "woT": turned("L0_attn_Wo"),
        "cos": a["L0_attn_cos"],
        "sin": a["L0_attn_sin"],
        "ffn_wT": turned("L0_ffn_weight"),
        "rramT": turned("L0_ffn_rram_variation"),
        "wkT": turned("L1_attn_W_K"),
        "wqT": turned("L1_attn_W_Q"),
        "wvT": turned("L1_attn_W_V"),
        "woT1": turned("L1_attn_W_O"),
        "gate_w": a["L1_ffn_gate_weight"],
        "gupT": a["L1_ffn_gate_up_proj"].transpose(0, 2, 1),
        "downT": a["L1_ffn_down_proj"].transpose(0, 2, 1),
        "o2n": a["L1_ffn_old_to_new"].reshape(E_OLD, 1),
    }
    arrays = {k: _np.ascontiguousarray(v) for k, v in arrays.items()}
    nc = _bacc.Bacc("TRN2", target_bir_lowering=False, num_devices=1)
    d = {k: nc.dram_tensor(k, v.shape, mybir.dt.from_np(v.dtype), kind="ExternalInput").ap() for k, v in arrays.items()}
    for name in ("scratch_a", "scratch_b"):
        d[name] = nc.dram_tensor(name, (SLOTS, D), F32).ap()
    out = nc.dram_tensor("out", (T, D), F32, kind="ExternalOutput").ap()
    build(nc, d, out, kernel_until)
    r = _run(nc, [arrays], core_ids=[0])
    return r.results[0]["out"].reshape(B, S, D)
```

```python
from contextlib import ExitStack

import numpy as np
import concourse.bass as bass
from concourse import mybir

F32 = mybir.dt.float32
F16 = mybir.dt.float16
BF16 = mybir.dt.bfloat16
I32 = mybir.dt.int32
U32 = mybir.dt.uint32
ALU = mybir.AluOpType
ACT = mybir.ActivationFunctionType
X = mybir.AxisListType.X

P = 128
T, D = 2048, 256
NT = T // P
S, B = 512, 4
TPB = S // P
KD = D // P
H = 16
NOPE, ROPE, LORA, DV = 128, 64, 64, 128
E_OLD, E, INTER, CAP, TOPK = 128, 48, 96, 96, 8
KG = 4
SLOTS = E * CAP

W_SCALE = 1024.0
P_SCALE = 4096.0
O_SCALE = 16.0

FREE = 1

Q_AT = {3: 0, 2: 512, 0: 896, 1: 1024}
K_AT = {2: 0, 0: 256, 1: 768, 3: 1152}
CAUSAL = 1280
HALF_AT = ((0, 768), (768, CAUSAL))


def dyn(start, size):
    return bass.ds(start, size)


def moved(pool, live, signal, due, t, always, move):
    for k in range(0, TOPK, KG):
        at = t * TOPK + k
        if always and k == 0:
            for i in range(KG):
                move(at + i).then_inc(signal, 16)
            pool.reg_add(due, due, 16 * KG)
            continue
        some = pool.value_load(live[0:1, at:at + 1], min_val=0, max_val=1)
        with pool.If(some > 0):
            for i in range(KG):
                move(at + i).then_inc(signal, 16)
        pool.reg_add(due, due, some * (16 * KG))


class Chain:

    def __init__(self, eng, done, start, per):
        self.eng, self.done, self.start, self.per, self.n = eng, done, start, per, 0

    def link(self, ins, spare=None):
        self.n += 1
        ins.then_inc(self.done, 1)
        self.eng.wait_ge(self.done, self.start + self.n)
        if spare is not None:
            self.eng.memset(spare, 0.0)

    def end(self):
        assert self.n == self.per, self.n


def prepare(nc, d, G, A, sem, sb, ps):
    loaded_x, loaded_w, loaded_g = sem("loaded_x"), sem("loaded_w"), sem("loaded_gate")
    zeroed, consts = sem("consts_zeroed"), sem("consts")
    chain = sem("prep_chain")
    picked, gate_mm, gate_hi = sem("gate_picked"), sem("gate_mm"), sem("gate_hi")
    with ExitStack() as c, nc.Block("prepare") as block:
        w = sb("w_raw", [P, KD, D], F32, c)
        rram = sb("rram_raw", [P, KD, D], F32, c)
        sign = sb("sign", [P, KD, D], F32, c)
        gate = sb("gate_raw", [P, D], F32, c)
        o2n_i = sb("o2n_i", [P, 1], I32, c)
        o2n = sb("o2n", [P, 1], F32, c)
        cols = sb("cols", [P, E], F32, c)
        sel = sb("sel", [P, E], F32, c)
        ones = sb("ones", [P, P], F32, c)
        gp = ps("gp", [P, KD + 1, E], F32, c)

        @block.sync
        def _(sp):
            sp.dma_start(w[:, :, :], d["ffn_wT"].rearrange("(k p) o -> p k o", p=P)).then_inc(loaded_w, 16)
            sp.dma_start(rram[:, :, :], d["rramT"].rearrange("(k p) o -> p k o", p=P)).then_inc(loaded_w, 16)
            sp.dma_start(gate[:, :], d["gate_w"]).then_inc(loaded_g, 16)
            sp.dma_start(o2n_i[:, :], d["o2n"]).then_inc(loaded_g, 16)
            sp.dma_start(G["x"][:, :].rearrange("p (t d) -> p t d", d=D), d["x"].rearrange("(t p) d -> p t d", p=P)).then_inc(loaded_x, 16)
            load_absorbed(sp, d, G, A)
            sp.wait_ge(loaded_x, 16)

        @block.gpsimd
        def _(pool):
            for t, v in ((G["ident"], 0.0), (G["ident_h"], 0.0), (G["ident_b"], 0.0), (G["mask_b"], 0.0),
                         (G["tri_b"], 1.0), (G["ones_b"], 1.0), (ones, 1.0)):
                pool.memset(t[:, :], v).then_inc(zeroed, 1)
            pool.wait_ge(zeroed, 7)
            for t in (G["ident"], G["ident_h"], G["ident_b"]):
                pool.affine_select(out=t[:, :], in_=t[:, :], compare_op=ALU.not_equal, fill=1.0, base=0,
                                   pattern=[[-1, P]], channel_multiplier=1).then_inc(consts, 1)
            pool.affine_select(out=G["mask_b"][:, :], in_=G["mask_b"][:, :], compare_op=ALU.is_ge, fill=-1e30,
                               base=0, pattern=[[-1, P]], channel_multiplier=1).then_inc(consts, 1)
            pool.affine_select(out=G["tri_b"][:, :], in_=G["tri_b"][:, :], compare_op=ALU.is_ge, fill=0.0,
                               base=0, pattern=[[1, P]], channel_multiplier=-1).then_inc(consts, 1)
            pool.iota(cols[:, :], pattern=[[1, E]], base=0, channel_multiplier=0,
                      allow_small_or_imprecise_dtypes=True).then_inc(consts, 1)

        @block.scalar
        def _(act):
            act.wait_ge(gate_mm, 1)
            act.activation(G["gate"][:, :, 0, :], gp[:, 0:KD, :], ACT.Copy, scale=W_SCALE).then_inc(gate_hi, 1)

        @block.tensor
        def _(pe):
            pe.wait_ge(picked, 1)
            for k in range(KD):
                pe.matmul(gp[:, k, :], gate[:, k * P:(k + 1) * P], sel[:, :], start=True, stop=True)
            pe.matmul(gp[:, KD, :], ones[:, :], sel[:, :], start=True, stop=True).then_inc(gate_mm, 1)

        @block.vector
        def _(dve):
            ch = Chain(dve, chain, 0, 10)
            dve.wait_ge(loaded_g, 32)
            dve.wait_ge(consts, 6)
            ch.link(dve.tensor_copy(o2n[:, :], o2n_i[:, :]))
            dve.tensor_scalar(sel[:, :], cols[:, :], o2n[:, 0:1], None, ALU.is_equal).then_inc(picked, 1)
            dve.wait_ge(loaded_w, 32)
            ch.link(dve.tensor_scalar(sign[:, :, :], w[:, :, :], 0.2, None, ALU.is_gt))
            ch.link(dve.scalar_tensor_tensor(sign[:, :, :], w[:, :, :], -0.2, sign[:, :, :], ALU.is_lt, ALU.subtract))
            ch.link(dve.scalar_tensor_tensor(w[:, :, :], sign[:, :, :], -0.6, rram[:, :, :], ALU.mult, ALU.add))
            for part in range(3):
                ch.link(dve.tensor_copy(G["ffn_w"][:, :, part, :], w[:, :, :]))
                if part < 2:
                    ch.link(dve.tensor_tensor(w[:, :, :], w[:, :, :], G["ffn_w"][:, :, part, :], ALU.subtract))
            dve.wait_ge(gate_hi, 1)
            dve.scalar_tensor_tensor(G["gate"][:, :, 1, :], gp[:, 0:KD, :], W_SCALE, G["gate"][:, :, 0, :],
                                     ALU.mult, ALU.subtract)
            ch.link(dve.tensor_scalar(G["absent"][:, :], gp[:, KD, :], 0.5, -3e38, ALU.is_lt, ALU.mult))
            ch.end()


def absorbed_weights(sem, sb, c):
    A = {n: sb(n, shape, F32, c) for n, shape in (
        ("wq_raw", [P, H, D]), ("wk_raw", [P, H, LORA]), ("wv_raw", [P, H, LORA]), ("wo_raw", [P, H, D]),
        ("wpe_raw", [P, KD, H * ROPE]), ("kva_raw", [P, KD, LORA]), ("kpe_raw", [ROPE, D]), ("cs", [ROPE, 2]))}
    A["loaded"] = {n: sem(f"loaded_{n}") for n in ("wq", "wk", "wpe", "wv", "wo", "kva", "rope")}
    return A


def load_absorbed(sp, d, G, A):
    loaded = A["loaded"]
    sp.dma_start(A["cs"][:, 0:1], d["cos"].rearrange("a r -> r a")).then_inc(loaded["rope"], 16)
    sp.dma_start(A["cs"][:, 1:2], d["sin"].rearrange("a r -> r a")).then_inc(loaded["rope"], 16)
    sp.dma_start(A["kpe_raw"][:, :], d["kpe_w"]).then_inc(loaded["rope"], 16)
    sp.dma_start(A["kva_raw"][:, :, :], d["kvaT"].rearrange("(k p) l -> p k l", p=P)).then_inc(loaded["kva"], 16)
    sp.dma_start(G["c_norm"][:, :], d["c_norm"]).then_inc(loaded["kva"], 16)
    kvb = d["kvb"].rearrange("(h r) l -> r h l", r=NOPE + DV)
    sp.dma_start(A["wq_raw"][:, :, :], d["wq"].rearrange("(h r) i -> r h i", r=NOPE + ROPE)[0:NOPE]).then_inc(loaded["wq"], 16)
    sp.dma_start(A["wk_raw"][:, :, :], kvb[0:NOPE]).then_inc(loaded["wk"], 16)
    sp.dma_start(A["wpe_raw"][:, :, :], d["wpeT"].rearrange("(k p) q -> p k q", p=P)).then_inc(loaded["wpe"], 16)
    sp.dma_start(A["wv_raw"][:, :, :], kvb[NOPE:NOPE + DV]).then_inc(loaded["wv"], 16)
    sp.dma_start(A["wo_raw"][:, :, :], d["woT"].rearrange("(h r) o -> r h o", r=DV)).then_inc(loaded["wo"], 16)


def absorb(nc, d, G, A, sem, sb, ps):
    loaded = A["loaded"]
    rot_made, rot_mm, rot_sq, pe_mm = sem("rot_made"), sem("rot_mm"), sem("rot_sq"), sem("rope_mm")
    swap0, swap1, chain = sem("swap_zeroed"), sem("swap_made"), sem("absorb_chain")
    filled, high, done = sem("absorb_filled"), sem("absorb_high"), sem("absorb_done")
    q_w, vo_w, kv_w = G["q_w"], G["vo_w"], G["kv_w"]
    HPB = 4
    with ExitStack() as c, nc.Block("absorb") as block:
        wq, wk, wv, wo, wpe, kva, kpe = (A[f"{n}_raw"] for n in ("wq", "wk", "wv", "wo", "wpe", "kva", "kpe"))
        cs = A["cs"]
        swap = sb("swap", [ROPE, ROPE], F32, c)
        rot = sb("rot", [ROPE, ROPE], F32, c)
        rr = sb("rr", [ROPE, ROPE], F32, c)
        bank = [ps(f"ab{i}", [P, 512], F32, c) for i in range(4)]
        rp = ps("rp", [P, 4, ROPE], F32, c)

        @block.gpsimd
        def _(pool):
            pool.memset(swap[:, :], 0.0).then_inc(swap0, 1)
            pool.wait_ge(swap0, 1)
            half = ROPE // 2
            pool.affine_select(out=swap[:, :], in_=swap[:, :], compare_op=ALU.not_equal, fill=-1.0, base=half,
                               pattern=[[-1, ROPE]], channel_multiplier=1).then_inc(swap0, 1)
            pool.wait_ge(swap0, 2)
            pool.affine_select(out=swap[:, :], in_=swap[:, :], compare_op=ALU.not_equal, fill=1.0, base=-half,
                               pattern=[[-1, ROPE]], channel_multiplier=1).then_inc(swap1, 1)

        @block.tensor
        def _(pe):
            pe.wait_ge(rot_made, 1)
            pe.matmul(rp[0:ROPE, 0, :], rot[:, :], rot[:, :], start=True, stop=True).then_inc(rot_mm, 1)
            pe.wait_ge(rot_sq, 1)
            for k in range(KD):
                last = pe.matmul(rp[:, 1 + k, :], kpe[:, k * P:(k + 1) * P], rr[:, :], start=True, stop=True)
            last.then_inc(pe_mm, 1)
            pe.wait_ge(loaded["wq"], 16)
            pe.wait_ge(loaded["wk"], 16)
            for g in range(H // HPB):
                for hh in range(HPB):
                    h = g * HPB + hh
                    for k in range(KD):
                        at = (k * HPB + hh) * LORA
                        last = pe.matmul(bank[g][:, at:at + LORA], wq[:, h, k * P:(k + 1) * P], wk[:, h, :],
                                         start=True, stop=True)
                last.then_inc(filled, 1)
            pe.wait_ge(loaded["wv"], 16)
            pe.wait_ge(loaded["wo"], 16)
            for g in range(H // 4):
                pe.wait_ge(done, g + 1)
                for hh in range(4):
                    h = g * 4 + hh
                    last = pe.matmul(bank[g][(hh % 2) * 64:(hh % 2) * 64 + 64, (hh // 2) * D:(hh // 2 + 1) * D],
                                     wv[:, h, :], wo[:, h, :], start=True, stop=True)
                last.then_inc(filled, 1)

        def nope(g, part):
            return q_w[:, :, part, g * HPB * P:(g + 1) * HPB * P].rearrange("p k (h c) -> p k h c", h=HPB)[:, :, :, 0:LORA]

        def rope(k, part):
            return q_w[:, k, part, :].rearrange("p (h c) -> p h c", h=H)[:, :, LORA:P]

        def raw_rope(k):
            return wpe[:, k, :].rearrange("p (h c) -> p h c", h=H)

        @block.scalar
        def _(act):
            act.wait_ge(loaded["wpe"], 16)
            for k in range(KD):
                act.activation(rope(k, 0), raw_rope(k), ACT.Copy, scale=W_SCALE)
            act.wait_ge(loaded["kva"], 32)
            act.activation(kv_w[:, :, 0, 0:LORA], kva[:, :, :], ACT.Copy, scale=W_SCALE)
            act.wait_ge(pe_mm, 1)
            act.activation(kv_w[:, :, 0, LORA:P], rp[:, 1:3, :], ACT.Copy, scale=W_SCALE).then_inc(high, 1)
            for g in range(H // HPB):
                act.wait_ge(filled, g + 1)
                for k in range(KD):
                    last = act.activation(nope(g, 0)[:, k], bank[g][:, k * 256:(k + 1) * 256].rearrange("p (h c) -> p h c", h=HPB),
                                          ACT.Copy, scale=W_SCALE)
                last.then_inc(high, 1)
            for g in range(H // 4):
                act.wait_ge(filled, 4 + g + 1)
                act.activation(vo_w[:, 2 * g:2 * g + 2, 0, :], bank[g][:, :].rearrange("p (a o) -> p a o", a=2),
                               ACT.Copy, scale=W_SCALE).then_inc(high, 1)

        @block.vector
        def _(dve):
            ch = Chain(dve, chain, 0, 2)
            dve.wait_ge(loaded["rope"], 48)
            dve.wait_ge(swap1, 1)
            ch.link(dve.tensor_scalar(rot[:, :], swap[:, :], cs[:, 1:2], None, ALU.mult))
            dve.scalar_tensor_tensor(rot[:, :], G["ident"][0:ROPE, 0:ROPE], cs[:, 0:1], rot[:, :],
                                     ALU.mult, ALU.add).then_inc(rot_made, 1)
            dve.wait_ge(rot_mm, 1)
            dve.tensor_copy(rr[:, :], rp[0:ROPE, 0, :]).then_inc(rot_sq, 1)
            dve.wait_ge(high, 1)
            for k in range(KD):
                dve.scalar_tensor_tensor(rope(k, 1), raw_rope(k), W_SCALE, rope(k, 0), ALU.mult, ALU.subtract)
            dve.scalar_tensor_tensor(kv_w[:, :, 1, 0:LORA], kva[:, :, :], W_SCALE, kv_w[:, :, 0, 0:LORA],
                                     ALU.mult, ALU.subtract)
            dve.scalar_tensor_tensor(kv_w[:, :, 1, LORA:P], rp[:, 1:3, :], W_SCALE, kv_w[:, :, 0, LORA:P],
                                     ALU.mult, ALU.subtract)
            for g in range(H // HPB):
                dve.wait_ge(high, g + 2)
                for k in range(KD):
                    last = dve.scalar_tensor_tensor(nope(g, 1)[:, k], bank[g][:, k * 256:(k + 1) * 256].rearrange("p (h c) -> p h c", h=HPB),
                                                    W_SCALE, nope(g, 0)[:, k], ALU.mult, ALU.subtract)
                last.then_inc(done, 1)
            for g in range(H // 4):
                dve.wait_ge(high, 4 + g + 2)
                last = dve.scalar_tensor_tensor(vo_w[:, 2 * g:2 * g + 2, 1, :], bank[g][:, :].rearrange("p (a o) -> p a o", a=2),
                                                W_SCALE, vo_w[:, 2 * g:2 * g + 2, 0, :], ALU.mult, ALU.subtract)
            ch.link(last)
            ch.end()



def tiles(nc, d, G, sem, sb, ps, tag, ffn=False, norm=True, latent=False, route=False):
    def s(name, used=True):
        return sem(f"{tag}_{name}") if used else None

    W = TPB * D
    x, hT = G["x"], G["hT"]
    stat_ready, rstd_ready, chain = s("stat_ready"), s("rstd_ready"), s("chain")
    consts = s("consts")
    q_ready, q_turned, qT_ready, y_ready, x_added = (
        s(n, ffn) for n in ("q_ready", "q_turned", "qT_ready", "y_ready", "x_added"))
    h_ready, h_hi, h_lo, h_turned = s("h_ready"), s("h_hi"), s("h_lo"), s("h_turned")
    hT_ready = s("hT_ready")
    ckv_mm, ckv_ready, c_ready, c_hi, c_lo, k_turned, kT_ready = (
        s(n, latent) for n in ("ckv_mm", "ckv_ready", "c_ready", "c_hi", "c_lo", "k_turned", "kT_ready"))
    logit_mm, top_ready, e_ready, mask_ready, count_mm = (
        s(n, route) for n in ("logit_mm", "top_ready", "e_ready", "mask_ready", "count_mm"))
    idx_ready, scattered, route_chain, held_ready, live_mm = (
        s(n, route) for n in ("idx_ready", "scattered", "route_chain", "held_ready", "live_mm"))
    LN0 = B * int(ffn)
    LN_CHAIN, FFN_CHAIN = 2, 2
    with ExitStack() as c, nc.Block(f"tiles_{tag}") as block:
        stats = sb("stats", [P, TPB, 6], F32, c)
        mv = sb("mv", [P, TPB, 2], F32, c)
        var = sb("var", [P, TPB], F32, c)
        rstd = sb("rstd", [P, TPB], F32, c)
        minus_half = sb("minus_half", [P, NT], F32, c)
        h = sb("h", [P, NT * D], F32, c)
        h_parts = sb("h_parts", [P, 2, NT * D], F16, c)
        turn_ps = ps("turn_ps", [P, KD, 2, S], F16, c)
        if ffn:
            above = sb("above", [P, W], BF16, c)
            q = sb("q", [P, NT * D], BF16, c)
            qT = sb("qT", [P, KD, S], BF16, c)
            q_ps = ps("q_ps", [P, KD, S], BF16, c)
            y_ps = ps("y_ps", [P, W], F32, c)
        if latent:
            ckv = sb("ckv", [P, NT, P], F32, c)
            sq = sb("sq", [P, NT, LORA], F32, c)
            c_var = sb("c_var", [P, NT], F32, c)
            c_rstd = sb("c_rstd", [P, NT], F32, c)
            ckv_ps = ps("ckv_ps", [P, TPB, P], F32, c)
            k_ps = ps("k_ps", [P, 2, S], F16, c)
        if route:
            logit = sb("logit", [P, TPB, E], F32, c)
            top = sb("top", [P, TPB, TOPK], F32, c)
            edge = sb("edge", [P, TPB], F32, c)
            ntop = sb("ntop", [P, TPB], F32, c)
            mask = sb("mask", [P, TPB, E], BF16, c)
            mask_sum = sb("mask_sum", [P, E], BF16, c)
            added = sb("added", [P, E], BF16, c)
            prob = sb("prob", [P, TPB, E], F32, c)
            key = sb("key", [P, TPB, E], F32, c)
            keyt = sb("keyt", [P, TPB, TOPK], F32, c)
            late = sb("late", [P, TPB * TOPK], F32, c)
            most = sb("most", [P, 1], F32, c)
            held = sb("held", [P, TPB * TOPK], BF16, c)
            den = sb("den", [P, TPB], F32, c)
            first_slot = sb("first_slot", [P, TPB, E], F32, c)
            same = sb("same", [P, TPB, TOPK, E], F32, c)
            LW = 64
            logit_ps = ps("logit_ps", [P, NT * LW], F32, c)
            counts = ps("count_ps", [P, TPB * (E + TOPK)], F32, c)
            count_ps = counts[:, 0:TPB * E].rearrange("p (j e) -> p j e", j=TPB)
            live_ps = counts[:, TPB * E:]
            CHAIN = 23

        def h_of(g):
            return h[:, dyn(g * W, W)]

        @block.gpsimd
        def _(pool):
            pool.memset(minus_half[:, :], -0.5).then_inc(consts, 1)
            if route:
                pool.iota(first_slot[:, :, :], pattern=[[0, TPB], [CAP, E]], base=0, channel_multiplier=0,
                          allow_small_or_imprecise_dtypes=True).then_inc(consts, 1)
            pool.wait_ge(consts, 1 + int(route))

            def root(n, out, of):
                pool.wait_ge(stat_ready, n + 1)
                pool.tensor_tensor(out, of, minus_half[:, 0:out.shape[-1]], ALU.pow).then_inc(rstd_ready, 1)

            def low(g):
                pool.wait_ge(h_hi, g + 1)
                pool.tensor_tensor(h_parts[:, 1, dyn(g * W, W)], h_of(g), h_parts[:, 0, dyn(g * W, W)],
                                   ALU.subtract).then_inc(h_lo, 1)

            if ffn:
                with pool.Fori(0, B) as g:
                    root(g, rstd[:, :], var[:, :])
            if not norm:
                return
            root(LN0, rstd[:, :], var[:, :])
            with pool.Fori(0, B - 1) as g:
                root(g + (LN0 + 1), rstd[:, :], var[:, :])
                low(g)
            low(B - 1)
            if latent:
                root(LN0 + B, c_rstd[:, :], c_var[:, :])
            if route:
                due = pool.alloc_register(f"{tag}_scatters_due")
                pool.reg_mov(due, 0)

                def scatter(g):
                    for t in range(g * TPB, (g + 1) * TPB):
                        moved(pool, G["live"], scattered, due, t, t == 0, lambda at: pool.indirect_dma_start(
                            out=d["scratch_a"], out_offset=bass.IndirectOffsetOnAxis(ap=G["slot"][:, at:at + 1], axis=0),
                            in_=h[:, t * D:(t + 1) * D], in_offset=None, bounds_check=SLOTS - 1, oob_is_err=False))

                for g in range(B):
                    pool.wait_ge(idx_ready, FREE + g + 1)
                    if g == 0:
                        scatter(g)
                    else:
                        some = pool.value_load(G["live_four"][0:1, g:g + 1], min_val=0, max_val=1)
                        with pool.If(some > 0):
                            scatter(g)
                pool.wait_ge(scattered, due)
                pool.free_register(due)

        @block.scalar
        def _(act):
            if ffn:
                with act.Fori(0, B) as g:
                    act.wait_ge(q_turned, g + 1)
                    act.activation(qT[:, :, :], q_ps[:, :, :], ACT.Copy).then_inc(qT_ready, 1)

            if not norm:
                return

            def high(g):
                act.wait_ge(h_ready, g + 1)
                act.activation(h_parts[:, 0, dyn(g * W, W)], h_of(g), ACT.Copy).then_inc(h_hi, 1)

            def keep(g):
                act.wait_ge(h_turned, g + 1)
                act.activation(hT[:, 0, :, dyn(g * S, S)], turn_ps[:, 0, :, :], ACT.Copy)
                act.activation(hT[:, 1, :, dyn(g * S, S)], turn_ps[:, 1, :, :], ACT.Copy).then_inc(hT_ready, 1)

            def take(g):
                if latent:
                    act.wait_ge(ckv_mm, g + 1)
                    act.activation(ckv[:, dyn(g * TPB, TPB), :], ckv_ps[:, :, :], ACT.Copy, scale=1 / W_SCALE).then_inc(ckv_ready, 1)

            high(0)
            high(1)
            keep(0)
            with act.Fori(1, B - 1) as g:
                high(g + 1)
                keep(g)
                take(g - 1)
            keep(B - 1)
            take(B - 2)
            take(B - 1)
            if latent:
                with act.Fori(0, B) as g:
                    act.wait_ge(c_ready, g + 1)
                    act.activation(G["c"][:, dyn(g * TPB, TPB), 0, :], ckv[:, dyn(g * TPB, TPB), :], ACT.Copy).then_inc(c_hi, 1)
                    act.wait_ge(k_turned, g + 1)
                    act.activation(G["kT"][:, :, dyn(g * S, S)], k_ps[:, :, :], ACT.Copy).then_inc(kT_ready, 1)
            if route:
                with act.Fori(0, B) as g:
                    act.wait_ge(top_ready, g + 1)
                    for j in range(TPB):
                        last = act.activation(prob[:, j, :], logit[:, j, :], ACT.Exp, bias=ntop[:, j:j + 1])
                    last.then_inc(e_ready, 1)

        @block.tensor
        def _(pe):
            for free in (hT_ready, qT_ready, x_added, kT_ready, ckv_ready, idx_ready):
                if free is not None:
                    pe.sem_inc(free, FREE)
            if ffn:
                with pe.Fori(0, B) as g:
                    pe.wait_ge(q_ready, g + 1)
                    pe.wait_ge(qT_ready, FREE + g)
                    for j in range(TPB):
                        for k in range(KD):
                            last = pe.transpose(q_ps[:, k, j * P:(j + 1) * P],
                                                q[:, dyn(g * W + (j * D + k * P), P)], G["ident_b"][:, :])
                    last.then_inc(q_turned, 1)
                    pe.wait_ge(qT_ready, FREE + g + 1)
                    pe.wait_ge(x_added, FREE + g)
                    for j in range(TPB):
                        for k in range(KD):
                            for part in range(3):
                                last = pe.matmul(y_ps[:, j * D:(j + 1) * D], qT[:, k, j * P:(j + 1) * P],
                                                 G["ffn_w"][:, k, part, :], start=k + part == 0, stop=k * part == 2)
                    last.then_inc(y_ready, 1)

            if not norm:
                return

            def turn(g):
                pe.wait_ge(h_lo, g + 1)
                pe.wait_ge(hT_ready, FREE + g)
                for k in range(KD):
                    for part in range(2):
                        for j in range(TPB):
                            last = pe.transpose(turn_ps[:, k, part, j * P:(j + 1) * P],
                                                h_parts[:, part, dyn(g * W + (j * D + k * P), P)], G["ident_h"][:, :])
                last.then_inc(h_turned, 1)

            def use(g):
                if latent or route:
                    pe.wait_ge(hT_ready, FREE + g + 1)
                if latent:
                    pe.wait_ge(ckv_ready, FREE + g)
                    for j in range(TPB):
                        for k in range(KD):
                            for a, b in ((0, 0), (0, 1), (1, 0)):
                                last = pe.matmul(ckv_ps[:, j, :], hT[:, k, a, dyn(g * S + j * P, P)],
                                                 G["kv_w"][:, k, b, :], start=k + a + b == 0, stop=k * a == 1)
                    last.then_inc(ckv_mm, 1)
                if route:
                    for j in range(TPB):
                        for k in range(KD):
                            for a, b in ((0, 0), (0, 1), (1, 0)):
                                last = pe.matmul(logit_ps[:, dyn((g * TPB + j) * LW, E)], hT[:, k, a, dyn(g * S + j * P, P)],
                                                 G["gate"][:, k, b, :], start=k + a + b == 0, stop=k * a == 1)
                    last.then_inc(logit_mm, 1)

            turn(0)
            with pe.Fori(0, B - 1) as g:
                turn(g + 1)
                use(g)
            use(B - 1)
            if latent:
                with pe.Fori(0, B) as g:
                    pe.wait_ge(c_lo, g + 1)
                    pe.wait_ge(kT_ready, FREE + g)
                    for part in range(2):
                        for j in range(TPB):
                            last = pe.transpose(k_ps[:, part, j * P:(j + 1) * P],
                                                G["c"][:, dyn(g * TPB + j, 1), part, :].rearrange("p a c -> p (a c)"), G["ident_h"][:, :])
                    last.then_inc(k_turned, 1)
            if route:
                pe.wait_ge(logit_mm, B)
                pe.sem_inc(logit_mm, 1)
                with pe.Fori(0, B) as g:
                    pe.wait_ge(mask_ready, g + 1)
                    pe.wait_ge(idx_ready, FREE + g)
                    for j in range(TPB):
                        pe.matmul(count_ps[:, j, :], G["ones_b"][:, :], mask_sum[:, :], start=True, stop=False)
                        for i in range(j):
                            pe.matmul(count_ps[:, j, :], G["ones_b"][:, :], mask[:, i, :], start=False, stop=False)
                        last = pe.matmul(count_ps[:, j, :], G["tri_b"][:, :], mask[:, j, :], start=False, stop=True)
                    last.then_inc(count_mm, 1)
                    pe.wait_ge(held_ready, g + 1)
                    pe.matmul(live_ps, G["ones_b"][:, :], held[:, :], start=True, stop=True).then_inc(live_mm, 1)

        @block.vector
        def _(dve):
            def layernorm(g, turn, done, meanwhile=lambda: None):
                ch = Chain(dve, chain, turn * LN_CHAIN, LN_CHAIN)
                for j in range(TPB):
                    last = dve.bn_stats(stats[:, j, :], x[:, dyn((g * TPB + j) * D, D)])
                ch.link(last, G["spare"][:, 0:1])
                for j in range(TPB):
                    last = dve.bn_aggr(mv[:, j, :], stats[:, j, :])
                ch.link(last)
                dve.tensor_scalar(var[:, :], mv[:, :, 1], 1e-5, None, ALU.add).then_inc(stat_ready, 1)
                meanwhile()
                dve.wait_ge(rstd_ready, turn + 1)
                for j in range(TPB):
                    at = j * D
                    to = h[:, dyn(g * W + at, D)]
                    last = dve.tensor_scalar(to, x[:, dyn(g * W + at, D)], mv[:, j, 0:1], rstd[:, j:j + 1],
                                             ALU.subtract, ALU.mult)
                last.then_inc(done, 1)
                ch.end()

            if ffn:
                ffn_chain = s("ffn_chain")

                def quantized(g, meanwhile=lambda: None):
                    layernorm(g, g, ffn_chain, meanwhile)
                    dve.wait_ge(ffn_chain, g * FFN_CHAIN + 1)
                    dve.tensor_scalar(above[:, :], h_of(g), 0.33, None, ALU.is_gt).then_inc(ffn_chain, 1)
                    dve.wait_ge(ffn_chain, g * FFN_CHAIN + 2)
                    dve.scalar_tensor_tensor(q[:, dyn(g * W, W)], h_of(g), -0.33, above[:, :],
                                             ALU.is_lt, ALU.subtract).then_inc(q_ready, 1)

                def add(g):
                    dve.wait_ge(y_ready, g + 1)
                    dve.scalar_tensor_tensor(x[:, dyn(g * W, W)], y_ps[:, :], -0.25, x[:, dyn(g * W, W)],
                                             ALU.mult, ALU.add).then_inc(x_added, 1)

                quantized(0)
                quantized(1)
                with dve.Fori(2, B) as g:
                    quantized(g, lambda: add(g - 2))
                if not norm:
                    add(B - 2)
                    add(B - 1)
                    return
                for g in range(2):
                    dve.wait_ge(x_added, FREE + g + 1)
                    layernorm(g, g + LN0, h_ready, lambda: add(B - 2 + g))
                with dve.Fori(2, B) as g:
                    dve.wait_ge(x_added, FREE + g + 1)
                    layernorm(g, g + LN0, h_ready)
            else:
                with dve.Fori(0, B) as g:
                    layernorm(g, g, h_ready)
            if latent:
                latent_chain = s("latent_chain")

                def scaled(g):
                    for j in range(TPB):
                        at = dyn(g * TPB + j, 1)
                        to = ckv[:, at, 0:LORA].rearrange("p a l -> p (a l)")
                        last = dve.scalar_tensor_tensor(to, to, c_rstd[:, at], G["c_norm"][:, :], ALU.mult, ALU.mult)
                    last.then_inc(c_ready, 1)

                def low(g):
                    tiles = dyn(g * TPB, TPB)
                    dve.wait_ge(c_hi, g + 1)
                    dve.tensor_tensor(G["c"][:, tiles, 1, :], ckv[:, tiles, :],
                                      G["c"][:, tiles, 0, :], ALU.subtract).then_inc(c_lo, 1)

                ch = Chain(dve, latent_chain, 0, 2)
                dve.wait_ge(ckv_ready, FREE + B)
                ch.link(dve.tensor_tensor(sq[:, :, :], ckv[:, :, 0:LORA], ckv[:, :, 0:LORA], ALU.mult))
                ch.link(dve.tensor_reduce(c_var[:, :], sq[:, :, :], X, ALU.add))
                ch.end()
                dve.tensor_scalar(c_var[:, :], c_var[:, :], 1 / LORA, 1e-6, ALU.mult, ALU.add).then_inc(stat_ready, 1)
                dve.wait_ge(rstd_ready, LN0 + B + 1)
                scaled(0)
                with dve.Fori(0, B - 1) as g:
                    scaled(g + 1)
                    low(g)
                low(B - 1)
            if route:
                zeroed = s("sum_zeroed")
                dve.memset(mask_sum[:, :], 0.0).then_inc(zeroed, 1)
                dve.wait_ge(zeroed, 1)
                dve.wait_ge(consts, 2)
                with dve.Fori(0, B) as g:
                    ch = Chain(dve, route_chain, g * CHAIN, CHAIN)
                    dve.wait_ge(logit_mm, g + 2)
                    for j in range(TPB):
                        last = dve.scalar_tensor_tensor(logit[:, j, :], logit_ps[:, dyn((g * TPB + j) * LW, E)], 1 / W_SCALE,
                                                        G["absent"][:, :], ALU.mult, ALU.add)
                    ch.link(last, G["spare"][:, 0:1])
                    for j in range(TPB):
                        last = dve.max(top[:, j, :], logit[:, j, :])
                    ch.link(last)
                    dve.tensor_scalar(ntop[:, :], top[:, :, 0], -1.0, None, ALU.mult).then_inc(top_ready, 1)
                    ch.link(dve.tensor_scalar(edge[:, :], top[:, :, TOPK - 1], -1e38, None, ALU.max))
                    for j in range(TPB):
                        last = dve.tensor_scalar(mask[:, j, :], logit[:, j, :], edge[:, j:j + 1], None, ALU.is_ge)
                    last.then_inc(mask_ready, 1)
                    dve.wait_ge(count_mm, g + 1)
                    ch.link(dve.tensor_tensor(key[:, :, :], count_ps[:, :, :], first_slot[:, :, :], ALU.add))
                    taken = same[:, :, 0, :]
                    dve.wait_ge(mask_ready, g + 1)
                    ch.link(dve.scalar_tensor_tensor(taken, count_ps[:, :, :], float(CAP), mask[:, :, :],
                                                     ALU.is_le, ALU.mult))
                    ch.link(dve.tensor_tensor(key[:, :, :], key[:, :, :], taken, ALU.mult), G["spare"][:, 0:1])
                    for j in range(TPB):
                        last = dve.max(keyt[:, j, :], key[:, j, :])
                    ch.link(last)
                    flat = keyt[:, :, :].rearrange("p j k -> p (j k)")
                    dve.tensor_scalar(held[:, :], flat, 0.5, None, ALU.is_gt).then_inc(held_ready, 1)
                    ch.link(dve.tensor_scalar(late[:, :], flat, 0.5, 1e6, ALU.is_lt, ALU.mult))
                    ch.link(dve.scalar_tensor_tensor(G["slot"][:, dyn(g * TPB * TOPK, TPB * TOPK)], flat, -1.0, late[:, :],
                                                     ALU.add, ALU.add))
                    ch.link(dve.tensor_tensor(added[:, :], mask[:, 0, :], mask[:, 1, :], ALU.add))
                    ch.link(dve.tensor_tensor(added[:, :], added[:, :], mask[:, 2, :], ALU.add))
                    ch.link(dve.tensor_tensor(added[:, :], added[:, :], mask[:, 3, :], ALU.add))
                    ch.link(dve.tensor_tensor(mask_sum[:, :], mask_sum[:, :], added[:, :], ALU.add))
                    dve.wait_ge(live_mm, g + 1)
                    ch.link(dve.tensor_reduce(most[:, :], live_ps, X, ALU.max))
                    ch.link(dve.tensor_scalar(G["live_four"][:, dyn(g, 1)], most[:, :], 0.5, None, ALU.is_gt))
                    dve.tensor_scalar(G["live"][:, dyn(g * TPB * TOPK, TPB * TOPK)], live_ps, 0.5, None,
                                      ALU.is_gt).then_inc(idx_ready, 1)
                    dve.wait_ge(e_ready, g + 1)
                    ch.link(dve.tensor_tensor(prob[:, :, :], prob[:, :, :], mask[:, :, :], ALU.mult))
                    ch.link(dve.tensor_reduce(den[:, :], prob[:, :, :], X, ALU.add))
                    ch.link(dve.reciprocal(den[:, :], den[:, :]))
                    for j in range(TPB):
                        last = dve.tensor_scalar(prob[:, j, :], prob[:, j, :], den[:, j:j + 1], 0.5, ALU.mult, ALU.mult)
                    ch.link(last)
                    ch.link(dve.tensor_tensor(prob[:, :, :], prob[:, :, :], taken, ALU.mult))
                    ch.link(dve.tensor_tensor(same[:, :, :, :], key[:, :, :].unsqueeze(2).to_broadcast([P, TPB, TOPK, E]),
                                              keyt[:, :, :].unsqueeze(3).to_broadcast([P, TPB, TOPK, E]), ALU.is_equal))
                    ch.link(dve.tensor_tensor(same[:, :, :, :], same[:, :, :, :],
                                              prob[:, :, :].unsqueeze(2).to_broadcast([P, TPB, TOPK, E]), ALU.mult))
                    ch.link(dve.tensor_reduce(G["slot_w"][:, dyn(g * TPB * TOPK, TPB * TOPK)], same[:, :, :, :].rearrange("p j k e -> p (j k) e"), X, ALU.add))
                    ch.end()


def experts(nc, d, G, sem, sb, ps, tag):
    def s(name):
        return sem(f"{tag}_{name}")

    EC = 4
    NCH = E // EC
    SW = 256
    RING = 3
    HID_SCALE = 16.0
    loaded = [s(f"loaded{i}") for i in range(RING)]
    stored = [s(f"stored{i}") for i in range(RING)]
    turned, xT_hi, xT_lo, up_hi, down_hi, w_lo, gu_mm, gate_ready, hid_ready, hid_hi, hid_lo, y_mm, y_ready = (
        s(n) for n in ("turned", "xT_hi", "xT_lo", "up_hi", "down_hi", "w_lo", "gu_mm", "gate_ready", "hid_ready",
                       "hid_hi", "hid_lo", "y_mm", "y_ready"))
    with ExitStack() as c, nc.Block(f"experts_{tag}") as block:
        gu = [sb(f"gu{i}", [P, EC, KD, 2 * INTER], F32, c) for i in range(RING)]
        gu_s = [sb(f"gu_s{i}", [P, 2, EC, KD, 2 * INTER], F16, c) for i in range(RING)]
        dn = [sb(f"dn{i}", [INTER, EC, D], F32, c) for i in range(RING)]
        dn_s = [sb(f"dn_s{i}", [INTER, 2, EC, D], F16, c) for i in range(RING)]
        xs = [sb(f"xs{i}", [CAP, EC, D], F32, c) for i in range(RING)]
        xT = [sb(f"xT{i}", [P, 2, EC, KD * CAP], F16, c) for i in range(RING)]
        gate = [sb(f"gate{i}", [INTER, EC, CAP], F32, c) for i in range(RING)]
        hid = [sb(f"hid{i}", [INTER, EC, CAP], F32, c) for i in range(RING)]
        hid_s = [sb(f"hid_s{i}", [INTER, 2, EC, CAP], F16, c) for i in range(RING)]
        ys = [sb(f"ys{i}", [CAP, EC, D], F32, c) for i in range(RING)]
        t_ps = ps("t_ps", [P, EC, SW], F32, c)
        gu_ps = ps("gu_ps", [P, EC, SW], F32, c)
        y_ps = ps("ye_ps", [P, EC, D], F32, c)
        gu_d = d["gupT"].rearrange("(n m) (k p) o -> n p m k o", m=EC, p=P)
        dn_d = d["downT"].rearrange("(n m) i o -> n i m o", m=EC)
        xs_d = d["scratch_a"].rearrange("(n m s) i -> n s m i", m=EC, s=CAP)
        ys_d = d["scratch_b"].rearrange("(n m s) i -> n s m i", m=EC, s=CAP)
        LOADS = 16 * (EC + 2)

        def steps(eng, step):
            last = NCH // RING - 1
            for i in range(RING):
                step(0, i)
            with eng.Fori(1, last) as it:
                for i in range(RING):
                    step(it, i)
            for i in range(RING):
                step(last, i)

        def after(it, i, by=1):
            if isinstance(it, int) and it * RING + i + by >= NCH:
                return None
            return it + (i + by) // RING, (i + by) % RING

        def before(it, i):
            if isinstance(it, int) and it * RING + i == 0:
                return None
            return (it, i - 1) if i else (it - 1, RING - 1)

        @block.sync
        def _(sp):
            for n in range(NCH + 4):
                if n < NCH:
                    i = n % RING
                    if n >= RING:
                        sp.wait_ge(w_lo, n - RING + 1)
                        sp.wait_ge(turned, n - RING + 1)
                    for m in range(EC):
                        sp.dma_start(gu[i][:, m], gu_d[n, :, m]).then_inc(loaded[i], 16)
                    sp.dma_start(dn[i][:, :, :], dn_d[n]).then_inc(loaded[i], 16)
                    sp.dma_start(xs[i][:, :, :], xs_d[n]).then_inc(loaded[i], 16)
                if n >= 4:
                    o = n - 4
                    sp.wait_ge(y_ready, FREE + o + 1)
                    sp.dma_start(ys_d[o], ys[o % RING][:, :, :]).then_inc(stored[o % RING], 16)
            for i in range(RING):
                sp.wait_ge(stored[i], 16 + 16 * NCH // RING)

        @block.tensor
        def _(pe):
            def turn(it, i):
                pe.wait_ge(loaded[i], LOADS * (it + 1))
                pe.wait_ge(xT_lo, FREE + it * RING + i)
                for m in range(EC):
                    for k in range(KD):
                        last = pe.transpose(t_ps[:, m, k * CAP:(k + 1) * CAP], xs[i][:, m, k * P:(k + 1) * P],
                                            G["ident"][0:CAP, 0:CAP])
                last.then_inc(turned, 1)

            def up(it, i):
                n = it * RING + i
                pe.wait_ge(xT_lo, FREE + n + 1)
                pe.wait_ge(w_lo, n + 1)
                pe.wait_ge(hid_ready, FREE + n)
                for m in range(EC):
                    for half in range(2):
                        for k in range(KD):
                            for a, b in ((0, 0), (0, 1), (1, 0)):
                                last = pe.matmul(gu_ps[0:INTER, m, half * CAP:(half + 1) * CAP],
                                                 gu_s[i][:, a, m, k, half * INTER:(half + 1) * INTER],
                                                 xT[i][:, b, m, k * CAP:(k + 1) * CAP],
                                                 start=k + a + b == 0, stop=k * a == 1)
                last.then_inc(gu_mm, 1)

            def down(it, i):
                n = it * RING + i
                pe.wait_ge(hid_lo, n + 1)
                pe.wait_ge(y_ready, FREE + n)
                for m in range(EC):
                    for a, b in ((0, 0), (0, 1), (1, 0)):
                        last = pe.matmul(y_ps[0:CAP, m, :], hid_s[i][:, a, m, :], dn_s[i][:, b, m, :],
                                         start=a + b == 0, stop=a == 1)
                last.then_inc(y_mm, 1)

            def step(it, i):
                if after(it, i):
                    turn(*after(it, i))
                up(it, i)
                if before(it, i):
                    down(*before(it, i))

            for free in (xT_lo, hid_ready, y_ready):
                pe.sem_inc(free, FREE)
            turn(0, 0)
            steps(pe, step)
            down(NCH // RING - 1, RING - 1)

        @block.scalar
        def _(act):
            def split_rows(it, i):
                act.wait_ge(turned, it * RING + i + 1)
                act.activation(xT[i][:, 0, :, :], t_ps[:, :, 0:KD * CAP], ACT.Copy).then_inc(xT_hi, 1)

            def split_up(it, i):
                act.wait_ge(loaded[i], LOADS * (it + 1))
                act.activation(gu_s[i][:, 0], gu[i][:, :, :, :], ACT.Copy, scale=W_SCALE).then_inc(up_hi, 1)

            def split_down(it, i):
                act.activation(dn_s[i][:, 0], dn[i][:, :, :], ACT.Copy, scale=W_SCALE).then_inc(down_hi, 1)

            def out(it, i):
                act.wait_ge(y_mm, it * RING + i + 1)
                act.wait_ge(stored[i], 16 * (it + 1))
                act.activation(ys[i][:, :, :], y_ps[0:CAP, :, :], ACT.Copy,
                               scale=1 / (W_SCALE * HID_SCALE)).then_inc(y_ready, 1)

            def step(it, i):
                if after(it, i):
                    split_rows(*after(it, i))
                n = it * RING + i
                act.wait_ge(gu_mm, n + 1)
                act.activation(gate[i][:, :, :], gu_ps[0:INTER, :, 0:CAP], ACT.Silu,
                               scale=1 / W_SCALE).then_inc(gate_ready, 1)
                if after(it, i, 2):
                    split_up(*after(it, i, 2))
                act.wait_ge(hid_ready, FREE + n + 1)
                act.activation(hid_s[i][:, 0], hid[i][:, :, :], ACT.Copy).then_inc(hid_hi, 1)
                if before(it, i):
                    out(*before(it, i))
                if after(it, i, 2):
                    split_down(*after(it, i, 2))

            for i in range(RING):
                act.sem_inc(stored[i], 16)
            split_rows(0, 0)
            for i in range(2):
                split_up(0, i)
                split_down(0, i)
            steps(act, step)
            out(NCH // RING - 1, RING - 1)

        @block.vector
        def _(dve):
            def split_rows(it, i):
                dve.wait_ge(xT_hi, it * RING + i + 1)
                dve.tensor_tensor(xT[i][:, 1, :, :], t_ps[:, :, 0:KD * CAP], xT[i][:, 0, :, :],
                                  ALU.subtract).then_inc(xT_lo, 1)

            def split_up(it, i):
                dve.wait_ge(up_hi, it * RING + i + 1)
                dve.scalar_tensor_tensor(gu_s[i][:, 1], gu[i][:, :, :, :], W_SCALE, gu_s[i][:, 0], ALU.mult, ALU.subtract)

            def split_down(it, i):
                dve.wait_ge(down_hi, it * RING + i + 1)
                dve.scalar_tensor_tensor(dn_s[i][:, 1], dn[i][:, :, :], W_SCALE, dn_s[i][:, 0], ALU.mult,
                                         ALU.subtract).then_inc(w_lo, 1)

            def step(it, i):
                if after(it, i):
                    split_rows(*after(it, i))
                n = it * RING + i
                dve.wait_ge(gate_ready, n + 1)
                dve.scalar_tensor_tensor(hid[i][:, :, :], gu_ps[0:INTER, :, CAP:2 * CAP], HID_SCALE / W_SCALE,
                                         gate[i][:, :, :], ALU.mult, ALU.mult).then_inc(hid_ready, 1)
                if after(it, i, 2):
                    split_up(*after(it, i, 2))
                dve.wait_ge(hid_hi, n + 1)
                dve.tensor_tensor(hid_s[i][:, 1], hid[i][:, :, :], hid_s[i][:, 0], ALU.subtract).then_inc(hid_lo, 1)
                if after(it, i, 2):
                    split_down(*after(it, i, 2))

            split_rows(0, 0)
            for i in range(2):
                split_up(0, i)
                split_down(0, i)
            steps(dve, step)


def combine(nc, d, G, sem, sb, tag, weights=False, out=None):
    def s(name):
        return sem(f"{tag}_{name}")

    NB = 4
    LAG = 2
    cleared = s("cleared")
    gathered = [s(f"gathered{i}") for i in range(NB)]
    rows_ready, combined, added = s("rows_ready"), s("combined"), s("added")
    with ExitStack() as c, nc.Block(f"combine_{tag}") as block:
        y = [sb(f"y{i}", [P, TOPK, D], F32, c) for i in range(NB)]
        if out is not None:
            stored = s("stored")

            @block.sync
            def _(sp):
                for g in range(NT // NB):
                    sp.wait_ge(combined, (g + 1) * NB)
                    rows = out[g * NB * P:(g + 1) * NB * P].rearrange("(t p) d -> p t d", p=P)
                    sp.dma_start(rows, G["x"][:, g * NB * D:(g + 1) * NB * D].rearrange("p (t d) -> p t d", d=D)).then_inc(stored, 16)
                sp.wait_ge(stored, 16 * NT // NB)

        if weights:
            raw_in, high, low = [s(f"raw_in{i}") for i in range(4)], s("weights_high"), s("weights_low")
            raw = [sb(f"raw{i}", [P, KD * H * P], F32, c) for i in range(2)]
            src = [d[n].rearrange("(k p) q -> p k q", p=P) for n in ("wqT", "wkT", "wvT")]
            src.append(d["woT1"].rearrange("(h r) o -> r h o", r=P))
            parts = [G[n] for n in ("w_q", "w_k", "w_v", "w_o")]
            view = [raw[i % 2][:, :].rearrange("p (a b) -> p a b", a=H if i == 3 else KD) for i in range(4)]

            @block.sync
            def _(sp):
                for i in range(4):
                    if i >= 2:
                        sp.wait_ge(low, i - 1)
                    sp.dma_start(view[i], src[i]).then_inc(raw_in[i], 16)

            @block.scalar
            def _(act):
                for i in range(4):
                    act.wait_ge(raw_in[i], 16)
                    act.activation(parts[i][:, :, 0, :], view[i], ACT.Copy, scale=W_SCALE).then_inc(high, 1)

        @block.gpsimd
        def _(pool):
            due = [pool.alloc_register(f"{tag}_gathers_due{i}") for i in range(NB)]
            for i in range(NB):
                pool.reg_mov(due[i], 0)

            def arrived(t):
                pool.wait_ge(gathered[t % NB], due[t % NB])
                pool.sem_inc(rows_ready, 1)

            def gather(g):
                for t in range(g * NB, (g + 1) * NB):
                    if g:
                        pool.wait_ge(combined, t - NB + 1)
                    else:
                        pool.wait_ge(cleared, t + 1)
                    moved(pool, G["live"], gathered[t % NB], due[t % NB], t, g == 0, lambda at: pool.indirect_dma_start(
                        out=y[t % NB][:, at % TOPK, :], out_offset=None, in_=d["scratch_b"],
                        in_offset=bass.IndirectOffsetOnAxis(ap=G["slot"][:, at:at + 1], axis=0),
                        bounds_check=SLOTS - 1, oob_is_err=False))
                    if t >= LAG:
                        arrived(t - LAG)

            gather(0)
            for g in range(1, NT // NB):
                some = pool.value_load(G["live_four"][0:1, g:g + 1], min_val=0, max_val=1)
                with pool.If(some > 0):
                    gather(g)
                with pool.Else():
                    for t in range(g * NB - LAG, g * NB):
                        arrived(t)
                    pool.sem_inc(rows_ready, NB - LAG)
            for t in range(NT - LAG, NT):
                arrived(t)
            for i in range(NB):
                pool.free_register(due[i])

        @block.vector
        def _(dve):
            dve.sem_inc(added, FREE)
            for i in range(NB):
                dve.memset(y[i][:, :, :], 0.0).then_inc(cleared, 1)

            def split(i):
                dve.wait_ge(high, i + 1)
                dve.scalar_tensor_tensor(parts[i][:, :, 1, :], view[i], W_SCALE, parts[i][:, :, 0, :],
                                         ALU.mult, ALU.subtract).then_inc(low, 1)

            def add(t, i, ks):
                xt = G["x"][:, dyn(t * D, D)]
                for k in ks:
                    dve.wait_ge(added, FREE + t * TOPK + k)
                    dve.scalar_tensor_tensor(xt, y[i][:, k, :], G["slot_w"][:, dyn(t * TOPK + k, 1)], xt,
                                             ALU.mult, ALU.add).then_inc(added, 1)

            def live(t, k):
                return dve.value_load(G["live"][0:1, dyn(t * TOPK + k, 1)], min_val=0, max_val=1)

            def four(it):
                some = dve.value_load(G["live_four"][0:1, dyn(it, 1)], min_val=0, max_val=1)
                with dve.If(some > 0):
                    for i in range(NB):
                        t = it * NB + i
                        dve.wait_ge(rows_ready, t + 1)
                        with dve.If(live(t, 0) > 0):
                            add(t, i, range(KG))
                            with dve.If(live(t, KG) > 0):
                                add(t, i, range(KG, TOPK))
                            with dve.Else():
                                dve.sem_inc(added, TOPK - KG)
                        with dve.Else():
                            dve.sem_inc(added, TOPK)
                        dve.wait_ge(added, FREE + (t + 1) * TOPK)
                        dve.sem_inc(combined, 1)
                with dve.Else():
                    dve.sem_inc(added, NB * TOPK)
                    dve.sem_inc(combined, NB)

            if weights:
                split(0)
                split(1)
                four(0)
                split(2)
                split(3)
            else:
                four(0)
            with dve.Fori(1, NT // NB) as it:
                four(it)


def attention(nc, d, G, sem, sb, ps, tag, latent):
    def s(name):
        return sem(f"{tag}_{name}")

    NPROJ = 1 if latent else 3
    NO = H // 2 if latent else H
    scale = (NOPE + ROPE if latent else DV) ** -0.5
    proj_mm, proj_hi, proj_done = s("proj_mm"), s("proj_hi"), s("proj_done")
    s_mm, max_ready, exp_done, rinv_ready, p_ready = s("scores_mm"), s("max_ready"), s("exp_done"), s("rinv_ready"), s("p_ready")
    turned, t_hi, t_done = s("p_turned"), s("pT_hi"), s("pT_done")
    o_mm, o_hi, o_done, y_mm, y_done = s("o_mm"), s("o_hi"), s("o_done"), s("y_mm"), s("y_done")
    v_ready = s("v_ready") if latent else None
    zeroed, zeros_out = (s("zeroed"), s("zeros_out")) if latent else (None, None)
    ZR = 12
    hT = G["hT"]
    order = (3, 2, 0, 1)
    PIECES = 4
    HALVES = 2
    A_BANKS = 1 if latent else 2
    QUERY, KEYS, VALUES = range(3)

    def proj_count(b, h, which):
        if latent:
            return b * H + h
        ends = isinstance(h, int)
        if which == VALUES:
            return b * 3 * H + (3 * H - 1 if ends and h == H - 1 else h * 3 + 4)
        if which == KEYS:
            return b * 3 * H + (1 if ends and h == 0 else h * 3)
        return b * 3 * H + (0 if ends and h == 0 else h * 3 - 1)

    with ExitStack() as c, nc.Block(f"attention_{tag}") as block:
        qT = [sb(f"qT{i}", [P, 2, S], F16, c) for i in range(2)]
        if latent:
            v = [sb("v_batch", [P, TPB, 2, LORA], F16, c)] * 2
        else:
            kTh = [sb(f"kTh{i}", [P, 2, S], F16, c) for i in range(2)]
            v = [sb(f"v{i}", [P, TPB, 2, P], F16, c) for i in range(2)]
        p = [sb(f"p{i}", [P, CAUSAL], F32, c) for i in range(2)]
        pT = [sb(f"pT{i}", [P, 2, CAUSAL], F16, c) for i in range(2)]
        nmax = [sb(f"nmax{i}", [P, TPB], F32, c) for i in range(2)]
        carrier = sb("carrier", [P, 2], F32, c)
        total = [sb(f"total{i}", [P, TPB], F32, c) for i in range(2)]
        rinv = [sb(f"rinv{i}", [P, TPB], F32, c) for i in range(2)]
        oT = sb("oT", [P, NO, 2, S], F16, c)
        T_AT = 6 * 512 - CAUSAL if latent else 5 * 512 - CAUSAL
        s_ps = ps("s_ps", [P, T_AT + CAUSAL], F32, c)
        t_ps = s_ps[:, T_AT:T_AT + CAUSAL]
        y_ps = s_ps[:, T_AT + CAUSAL - TPB * D:T_AT + CAUSAL]
        o_ps = ps("o_ps", [P, S], F32, c)
        a_ps = [ps(f"a_ps{i}", [P, S], F32, c) for i in range(A_BANKS)]

        if latent:
            zero = sb("zero", [P, ZR * D], F32, c)

            @block.sync
            def _(sp):
                sp.wait_ge(zeroed, 1)
                rows = d["scratch_a"].rearrange("(a p r) d -> a p (r d)", p=P, r=ZR)
                for i in range(SLOTS // (P * ZR)):
                    sp.dma_start(rows[i], zero[:, :]).then_inc(zeros_out, 16)
                sp.wait_ge(zeros_out, 16 * SLOTS // (P * ZR))

        def heads(eng, opening, step, finish):
            def sequence(b, more):
                for h in range(4):
                    step(b, h, h % 2)
                with eng.Fori(4, H - 4, 2) as h:
                    step(b, h, 0)
                    step(b, h + 1, 1)
                for h in range(H - 4, H):
                    step(b, h, h % 2)
                finish(b, more)

            opening(0)
            with eng.Fori(0, B - 1) as b:
                sequence(b, True)
            sequence(B - 1, False)

        def inner(h):
            return not isinstance(h, int)

        def a_bank(h, par, which):
            if latent:
                return a_ps[0]
            if not inner(h) and h == 0 and which != VALUES:
                return a_ps[which]
            return a_ps[1 - par if which == QUERY else par]

        def first(b, project):
            project(b, 0, 0, QUERY)
            if latent:
                project(b, 1, 1, QUERY)
            else:
                project(b, 0, 0, KEYS)

        @block.tensor
        def _(pe):
            def project(b, h, par, which):
                pe.wait_ge(proj_done, proj_count(b, h, which) + 1)
                tok, to = dyn(b * S, S), a_bank(h, par, which)
                if which != VALUES:
                    w = G["q_w"] if latent else (G["w_q"], G["w_k"])[which]
                    for k in range(KD):
                        for a, x in ((0, 0), (0, 1), (1, 0)):
                            last = pe.matmul(to[:, :], w[:, k, a, dyn(h * P, P)], hT[:, k, x, tok],
                                             start=k + a + x == 0, stop=k * a == 1)
                else:
                    for j in range(TPB):
                        for k in range(KD):
                            for a, x in ((0, 0), (0, 1), (1, 0)):
                                last = pe.matmul(to[:, j * P:(j + 1) * P], hT[:, k, a, dyn(b * S + j * P, P)],
                                                 G["w_v"][:, k, x, dyn(h * P, P)], start=k + a + x == 0, stop=k * a == 1)
                last.then_inc(proj_mm, 1)

            def scores(b, h, par):
                n = b * H + h
                pe.wait_ge(proj_done, A_BANKS + proj_count(b, h, KEYS) + 1)
                for i, upto in zip(order, (1, 3, 3, 4)):
                    pe.wait_ge(exp_done, n * PIECES + upto)
                    if not latent and i == 1:
                        pe.wait_ge(t_done, t_count(b, h))
                    cols = (i + 1) * P
                    here = s_ps[:, Q_AT[i]:Q_AT[i] + cols]
                    for e, (a, x) in enumerate(((0, 0), (0, 1), (1, 0))):
                        keys = G["kT"][:, x, dyn(b * S, cols)] if latent else kTh[par][:, x, 0:cols]
                        last = pe.matmul(here, qT[par][:, a, i * P:(i + 1) * P], keys, start=e == 0, stop=e == 2)
                        if e == 0:
                            pe.matmul(s_ps[:, Q_AT[i] + i * P:Q_AT[i] + cols], G["ident_b"][:, :], G["mask_b"][:, :],
                                      start=False, stop=False)
                    last.then_inc(s_mm, 1)

            def t_count(b, h):
                return FREE + b * H * HALVES + (0 if not inner(h) and h < 2 else (h - 1) * HALVES)

            def turn(b, h, par):
                n = b * H + h
                pe.wait_ge(p_ready, n * PIECES + PIECES)
                if not inner(h) and h == 0:
                    pe.wait_ge(y_done, FREE + b)
                if not latent:
                    pe.wait_ge(exp_done, (n + (2 if inner(h) or h < H - 1 else 1)) * PIECES + PIECES)
                for half, tiles in enumerate(((2, 0), (1, 3))):
                    pe.wait_ge(t_done, n * HALVES + half + 1)
                    for j in tiles:
                        for i in range(j, TPB):
                            at = K_AT[j] + (i - j) * P
                            last = pe.transpose(t_ps[:, at:at + P], p[par][:, Q_AT[i] + j * P:Q_AT[i] + (j + 1) * P],
                                                G["ident"][:, :])
                    last.then_inc(turned, 1)

            def outputs(b, h, pars):
                pe.wait_ge(t_done, (b * H + h) * HALVES + 2 * HALVES)
                if not latent:
                    pe.wait_ge(proj_done, A_BANKS + proj_count(b, h, VALUES) + 1)
                pe.wait_ge(o_done, FREE + b * NO + ((h >> 1) if latent else h))
                rows = P // len(pars)
                for j in range(TPB):
                    for e, (a, x) in enumerate(((0, 0), (0, 1), (1, 0))):
                        for side, par in enumerate(pars):
                            last = pe.matmul(o_ps[side * rows:(side + 1) * rows, j * P:S], v[par][:, j, a, :],
                                             pT[par][:, x, K_AT[j]:K_AT[j] + (TPB - j) * P],
                                             start=j + e == 0, stop=j == TPB - 1 and e == 2)
                last.then_inc(o_mm, 1)

            def step(b, h, par):
                if latent and par == 0 and (inner(h) or h >= 4):
                    outputs(b, h - 3, (0, 1))
                if inner(h) or h >= 2:
                    turn(b, h - 2, par)
                if not latent and (inner(h) or h >= 1):
                    project(b, h - 1, 1 - par, VALUES)
                if inner(h) or h >= 1:
                    scores(b, h, par)
                elif latent:
                    pe.wait_ge(v_ready, b + 1)
                if latent:
                    if inner(h) or h < H - 2:
                        project(b, h + 2, par, QUERY)
                    return
                if inner(h) or h < H - 1:
                    project(b, h + 1, 1 - par, QUERY)
                if inner(h) or h >= 2:
                    outputs(b, h - 2, (par,))
                if inner(h) or h < H - 1:
                    project(b, h + 1, 1 - par, KEYS)

            def finish(b, more):
                if latent:
                    outputs(b, H - 3, (0, 1))
                turn(b, H - 2, 0)
                if not latent:
                    project(b, H - 1, 1, VALUES)
                    outputs(b, H - 2, (0,))
                if more:
                    first(b + 1, project)
                turn(b, H - 1, 1)
                if more:
                    scores(b + 1, 0, 0)
                outputs(b, H - 1, (0, 1) if latent else (1,))
                pe.wait_ge(o_done, FREE + (b + 1) * NO)
                w = G["vo_w"] if latent else G["w_o"]
                for i in range(TPB):
                    for m in range(NO):
                        for a, x in ((0, 0), (0, 1), (1, 0)):
                            last = pe.matmul(y_ps[:, i * D:(i + 1) * D], oT[:, m, a, i * P:(i + 1) * P], w[:, m, x, :],
                                             start=m + a + x == 0, stop=m == NO - 1 and a == 1)
                last.then_inc(y_mm, 1)

            def opening(b):
                first(b, project)
                scores(b, 0, 0)

            for free in (o_done, y_done):
                pe.sem_inc(free, FREE)
            pe.sem_inc(proj_done, A_BANKS)
            pe.sem_inc(exp_done, PIECES)
            pe.sem_inc(t_done, HALVES)
            heads(pe, opening, step, finish)

        def proj_out(h, par, which):
            src = a_bank(h, par, which)[:, :]
            if which == QUERY:
                return (lambda part: qT[par][:, part, :]), src
            if which == KEYS:
                return (lambda part: kTh[par][:, part, :]), src
            return (lambda part: v[par][:, :, part, :]), src.rearrange("p (j d) -> p j d", j=TPB)

        def proj_scale(which):
            return (scale if which == QUERY else 1.0) / W_SCALE

        def o_part(at, part):
            return oT[:, at, part, :] if isinstance(at, int) else oT[:, dyn(at, 1), part, :].rearrange("p a c -> p (a c)")

        @block.scalar
        def _(act):
            def project(b, h, par, which):
                act.wait_ge(proj_mm, proj_count(b, h, which) + 1)
                to, src = proj_out(h, par, which)
                act.activation(to(0), src, ACT.Copy, scale=proj_scale(which)).then_inc(proj_hi, 1)

            def exps(b, h, par):
                for i, upto in zip(order, (1, 3, 3, 4)):
                    act.wait_ge(max_ready, (b * H + h) * PIECES + upto)
                    cols = (i + 1) * P
                    act.activation(p[par][:, Q_AT[i]:Q_AT[i] + cols], s_ps[:, Q_AT[i]:Q_AT[i] + cols], ACT.Exp,
                                   bias=nmax[par][:, i:i + 1], accum_out=total[par][:, i:i + 1]).then_inc(exp_done, 1)

            def turn(b, h, par):
                n = b * H + h
                for half, (lo, hi) in enumerate(HALF_AT):
                    act.wait_ge(turned, n * HALVES + half + 1)
                    act.activation(pT[par][:, 0, lo:hi], t_ps[:, lo:hi], ACT.Copy).then_inc(t_hi, 1)

            def outputs(b, h):
                at = (h >> 1) if latent else h
                act.wait_ge(o_mm, b * NO + at + 1)
                act.activation(o_part(at, 0), o_ps[:, :], ACT.Copy, scale=O_SCALE / P_SCALE).then_inc(o_hi, 1)

            def values(b):
                if latent:
                    act.activation(v[0][:, :, :, :], G["c"][:, dyn(b * TPB, TPB), :, 0:LORA], ACT.Copy).then_inc(v_ready, 1)

            def step(b, h, par):
                if latent and (inner(h) or 1 <= h < H - 1):
                    project(b, h + 1, 1 - par, QUERY)
                if inner(h) or h >= 2:
                    turn(b, h - 2, par)
                if latent and par == 0 and (inner(h) or h >= 4):
                    outputs(b, h - 4)
                if not latent and (inner(h) or h >= 1):
                    project(b, h - 1, 1 - par, VALUES)
                if inner(h) or h >= 1:
                    exps(b, h, par)
                if latent:
                    return
                if inner(h) or h < H - 1:
                    project(b, h + 1, 1 - par, QUERY)
                if inner(h) or h >= 2:
                    outputs(b, h - 2)
                if inner(h) or h < H - 1:
                    project(b, h + 1, 1 - par, KEYS)

            def finish(b, more):
                if latent:
                    outputs(b, H - 4)
                turn(b, H - 2, 0)
                if not latent:
                    project(b, H - 1, 1, VALUES)
                    outputs(b, H - 2)
                if more:
                    first(b + 1, project)
                turn(b, H - 1, 1)
                if more:
                    exps(b + 1, 0, 0)
                outputs(b, H - 1)
                if more:
                    values(b + 1)

            def opening(b):
                values(b)
                first(b, project)
                exps(b, 0, 0)

            heads(act, opening, step, finish)

        @block.vector
        def _(dve):
            def project(b, h, par, which):
                dve.wait_ge(proj_hi, proj_count(b, h, which) + 1)
                to, src = proj_out(h, par, which)
                dve.scalar_tensor_tensor(to(1), src, proj_scale(which), to(0), ALU.mult, ALU.subtract).then_inc(proj_done, 1)

            def maxima(b, h, par):
                n = b * H + h
                for i, upto in zip(order, (1, 3, 3, 4)):
                    dve.wait_ge(s_mm, n * PIECES + upto)
                    dve.tensor_reduce(nmax[par][:, i:i + 1], s_ps[:, Q_AT[i]:Q_AT[i] + (i + 1) * P], X, ALU.max,
                                      negate=True).then_inc(max_ready, 1)

            def inverse(b, h, par):
                dve.wait_ge(exp_done, (b * H + h) * PIECES + 2 * PIECES)
                dve.reciprocal(rinv[par][:, :], total[par][:, :]).then_inc(rinv_ready, 1)

            def turn(b, h, par):
                n = b * H + h
                for half, (lo, hi) in enumerate(HALF_AT):
                    dve.wait_ge(t_hi, n * HALVES + half + 1)
                    dve.tensor_tensor(pT[par][:, 1, lo:hi], t_ps[:, lo:hi], pT[par][:, 0, lo:hi],
                                      ALU.subtract).then_inc(t_done, 1)

            def outputs(b, h):
                at = (h >> 1) if latent else h
                dve.wait_ge(o_hi, b * NO + at + 1)
                dve.scalar_tensor_tensor(o_part(at, 1), o_ps[:, :], O_SCALE / P_SCALE, o_part(at, 0), ALU.mult,
                                         ALU.subtract).then_inc(o_done, 1)

            def step(b, h, par):
                if inner(h) or h >= 1:
                    inverse(b, h - 1, 1 - par)
                if latent and (inner(h) or 1 <= h < H - 1):
                    project(b, h + 1, 1 - par, QUERY)
                if latent and par == 0 and (inner(h) or h >= 1):
                    maxima(b, h, par)
                if inner(h) or h >= 2:
                    turn(b, h - 2, par)
                if not latent and (inner(h) or h >= 1):
                    project(b, h - 1, 1 - par, VALUES)
                if (not latent or par == 1) and (inner(h) or h >= 1):
                    maxima(b, h, par)
                if latent:
                    if par == 0 and (inner(h) or h >= 4):
                        outputs(b, h - 4)
                    return
                if inner(h) or h < H - 1:
                    project(b, h + 1, 1 - par, QUERY)
                if inner(h) or h >= 2:
                    outputs(b, h - 2)
                if inner(h) or h < H - 1:
                    project(b, h + 1, 1 - par, KEYS)

            def finish(b, more):
                if latent:
                    outputs(b, H - 4)
                inverse(b, H - 1, 1)
                turn(b, H - 2, 0)
                if not latent:
                    project(b, H - 1, 1, VALUES)
                    outputs(b, H - 2)
                if more:
                    first(b + 1, project)
                turn(b, H - 1, 1)
                if more:
                    maxima(b + 1, 0, 0)
                outputs(b, H - 1)
                dve.wait_ge(y_mm, b + 1)
                xs = G["x"][:, dyn(b * TPB * D, TPB * D)]
                dve.scalar_tensor_tensor(xs, y_ps, 1 / (W_SCALE * O_SCALE), xs, ALU.mult, ALU.add).then_inc(y_done, 1)

            def opening(b):
                first(b, project)
                maxima(b, 0, 0)

            heads(dve, opening, step, finish)

        @block.gpsimd
        def _(pool):
            def step(b, h, par):
                pool.wait_ge(rinv_ready, b * H + h + 1)
                pool.tensor_tensor(carrier[:, par:par + 1], rinv[par][:, 0:1], rinv[par][:, 0:1], ALU.add)
                for i in order:
                    part = p[par][:, Q_AT[i]:Q_AT[i] + (i + 1) * P]
                    pool.tensor_scalar(part, part, rinv[par][:, i:i + 1], P_SCALE, ALU.mult, ALU.mult).then_inc(p_ready, 1)

            if latent:
                pool.memset(zero[:, :], 0.0).then_inc(zeroed, 1)
            heads(pool, lambda b: None, step, lambda b, more: None)


def build(nc, d, out):
    ctx = ExitStack()
    with ctx:
        held = []

        def sem(name):
            held.append(nc.alloc_semaphore(name=name))
            return held[-1]

        def renew_semaphores():
            nc.clear_and_free_semaphores(held)
            held.clear()
            nc.all_engine_barrier()

        taken = set(d)

        def fresh(name):
            while name in taken:
                name += "_"
            taken.add(name)
            return name

        def sb(name, shape, dt=F32, c=ctx):
            return c.enter_context(nc.sbuf_tensor(fresh(name), shape, dt))

        def ps(name, shape, dt=F32, c=ctx):
            return c.enter_context(nc.psum_tensor(fresh(name), shape, dt))

        G = {"spare": sb("spare", [P, 1])}
        G["x"] = sb("x", [P, NT * D])
        G["ident"] = sb("ident", [P, P])
        G["ident_h"] = sb("ident_h", [P, P], F16)
        G["ident_b"] = sb("ident_b", [P, P], BF16)
        G["mask_b"] = sb("mask_b", [P, P], BF16)
        G["ffn_w"] = sb("ffn_w", [P, KD, 3, D], BF16)
        G["gate"] = sb("gate", [P, KD, 2, E], F16)
        G["absent"] = sb("absent", [P, E])
        G["tri_b"] = sb("tri_b", [P, P], BF16)
        G["ones_b"] = sb("ones_b", [P, P], BF16)
        G["hT"] = sb("hT", [P, KD, 2, T], F16)
        G["slot"] = sb("slot", [P, NT * TOPK], U32)
        G["slot_w"] = sb("slot_w", [P, NT * TOPK])
        G["live_four"] = sb("live_four", [P, NT // TPB], I32)
        G["live"] = sb("live", [P, NT * TOPK], I32)
        with ExitStack() as c0:
            G["kT"] = sb("kT", [P, 2, T], F16, c0)
            G["c"] = sb("c_nat", [P, NT, 2, P], F16, c0)
            G["q_w"] = sb("q_w", [P, KD, 2, H * P], F16, c0)
            G["vo_w"] = sb("vo_w", [P, H // 2, 2, D], F16, c0)
            G["kv_w"] = sb("kv_w", [P, KD, 2, P], F16, c0)
            G["c_norm"] = sb("c_norm", [P, LORA], F32, c0)
            with ExitStack() as c_raw:
                A = absorbed_weights(sem, sb, c_raw)
                prepare(nc, d, G, A, sem, sb, ps)
                tiles(nc, d, G, sem, sb, ps, "f", ffn=True, norm=False)
                absorb(nc, d, G, A, sem, sb, ps)
            tiles(nc, d, G, sem, sb, ps, "a", latent=True)
            attention(nc, d, G, sem, sb, ps, "l0", latent=True)
        tiles(nc, d, G, sem, sb, ps, "b", ffn=True, route=True)
        experts(nc, d, G, sem, sb, ps, "m0")
        with ExitStack() as c1:
            for n in ("w_q", "w_k", "w_v"):
                G[n] = sb(n, [P, KD, 2, H * P], F16, c1)
            G["w_o"] = sb("w_o", [P, H, 2, D], F16, c1)
            combine(nc, d, G, sem, sb, "m0", weights=True)
            renew_semaphores()
            tiles(nc, d, G, sem, sb, ps, "c")
            attention(nc, d, G, sem, sb, ps, "l1", latent=False)
        tiles(nc, d, G, sem, sb, ps, "d", route=True)
        experts(nc, d, G, sem, sb, ps, "m1")
        combine(nc, d, G, sem, sb, "m1", out=out)


def kernel(**inputs):
    import numpy as _np
    import concourse.bacc as _bacc
    from concourse.bass_utils import run_bass_kernel_spmd as _run

    a = {k: _np.asarray(v) for k, v in inputs.items()}
    wq = a["L0_attn_Wq"]
    heads = wq.reshape(H, NOPE + ROPE, D)

    def turned(name):
        w = a[name]
        return w.reshape(-1, w.shape[-1]).T

    arrays = {
        "x": a["L0_attn_hidden_states"].reshape(T, D),
        "wq": wq,
        "wpeT": heads[:, NOPE:].transpose(2, 0, 1).reshape(D, H * ROPE),
        "kvaT": a["L0_attn_Wkva"][:LORA].T,
        "kpe_w": a["L0_attn_Wkva"][LORA:],
        "c_norm": _np.broadcast_to(a["L0_attn_kv_a_norm_weight"], (P, LORA)),
        "kvb": a["L0_attn_Wkvb"],
        "woT": turned("L0_attn_Wo"),
        "cos": a["L0_attn_cos"],
        "sin": a["L0_attn_sin"],
        "ffn_wT": turned("L0_ffn_weight"),
        "rramT": turned("L0_ffn_rram_variation"),
        "wkT": turned("L1_attn_W_K"),
        "wqT": turned("L1_attn_W_Q"),
        "wvT": turned("L1_attn_W_V"),
        "woT1": turned("L1_attn_W_O"),
        "gate_w": a["L1_ffn_gate_weight"],
        "gupT": a["L1_ffn_gate_up_proj"].transpose(0, 2, 1),
        "downT": a["L1_ffn_down_proj"].transpose(0, 2, 1),
        "o2n": a["L1_ffn_old_to_new"].reshape(E_OLD, 1),
    }
    arrays = {k: _np.ascontiguousarray(v) for k, v in arrays.items()}
    nc = _bacc.Bacc("TRN2", target_bir_lowering=False, num_devices=1)
    d = {k: nc.dram_tensor(k, v.shape, mybir.dt.from_np(v.dtype), kind="ExternalInput").ap() for k, v in arrays.items()}
    for name in ("scratch_a", "scratch_b"):
        d[name] = nc.dram_tensor(name, (SLOTS, D), F32).ap()
    out = nc.dram_tensor("out", (T, D), F32, kind="ExternalOutput").ap()
    build(nc, d, out)
    r = _run(nc, [arrays], core_ids=[0])
    return r.results[0]["out"].reshape(B, S, D)
```
